# Optimizing a Trainium2 kernel written in Bass

```python
import numpy as np
import jax
import jax.numpy as jnp

def _softmax(x, axis=-1):
    return jax.nn.softmax(x, axis=axis)

def _gelu(x):
    return jax.nn.gelu(x, approximate=True)

def _silu(x):
    return jax.nn.silu(x)

def _sigmoid(x):
    return jax.nn.sigmoid(x)

def _layernorm(x, axis=-1, eps=1e-05):
    m = jnp.mean(x, axis=axis, keepdims=True)
    v = jnp.var(x, axis=axis, keepdims=True)
    return (x - m) / jnp.sqrt(v + eps)

def _scatter_add(tgt, idx, src, axis=0):
    return tgt.at[idx].add(src)

def _segment_sum(src, seg, n):
    return jax.ops.segment_sum(src, seg, n)
kernel_name = 'mk_conv_attn_hybrid_d2_conv_nhwc128_r2_4745e6'

def setup_inputs(seed: int=0):
    np.random.seed(seed)
    _w = jnp.asarray

    def _rec_inputs():
        import jax
        import jax.numpy as jnp
        _gk = jax.random.key(seed)
        x = -0.0002928 + 1 * jax.random.normal(jax.random.fold_in(_gk, 1), (8, 32, 32, 64), jnp.float32)
        return x
    x = _rec_inputs()

    def _L0_conv_setup():
        import jax, jax.numpy as jnp
        import numpy as np
        from jax import lax
        KH, KW = (3, 3)
        KK = KH * KW
        PAD = 1

        def _deform_conv(x, kernel, bias, offset_w, offset_b):
            B, H, W, C = x.shape
            F = kernel.shape[-1]
            offsets = lax.conv_general_dilated(x, offset_w, window_strides=(1, 1), padding='SAME', dimension_numbers=('NHWC', 'HWIO', 'NHWC')) + offset_b
            offsets = offsets.reshape(B, H, W, KK, 2)
            dy, dx = (offsets[..., 0], offsets[..., 1])
            ky = jnp.repeat(jnp.arange(KH, dtype=jnp.float32) - PAD, KW)
            kx = jnp.tile(jnp.arange(KW, dtype=jnp.float32) - PAD, KH)
            py = jnp.arange(H, dtype=jnp.float32)[None, :, None, None] + ky + dy
            px = jnp.arange(W, dtype=jnp.float32)[None, None, :, None] + kx + dx
            y0 = jnp.floor(py)
            x0 = jnp.floor(px)
            wy = py - y0
            wx = px - x0
            y0i = y0.astype(jnp.int32)
            x0i = x0.astype(jnp.int32)
            b_idx = jnp.arange(B)[:, None, None, None]

            def gather(yi, xi):
                valid = (yi >= 0) & (yi < H) & (xi >= 0) & (xi < W)
                yc = jnp.clip(yi, 0, H - 1)
                xc = jnp.clip(xi, 0, W - 1)
                v = x[b_idx, yc, xc]
                return v * valid[..., None].astype(x.dtype)
            val = gather(y0i, x0i) * ((1 - wy) * (1 - wx))[..., None] + gather(y0i, x0i + 1) * ((1 - wy) * wx)[..., None] + gather(y0i + 1, x0i) * (wy * (1 - wx))[..., None] + gather(y0i + 1, x0i + 1) * (wy * wx)[..., None]
            out = jnp.einsum('bhwkc,kcf->bhwf', val, kernel.reshape(KK, C, F))
            return out + bias
        key = jax.random.key(seed)
        k1, k2, k3 = jax.random.split(key, 3)
        B, H, W, C, F = (8, 32, 32, 64, 64)
        x = jax.random.normal(k1, (B, H, W, C), dtype=jnp.float32)
        kernel = jax.random.normal(k2, (KH, KW, C, F), dtype=jnp.float32) * 0.05
        bias = jnp.zeros((F,), dtype=jnp.float32)
        offset_w = jax.random.normal(k3, (KH, KW, C, 2 * KK), dtype=jnp.float32) * 0.01
        offset_b = jnp.zeros((2 * KK,), dtype=jnp.float32)
        return {'x': x, 'kernel': kernel, 'bias': bias, 'offset_w': offset_w, 'offset_b': offset_b}
    _L0_conv_all = _L0_conv_setup()
    _L0_conv_in = {k: v for k, v in _L0_conv_all.items() if k in ('kernel', 'bias', 'offset_w', 'offset_b')}
    del _L0_conv_all

    def _L1_attn_setup():
        import jax, jax.numpy as jnp
        import numpy as np
        HEAD_SIZE = 64
        N_EMBD = 64
        B, T = (16, 1024)
        key = jax.random.key(seed)
        ks = jax.random.split(key, 7)
        s = 1.0 / np.sqrt(N_EMBD)
        return {'x': jax.random.normal(ks[0], (B, T, N_EMBD), dtype=jnp.float32), 'Wq': jax.random.normal(ks[1], (N_EMBD, HEAD_SIZE), dtype=jnp.float32) * s, 'bq': jax.random.normal(ks[2], (HEAD_SIZE,), dtype=jnp.float32) * s, 'Wk': jax.random.normal(ks[3], (N_EMBD, HEAD_SIZE), dtype=jnp.float32) * s, 'bk': jax.random.normal(ks[4], (HEAD_SIZE,), dtype=jnp.float32) * s, 'Wv': jax.random.normal(ks[5], (N_EMBD, HEAD_SIZE), dtype=jnp.float32) * s, 'bv': jax.random.normal(ks[6], (HEAD_SIZE,), dtype=jnp.float32) * s}
    _L1_attn_all = _L1_attn_setup()
    _L1_attn_in = {k: v for k, v in _L1_attn_all.items() if k in ('Wq', 'bq', 'Wk', 'bk', 'Wv', 'bv')}
    del _L1_attn_all

    def _L1_ffn_setup():
        import jax, jax.numpy as jnp
        import numpy as np
        B, S, D, E, H, O, K = (256, 1024, 64, 32, 256, 64, 8)
        key = jax.random.key(seed)
        k0, k1, k2, k3 = jax.random.split(key, 4)
        x = jax.random.normal(k0, (B, S, D), dtype=jnp.float32)
        gate_w = jax.random.normal(k1, (E, D), dtype=jnp.float32) * (1.0 / np.sqrt(D))
        gate_b = jnp.zeros((E,), dtype=jnp.float32)
        weight1 = jax.random.uniform(k2, (E, D + 1, H), dtype=jnp.float32, minval=-1.0, maxval=1.0) * (1.0 / np.sqrt(D + 1))
        weight2 = jax.random.uniform(k3, (E, H + 1, O), dtype=jnp.float32, minval=-1.0, maxval=1.0) * (1.0 / np.sqrt(H + 1))
        return {'x': x, 'gate_w': gate_w, 'gate_b': gate_b, 'weight1': weight1, 'weight2': weight2}
    _L1_ffn_all = _L1_ffn_setup()
    _L1_ffn_in = {k: v for k, v in _L1_ffn_all.items() if k in ('gate_w', 'gate_b', 'weight1', 'weight2')}
    del _L1_ffn_all
    return {'x': x, 'L0_conv_kernel': _L0_conv_in['kernel'], 'L0_conv_bias': _L0_conv_in['bias'], 'L0_conv_offset_w': _L0_conv_in['offset_w'], 'L0_conv_offset_b': _L0_conv_in['offset_b'], 'L1_attn_Wq': _L1_attn_in['Wq'], 'L1_attn_bq': _L1_attn_in['bq'], 'L1_attn_Wk': _L1_attn_in['Wk'], 'L1_attn_bk': _L1_attn_in['bk'], 'L1_attn_Wv': _L1_attn_in['Wv'], 'L1_attn_bv': _L1_attn_in['bv'], 'L1_ffn_gate_w': _L1_ffn_in['gate_w'], 'L1_ffn_gate_b': _L1_ffn_in['gate_b'], 'L1_ffn_weight1': _L1_ffn_in['weight1'], 'L1_ffn_weight2': _L1_ffn_in['weight2']}

def reference(x, L0_conv_kernel, L0_conv_bias, L0_conv_offset_w, L0_conv_offset_b, L1_attn_Wq, L1_attn_bq, L1_attn_Wk, L1_attn_bk, L1_attn_Wv, L1_attn_bv, L1_ffn_gate_w, L1_ffn_gate_b, L1_ffn_weight1, L1_ffn_weight2):
    import jax
    import jax.numpy as jnp

    def _L0_conv_ref(x, kernel, bias, offset_w, offset_b):
        import jax, jax.numpy as jnp
        import numpy as np
        from jax import lax
        KH, KW = (3, 3)
        KK = KH * KW
        PAD = 1

        def _deform_conv(x, kernel, bias, offset_w, offset_b):
            B, H, W, C = x.shape
            F = kernel.shape[-1]
            offsets = lax.conv_general_dilated(x, offset_w, window_strides=(1, 1), padding='SAME', dimension_numbers=('NHWC', 'HWIO', 'NHWC')) + offset_b
            offsets = offsets.reshape(B, H, W, KK, 2)
            dy, dx = (offsets[..., 0], offsets[..., 1])
            ky = jnp.repeat(jnp.arange(KH, dtype=jnp.float32) - PAD, KW)
            kx = jnp.tile(jnp.arange(KW, dtype=jnp.float32) - PAD, KH)
            py = jnp.arange(H, dtype=jnp.float32)[None, :, None, None] + ky + dy
            px = jnp.arange(W, dtype=jnp.float32)[None, None, :, None] + kx + dx
            y0 = jnp.floor(py)
            x0 = jnp.floor(px)
            wy = py - y0
            wx = px - x0
            y0i = y0.astype(jnp.int32)
            x0i = x0.astype(jnp.int32)
            b_idx = jnp.arange(B)[:, None, None, None]

            def gather(yi, xi):
                valid = (yi >= 0) & (yi < H) & (xi >= 0) & (xi < W)
                yc = jnp.clip(yi, 0, H - 1)
                xc = jnp.clip(xi, 0, W - 1)
                v = x[b_idx, yc, xc]
                return v * valid[..., None].astype(x.dtype)
            val = gather(y0i, x0i) * ((1 - wy) * (1 - wx))[..., None] + gather(y0i, x0i + 1) * ((1 - wy) * wx)[..., None] + gather(y0i + 1, x0i) * (wy * (1 - wx))[..., None] + gather(y0i + 1, x0i + 1) * (wy * wx)[..., None]
            out = jnp.einsum('bhwkc,kcf->bhwf', val, kernel.reshape(KK, C, F))
            return out + bias
        return _deform_conv(x, kernel, bias, offset_w, offset_b)

    def _L1_attn_ref(x, Wq, bq, Wk, bk, Wv, bv):
        import jax, jax.numpy as jnp
        import numpy as np
        HEAD_SIZE = 64
        N_EMBD = 64
        B, T = (16, 1024)
        q = jnp.einsum('bte,eh->bth', x, Wq) + bq
        k = jnp.einsum('bte,eh->bth', x, Wk) + bk
        v = jnp.einsum('bte,eh->bth', x, Wv) + bv
        scale = 1.0 / HEAD_SIZE ** 0.5
        scores = jnp.einsum('bqh,bkh->bqk', q, k) * scale
        t = x.shape[1]
        tril = jnp.tril(jnp.ones((t, t), dtype=scores.dtype))
        scores = scores * tril - 1000000000000.0 * (1.0 - tril)
        attn = jax.nn.softmax(scores, axis=-1)
        out = jnp.einsum('bqk,bkh->bqh', attn, v)
        return out

    def _L1_ffn_ref(x, gate_w, gate_b, weight1, weight2):
        import jax, jax.numpy as jnp
        import numpy as np
        B, S, D, E, H, O, K = (256, 1024, 64, 32, 256, 64, 8)
        Bn, Sn, Dn = x.shape
        logits = jnp.einsum('bsd,ed->bse', x, gate_w) + gate_b
        probs = jax.nn.softmax(logits, axis=1)
        vals, idx = jax.lax.top_k(probs.transpose(0, 2, 1), K)
        topv = vals.transpose(0, 2, 1)
        topi = idx.transpose(0, 2, 1)
        flat_idx = topi.reshape(Bn, K * E)
        gathered = jnp.take_along_axis(x, flat_idx[:, :, None], axis=1)
        gathered = gathered.reshape(Bn, K, E, Dn)
        pooled = jnp.einsum('bked,bke->bed', gathered, topv)
        ones = jnp.ones((E, Bn, 1), dtype=x.dtype)
        h = jnp.concatenate([pooled.transpose(1, 0, 2), ones], axis=-1)
        h = jax.nn.gelu(jnp.einsum('ebd,edh->ebh', h, weight1), approximate=False)
        h = jnp.concatenate([h, ones], axis=-1)
        out = jnp.einsum('ebh,eho->ebo', h, weight2)
        out = out.transpose(1, 0, 2)
        weighted = jnp.einsum('beo,bke->bkeo', out, topv).reshape(Bn, K * E, O)
        outputs = jnp.zeros((Bn, Sn, O), dtype=x.dtype)
        outputs = outputs.at[jnp.arange(Bn)[:, None], flat_idx].add(weighted)
        return outputs

    def _gn(v, G=32, eps=1e-05):
        B_, H_, W_, C_ = v.shape
        g = v.reshape(B_, H_, W_, G, C_ // G)
        m = jnp.mean(g, axis=(1, 2, 4), keepdims=True)
        s = jnp.var(g, axis=(1, 2, 4), keepdims=True)
        return ((g - m) / jnp.sqrt(s + eps)).reshape(v.shape)

    def _ln_c(v, eps=1e-06):
        m = jnp.mean(v, axis=-1, keepdims=True)
        s = jnp.var(v, axis=-1, keepdims=True)
        return (v - m) / jnp.sqrt(s + eps)

    def _ln_t(v, eps=1e-05):
        m = jnp.mean(v, axis=-1, keepdims=True)
        s = jnp.var(v, axis=-1, keepdims=True)
        return (v - m) / jnp.sqrt(s + eps)

    def _to_tokens(v):
        B_, H_, W_, C_ = v.shape
        return v.reshape(B_, H_ * W_, C_)

    def _from_tokens(t, like):
        return t.reshape(like.shape)
    x = x + _L0_conv_ref(_gn(x), L0_conv_kernel, L0_conv_bias, L0_conv_offset_w, L0_conv_offset_b)
    t = _to_tokens(x)
    t = t + _L1_attn_ref(_ln_t(t), L1_attn_Wq, L1_attn_bq, L1_attn_Wk, L1_attn_bk, L1_attn_Wv, L1_attn_bv)
    t = t + _L1_ffn_ref(_ln_t(t), L1_ffn_gate_w, L1_ffn_gate_b, L1_ffn_weight1, L1_ffn_weight2)
    x = _from_tokens(t, x)
    return x

_drawn_inputs = setup_inputs


def setup_inputs(seed=0):
    import zlib

    import numpy as np

    out = dict(_drawn_inputs(seed))
    spreads = {'L0_conv_bias': (0.0, 0.1), 'L0_conv_offset_b': (0.0, 0.1), 'L1_ffn_gate_b': (0.0, 0.1)}
    factors = {'L1_attn_bq': 3.828,
     'L1_attn_bk': 8.0,
     'L1_ffn_gate_w': 8.0,
     'L1_ffn_weight1': 8.0,
     'L1_ffn_weight2': 8.0}
    for name, (base, spread) in spreads.items():
        noise = np.random.default_rng([zlib.crc32(name.encode()), seed]).standard_normal(out[name].shape)
        drawn = base * np.exp(spread * noise) if base else spread * noise
        out[name] = jnp.asarray(drawn.astype(out[name].dtype))
    for name, factor in factors.items():
        out[name] = (out[name] * factor).astype(out[name].dtype)
    return out
```

```python
from contextlib import ExitStack

import numpy as np

import concourse.bass as bass
from concourse import mybir

F32 = mybir.dt.float32
I32 = mybir.dt.int32
ALU = mybir.AluOpType
ACT = mybir.ActivationFunctionType
AX = mybir.AxisListType

B, H, W, C = 8, 32, 32, 64
T = H * W
P = 128
NT = T // P
BR = P // W
K = 3
NCH = NT + 1
HALO = 3
PR = 38
OCH = 2 * K * K
SLOTS = (K * K + 1) // 2
HB = 512
E, HID, TOP = 32, 256, 8
GI = P // E
NG = B // GI
LIMIT = 2.0
WIN = 2 * BR
GN_EPS, LN_EPS = 1e-5, 1e-5
NEG = -1e13


def constants():
    p = np.arange(P)
    r, w = p // W, p % W
    ident = np.eye(P)
    same = (p[:, None] // 2 == p[None, :] // 2) * 0.5
    diff = same * np.where(p[:, None] % 2 == 0, 1.0, -1.0)
    ybase = r[:, None] + 2 - np.arange(WIN)[None, :]
    xbase = (w[:, None, None] + (np.arange(K) - 1)[None, :, None] - np.arange(W)[None, None, :]).reshape(P, -1)
    mask = np.where(p[None, :] > p[:, None], NEG, 0.0)
    half = np.full((P, NT), -0.5)
    yall = ((r + 2)[:, None, None] + BR * np.arange(NT)[None, :, None] - np.arange(BR * NCH)[None, None, :]).reshape(P, -1)
    yall = ((r + 2)[:, None, None] + BR * np.arange(NT)[None, :, None] - np.arange(BR * NCH)[None, None, :]).reshape(P, -1)
    yall = ((r + 2)[:, None, None] + BR * np.arange(NT)[None, :, None] - np.arange(BR * NCH)[None, None, :]).reshape(P, -1)
    yall = ((r + 2)[:, None, None] + BR * np.arange(NT)[None, :, None] - np.arange(BR * NCH)[None, None, :]).reshape(P, -1)
    yall = ((r + 2)[:, None, None] + BR * np.arange(NT)[None, :, None] - np.arange(BR * NCH)[None, None, :]).reshape(P, -1)
    yall = ((r + 2)[:, None, None] + BR * np.arange(NT)[None, :, None] - np.arange(BR * NCH)[None, None, :]).reshape(P, -1)
    yall = ((r + 2)[:, None, None] + BR * np.arange(NT)[None, :, None] - np.arange(BR * NCH)[None, None, :]).reshape(P, -1)
    yall = ((r + 2)[:, None, None] + BR * np.arange(NT)[None, :, None] - np.arange(BR * NCH)[None, None, :]).reshape(P, -1)
    parts = dict(ident=ident, same=same, diff=diff, ybase=ybase, xbase=xbase, mask=mask, half=half, yall=yall)
    at, cols = {}, 0
    for n, a in parts.items():
        at[n] = (cols, cols + a.shape[1])
        cols += a.shape[1]
    return np.concatenate(list(parts.values()), 1).astype(np.float32), at



class Steps:

    def __init__(self, sem, it, per):
        self.sem, self.it, self.per, self.n = sem, it, per, 0

    def done(self, ins):
        ins.then_inc(self.sem, 1)
        self.n += 1

    def value(self):
        assert self.n <= self.per
        return self.it * self.per + self.n


def each_image(eng):
    with eng.Fori(0, B // 2) as i:
        for u in range(2):
            yield u, i * 2 + u, i



class Steps:

    def __init__(self, sem, it, per):
        self.sem, self.it, self.per, self.n = sem, it, per, 0

    def done(self, ins):
        ins.then_inc(self.sem, 1)
        self.n += 1

    def value(self):
        assert self.n <= self.per
        return self.it * self.per + self.n


def each_image(eng):
    with eng.Fori(0, B // 2) as i:
        for u in range(2):
            yield u, i * 2 + u, i



class Steps:

    def __init__(self, sem, it, per):
        self.sem, self.it, self.per, self.n = sem, it, per, 0

    def done(self, ins):
        ins.then_inc(self.sem, 1)
        self.n += 1

    def value(self):
        assert self.n <= self.per
        return self.it * self.per + self.n


def each_image(eng):
    with eng.Fori(0, B // 2) as i:
        for u in range(2):
            yield u, i * 2 + u, i



class Steps:

    def __init__(self, sem, it, per):
        self.sem, self.it, self.per, self.n = sem, it, per, 0

    def done(self, ins):
        ins.then_inc(self.sem, 1)
        self.n += 1

    def value(self):
        assert self.n <= self.per
        return self.it * self.per + self.n


def each_image(eng):
    with eng.Fori(0, B // 2) as i:
        for u in range(2):
            yield u, i * 2 + u, i



class Steps:

    def __init__(self, sem, it, per):
        self.sem, self.it, self.per, self.n = sem, it, per, 0

    def done(self, ins):
        ins.then_inc(self.sem, 1)
        self.n += 1

    def value(self):
        assert self.n <= self.per
        return self.it * self.per + self.n


def settle(eng, s_const):
    eng.wait_ge(s_const, 16)


def each_image(eng):
    with eng.Fori(0, B // 2) as i:
        for u in range(2):
            yield u, i * 2 + u, i



class Steps:

    def __init__(self, sem, it, per):
        self.sem, self.it, self.per, self.n = sem, it, per, 0

    def done(self, ins):
        ins.then_inc(self.sem, 1)
        self.n += 1

    def value(self):
        assert self.n <= self.per
        return self.it * self.per + self.n


def settle(eng, s_const):
    eng.wait_ge(s_const, 16)


def each_image(eng):
    with eng.Fori(0, B // 2) as i:
        for u in range(2):
            yield u, i * 2 + u, i



class Steps:

    def __init__(self, sem, it, per):
        self.sem, self.it, self.per, self.n = sem, it, per, 0

    def done(self, ins):
        ins.then_inc(self.sem, 1)
        self.n += 1

    def value(self):
        assert self.n <= self.per
        return self.it * self.per + self.n


def each_image(eng):
    with eng.Fori(0, B // 2) as i:
        for u in range(2):
            yield u, i * 2 + u, i



class Steps:

    def __init__(self, sem, it, per):
        self.sem, self.it, self.per, self.n = sem, it, per, 0

    def done(self, ins):
        ins.then_inc(self.sem, 1)
        self.n += 1

    def value(self):
        assert self.n <= self.per
        return self.it * self.per + self.n


def each_image(eng):
    with eng.Fori(0, B // 2) as i:
        for u in range(2):
            yield u, i * 2 + u, i


def build(nc, dram, out):
    table, at = constants()
    x_blk = dram["x"].rearrange("b (t r) w c -> b (r w) t c", r=BR)
    out_blk = out.rearrange("b (t r) w c -> b (r w) t c", r=BR)
    with ExitStack() as ctx:
        def sb(name, shape, dt=F32):
            return ctx.enter_context(nc.sbuf_tensor(name, shape, dt))

        def sem(name):
            return ctx.enter_context(nc.semaphore(name))

        const = sb("const", [P, table.shape[1]])

        def cst(name):
            return const[:, at[name][0]:at[name][1]]

        tok = sb("tok", [P, B, NT, C])
        wqk = sb("wqk", [C + 1, 2 * C])
        wv = sb("wv", [C + 1, C])
        gate = sb("gate", [C + 1, E])
        s_const, s_tok = sem("s_const"), sem("s_tok")
        s_past = sem("s_past")
        psum = ctx.enter_context(nc.psum_tensor("psum", [P, 8, HB], F32))
        with ExitStack() as conv:
            def csb(name, shape, dt=F32):
                return conv.enter_context(nc.sbuf_tensor(name, shape, dt))

            off = csb("off", [P, B, NT, OCH])
            pix = csb("pix", [P, B, K, NCH, C])
            flag = csb("flag", [1, 1], I32)
            kp = csb("kp", [P, SLOTS, C])
            kbias = csb("kbias", [P, 1])
            prepare(nc, dram, cst, const, psum, tok, x_blk, off, pix, flag, kp, kbias, wqk, wv, gate, s_const, s_tok, s_past)
            sample(nc, cst, psum, tok, off, pix, flag, kp, kbias, s_past)
        w1 = sb("w1", [C + 1, E, HID])
        w2 = sb("w2", [P, 2, E, C])
        b2 = sb("b2", [C, E])
        s_w = sem("s_w")
        attention(nc, dram, cst, psum, tok, wqk, wv, w1, w2, b2, s_w, s_past)
        pm = sb("pm", [P, NG, T])
        pooled_t = sb("pooled_t", [C + 1, B, E])
        route(nc, cst, psum, tok, gate, pm, pooled_t, s_past)
        expert_out = sb("expert_out", [P, NG, C])
        mlp(nc, cst, psum, w1, w2, b2, s_w, pooled_t, expert_out)
        combine(nc, psum, tok, pm, expert_out, out_blk)


def prepare(nc, dram, cst, const, psum, tok, x_blk, off, pix, flag, kp, kbias, wqk, wv, gate, s_const, s_tok, s_past):
    ident = cst("ident")
    with ExitStack() as ctx:
        def sb(name, shape, dt=F32):
            return ctx.enter_context(nc.sbuf_tensor(name, shape, dt))

        def sem(name):
            return ctx.enter_context(nc.semaphore(name))

        xs = sb("xs", [P, 2, NT, 2, C])
        ow_pair = sb("ow_pair", [P, K, 32])
        ow_last = sb("ow_last", [C, K, 32])
        ob = sb("ob", [P, 1])
        pxn = sb("pxn", [P, 2, PR, W])
        offT = sb("offT", [P, 2, 128])
        st = sb("st", [P, 2, 6])
        mv = sb("mv", [P, 2])
        gs = sb("gs", [P, 8])
        mx = sb("mx", [P, 1])
        mrow = sb("mrow", [1, 2])
        xT = psum[:, 0:2, :]
        offP = psum[:, 2, 0:256]
        offTok = psum[:, 2, 256:512]
        grp = psum[:, 3, 0:3]
        mxT = psum[0:1, 3, 128:256]
        s_ld = [sem(f"s_ld{u}") for u in range(2)]
        names = ("xs_free x_t pad0 st mv gavg vv rs1 rstd nmr g1 pn_lo pn_hi px_free off_mm off_sb pix_t "
                 "pix_ev off_t off_tok m1 m2 m3 m4").split()
        s = {n: sem("p_" + n) for n in names}

        with nc.Block() as block:
            @block.sync
            def _(sync):
                sync.dma_start(const[:, :], dram["const"]).then_inc(s_const, 16)
                for dst, name in ((ow_pair[:, :, :], "ow_pair"), (ow_last[:, :, :], "ow_last"), (ob[:, :], "ob"),
                                  (kp[:, :, :], "kp"), (kbias[:, :], "kbias"), (wqk[:, :], "wqk"),
                                  (wv[:, :], "wv"), (gate[:, :], "gate")):
                    sync.dma_start(dst, dram[name]).then_inc(s_const, 16)
                for u, b, i in each_image(sync):
                    sync.wait_ge(s["xs_free"], b + 1)
                    sync.dma_start(xs[:, u, :, 0, :], x_blk[b]).then_inc(s_ld[u], 16)
                    sync.dma_start(xs[:, u, :, 1, :], x_blk[b]).then_inc(s_ld[u], 16)

            @block.gpsimd
            def _(pool):
                pool.memset(pxn[:, :, :, :], 0.0).then_inc(s["pad0"], 1)
                for u, b, i in each_image(pool):
                    pool.dma_start(tok[:, b, :, :], x_blk[b]).then_inc(s_tok, 16)
                    pool.wait_ge(s["vv"], b + 1)
                    pool.sem_inc(s_past, 1)
                    pool.tensor_scalar(gs[:, 3:4], gs[:, 3:4], GN_EPS, None, ALU.add).then_inc(s["rs1"], 1)
                    pool.wait_ge(s["rs1"], b + 1)
                    pool.tensor_tensor(gs[:, 4:5], gs[:, 3:4], cst("half")[:, 0:1], ALU.pow).then_inc(s["rstd"], 1)
                pool.wait_ge(s_tok, 16 * B)

            @block.tensor
            def _(pe):
                pe.sem_inc(s["xs_free"], 2)
                pe.sem_inc(s["px_free"], 2)
                pe.wait_ge(s_const, 16 * 9)
                for u, b, i in each_image(pe):
                    pe.wait_ge(s_ld[u], i * 32 + 32)
                    pe.wait_ge(s["pn_lo"], b)
                    pe.wait_ge(s["pn_hi"], b)
                    for t in range(NT):
                        ins = pe.transpose(xT[:, t // 4, (t % 4) * P:(t % 4 + 1) * P],
                                           xs[:, u, t, :, :].rearrange("p a c -> p (a c)"), ident)
                    ins.then_inc(s["x_t"], 1)
                    pe.wait_ge(s["mv"], b + 1)
                    pe.matmul(grp[:, 0:2], cst("same"), mv[:, :], start=True, stop=True).then_inc(s["xs_free"], 1)
                    pe.matmul(grp[:, 2:3], cst("diff"), mv[:, 0:1], start=True, stop=True).then_inc(s["gavg"], 1)
                    pe.wait_ge(s["pn_lo"], b + 1)
                    pe.wait_ge(s["pn_hi"], b + 1)
                    pe.wait_ge(s["off_tok"], b)
                    for n, kx in enumerate((1, 0, 2)):
                        a, z = max(0, 1 - kx), min(W, W + 1 - kx)
                        for j in range(4):
                            pe.matmul(offP[32 * j:32 * j + 32, :].rearrange("m (h w) -> m h w", w=W)[:, :, a:z],
                                      ow_pair[:, kx, :],
                                      pxn[:, u, 8 * j + 2:8 * j + 10, a + kx - 1:z + kx - 1],
                                      start=(n == 0), stop=False)
                    for n, kx in enumerate((0, 2, 1)):
                        a, z = max(0, 1 - kx), min(W, W + 1 - kx)
                        for j in range(4):
                            ins = pe.matmul(offP[32 * j:32 * j + 32, :].rearrange("m (h w) -> m h w", w=W)[:, :, a:z],
                                            ow_last[:, kx, :],
                                            pxn[0:C, u, 8 * j + 4:8 * j + 12, a + kx - 1:z + kx - 1],
                                            start=False, stop=(n == K - 1))
                    ins.then_inc(s["off_mm"], 1)
                    pe.wait_ge(s["pix_ev"], b)
                    pe.sem_inc(s_past, 1)
                    for k in range(K):
                        for c in range(NCH):
                            dst = psum[:, 4 + k, c * C:(c + 1) * C] if c < NT else psum[:, 7, k * C:(k + 1) * C]
                            ins = pe.transpose(dst, pxn[0:C, u, BR * c + k:BR * c + k + BR, :].rearrange("c r w -> c (r w)"),
                                               ident[0:C, 0:C])
                    ins.then_inc(s["pix_t"], 1)
                    pe.wait_ge(s["off_sb"], b + 1)
                    pe.transpose(offTok[:, 0:P], offT[:, 0, :], ident).then_inc(s["px_free"], 1)
                    pe.transpose(offTok[:, P:2 * P], offT[:, 1, :], ident).then_inc(s["off_t"], 1)
                pe.wait_ge(s["m1"], 1)
                pe.transpose(mxT, mx[:, :], ident).then_inc(s["m2"], 1)

            @block.scalar
            def _(act):
                act.wait_ge(s_const, 16 * 9)
                act.wait_ge(s["pad0"], 1)
                for u, b, i in each_image(act):
                    act.wait_ge(s["nmr"], b + 1)
                    act.wait_ge(s["px_free"], b + 1)
                    act.activation(pxn[0:C, u, HALO:HALO + H, :],
                                   xT[0:C, :, :].rearrange("c a (h w) -> c (a h) w", w=W), ACT.Identity,
                                   bias=gs[0:C, 5:6], scale=gs[0:C, 4:5]).then_inc(s["pn_lo"], 1)
                    act.wait_ge(s["off_mm"], b + 1)
                    act.wait_ge(s["off_t"], b)
                    act.activation(offT[:, :, :], offP.rearrange("p (h q) -> p h q", h=2), ACT.Identity,
                                   bias=ob[:, 0:1]).then_inc(s["off_sb"], 1)
                    act.wait_ge(s["pix_t"], b + 1)
                    act.activation(pix[:, b, :, 0:NT, :],
                                   psum[:, 4:7, :].rearrange("p k (c f) -> p k c f", f=C), ACT.Copy)
                    act.activation(pix[:, b, :, NT, :],
                                   psum[:, 7, 0:K * C].rearrange("p (k f) -> p k f", f=C),
                                   ACT.Copy).then_inc(s["pix_ev"], 1)

            @block.vector
            def _(dve):
                dve.wait_ge(s["pad0"], 1)
                for u, b, i in each_image(dve):
                    v = Steps(s["st"], b, 3)
                    dve.wait_ge(s["x_t"], b + 1)
                    v.done(dve.bn_stats(st[:, 0, :], xT[:, 0, :]))
                    v.done(dve.bn_stats(st[:, 1, :], xT[:, 1, :]))
                    dve.wait_ge(s["st"], v.value())
                    dve.sem_inc(s_past, 1)
                    dve.bn_aggr(mv[:, :], st[:, :, :]).then_inc(s["mv"], 1)
                    dve.wait_ge(s["gavg"], b + 1)
                    dve.wait_ge(s["pn_lo"], b)
                    v.done(dve.tensor_copy(gs[:, 0:3], grp))
                    dve.wait_ge(s["st"], v.value())
                    dve.scalar_tensor_tensor(gs[:, 3:4], gs[:, 2:3], gs[:, 2:3], gs[:, 1:2],
                                             ALU.mult, ALU.add).then_inc(s["vv"], 1)
                    dve.wait_ge(s["rstd"], b + 1)
                    dve.scalar_tensor_tensor(gs[:, 5:6], gs[:, 0:1], -1.0, gs[:, 4:5],
                                             ALU.mult, ALU.mult).then_inc(s["nmr"], 1)
                    dve.wait_ge(s["nmr"], b + 1)
                    dve.wait_ge(s["px_free"], b + 1)
                    dve.tensor_scalar(pxn[C:P, u, HALO - 1:HALO - 1 + H, :],
                                      xT[C:P, :, :].rearrange("c a (h w) -> c (a h) w", w=W),
                                      gs[C:P, 4:5], gs[C:P, 5:6], ALU.mult, ALU.add).then_inc(s["pn_hi"], 1)
                    dve.wait_ge(s["off_t"], b + 1)
                    dve.tensor_copy(off[:, b, :, :].rearrange("p (j h) o -> p j h o", h=2),
                                    offTok.rearrange("p (h j o) -> p j h o", h=2, j=4)[:, :, :, 0:OCH]
                                    ).then_inc(s["off_tok"], 1)
                dve.wait_ge(s["off_tok"], B)
                dve.tensor_reduce(mx[:, :], off.rearrange("p b t (k d) -> p (b t k) d", d=2)[:, :, 0], AX.X, ALU.max,
                                  apply_absolute_value=True).then_inc(s["m1"], 1)
                dve.wait_ge(s["m2"], 1)
                dve.tensor_reduce(mrow[:, 0:1], mxT, AX.X, ALU.max).then_inc(s["m3"], 1)
                dve.wait_ge(s["m3"], 1)
                dve.tensor_scalar(flag[:, :], mrow[:, 0:1], LIMIT, None, ALU.is_ge).then_inc(s["m4"], 1)
                dve.wait_ge(s["m4"], 1)


def tap(k, kx):
    n = K * k + kx
    return n // 2, (n % 2) * C


def sample(nc, cst, psum, tok, off, pix, flag, kp, kbias, s_past):
    ident = cst("ident")
    NU = NT * K
    XN = NT * K * K * W
    YN = NT * K * K * WIN
    with ExitStack() as ctx:
        def sb(name, shape, dt=F32):
            return ctx.enter_context(nc.sbuf_tensor(name, shape, dt))

        def sem(name):
            return ctx.enter_context(nc.semaphore(name))

        rows = sb("rows", [P, 2, K, NCH, C])
        tent = sb("tent", [P, 2, XN + YN])
        wt = sb("wt", [P, 2, K, 2, P])
        wtT = sb("wtT", [P, 2, 2, K, P])
        val = sb("val", [P, SLOTS, T])
        conv_sb = sb("conv_sb", [P, HB])
        gy = sb("gy", [P, K * K, BR * NCH])
        gT = sb("gT", [P, NCH, K, P])
        names = ("zeroed rows_ok rows_free dist tent_ok tent_free a1 w_ok tp wT mm val_ok ko_mm ko_sb xo_t x1 "
                 "g_rows g_d g_a g_tent g_yd g_ya g_y g_w g_tp g_ev g_mm g_val g_ko g_kosb g_xo g_x1 g_used").split()
        s = {n: sem("c_" + n) for n in names}
        xpart = tent[:, :, 0:XN].rearrange("p u (t k x q) -> p u t k x q", t=NT, k=K, x=K)
        ypart = tent[:, :, XN:XN + YN].rearrange("p u (t k x m) -> p u t k x m", t=NT, k=K, x=K)
        xbase = cst("xbase").rearrange("p (x q) -> p x q", x=K)
        KO = psum[:, 7, :]

        def distances(pool, u, b, sem_d):
            dx = off[:, b, :, :].rearrange("p t (k x d) -> p (t k) x d", k=K, d=2)[:, :, :, 1]
            pool.tensor_tensor(tent[:, u, 0:XN].rearrange("p (a x q) -> p a x q", x=K, q=W),
                               dx.unsqueeze(3).to_broadcast([P, NT * K, K, W]),
                               xbase.unsqueeze(1).to_broadcast([P, NT * K, K, W]), ALU.add).then_inc(sem_d, 1)
            dy = off[:, b, :, :].rearrange("p t (a d) -> p (t a) d", d=2)[:, :, 0]
            pool.tensor_tensor(tent[:, u, XN:XN + YN].rearrange("p (a m) -> p a m", m=WIN),
                               dy.unsqueeze(2).to_broadcast([P, NT * K * K, WIN]),
                               cst("ybase").unsqueeze(1).to_broadcast([P, NT * K * K, WIN]),
                               ALU.add).then_inc(sem_d, 1)

        def product_over_kernel(pe, halves_done):
            for sl in range(SLOTS):
                for hf in range(2):
                    ins = pe.matmul(KO[C * hf:C * hf + C, :], kp[:, sl, :],
                                    val[:, sl, hf * HB:(hf + 1) * HB],
                                    start=(sl == 0), stop=(sl == SLOTS - 1))
            ins.then_inc(halves_done, 1)

        def back_to_tokens(pe, done):
            for q in range(4):
                ins = pe.transpose(KO[:, q * P:(q + 1) * P], conv_sb[:, q * P:(q + 1) * P], ident)
            ins.then_inc(done, 1)

        def add_to_tokens(dve, b, done):
            x1 = tok[:, b, :, :].rearrange("p (h q) f -> p q h f", h=2)
            dve.tensor_tensor(x1, KO.rearrange("p (q h f) -> p q h f", q=4, h=2), x1, ALU.add).then_inc(done, 1)

        def load_flag(eng):
            return eng.value_load(flag[0:1, 0:1], min_val=0, max_val=1)

        with nc.Block() as block:
            @block.gpsimd
            def _(pool):
                large = load_flag(pool)
                with pool.If(large < 1):
                    for u, b, i in each_image(pool):
                        pool.wait_ge(s["rows_free"], b + 1)
                        pool.tensor_copy(rows[:, u, :, :, :], pix[:, b, :, :, :]).then_inc(s["rows_ok"], 1)
                        pool.wait_ge(s["tent_free"], b + 1)
                        distances(pool, u, b, s["dist"])
                with pool.Else():
                    with pool.Fori(0, B) as b:
                        pool.wait_ge(s["g_x1"], b)
                        pool.tensor_copy(rows[:, 0, :, :, :], pix[:, b, :, :, :]).then_inc(s["g_rows"], 1)
                        distances(pool, 0, b, s["g_d"])
                pool.nop()

            @block.scalar
            def _(act):
                large = load_flag(act)
                with act.If(large < 1):
                    act.sem_inc(s["mm"], 1)
                    for u, b, i in each_image(act):
                        act.wait_ge(s["dist"], b * 2 + 2)
                        act.activation(tent[:, u, :], tent[:, u, :], ACT.Abs).then_inc(s["a1"], 1)
                        act.wait_ge(s["a1"], b + 1)
                        act.activation(tent[:, u, :], tent[:, u, :], ACT.Relu, bias=1.0,
                                       scale=-1.0).then_inc(s["tent_ok"], 1)
                        for n in range(NU):
                            q = b * NU + n
                            act.wait_ge(s["tp"], q + 2)
                            act.wait_ge(s["mm"], q)
                            act.activation(wtT[:, n % 2, :, :, :].rearrange("p c x q -> p c (x q)"),
                                           psum[:, 2 * (n % 2):2 * (n % 2) + 2, 0:K * P],
                                           ACT.Copy).then_inc(s["wT"], 1)
                        act.wait_ge(s["ko_mm"], b + 1)
                        act.activation(conv_sb[:, :], KO, ACT.Identity, bias=kbias[:, 0:1]).then_inc(s["ko_sb"], 1)
                with act.Else():
                    with act.Fori(0, B) as b:
                        act.wait_ge(s["g_d"], b * 2 + 2)
                        act.activation(tent[:, 0, :], tent[:, 0, :], ACT.Abs).then_inc(s["g_a"], 1)
                        act.wait_ge(s["g_a"], b + 1)
                        act.activation(tent[:, 0, :], tent[:, 0, :], ACT.Relu, bias=1.0,
                                       scale=-1.0).then_inc(s["g_tent"], 1)
                        with act.Fori(0, NT) as t:
                            bt = b * NT + t
                            act.wait_ge(s["g_yd"], bt + 1)
                            act.activation(gy[:, :, :], gy[:, :, :], ACT.Abs).then_inc(s["g_ya"], 1)
                            act.wait_ge(s["g_ya"], bt + 1)
                            act.activation(gy[:, :, :], gy[:, :, :], ACT.Relu, bias=1.0,
                                           scale=-1.0).then_inc(s["g_y"], 1)
                            for k in range(K):
                                for c in range(NCH):
                                    act.wait_ge(s["g_tp"], bt * K * NCH + (k * NCH + c + 1))
                                    if c == 0:
                                        act.wait_ge(s["g_mm"], bt * K + k)
                                    act.activation(gT[:, c, :, :].rearrange("p x q -> p (x q)"),
                                                   psum[:, 0, 0:K * P], ACT.Copy).then_inc(s["g_ev"], 1)
                        act.wait_ge(s["g_ko"], b + 1)
                        act.activation(conv_sb[:, :], KO, ACT.Identity, bias=kbias[:, 0:1]).then_inc(s["g_kosb"], 1)
                act.nop()

            @block.vector
            def _(dve):
                dve.memset(val[:, SLOTS - 1, :], 0.0).then_inc(s["zeroed"], 1)
                dve.wait_ge(s["zeroed"], 1)
                large = load_flag(dve)
                with dve.If(large < 1):
                    for u, b, i in each_image(dve):
                        dve.wait_ge(s["tent_ok"], b + 1)

                        def leave(t):
                            dve.wait_ge(s["mm"], b * NU + (K * t + K + 1))
                            if t == 0:
                                dve.wait_ge(s["ko_mm"], b)
                            dve.tensor_copy(val[:, 0:4, t * P:(t + 1) * P],
                                            psum[:, 4 + t % 2, :].rearrange("p (s q) -> p s q", s=4))
                            lo = (t % 2) * C
                            dve.tensor_copy(val[lo:lo + C, 4, t * P:(t + 1) * P],
                                            psum[lo:lo + C, 6, 0:P]).then_inc(s["val_ok"], 1)

                        for n in range(NU):
                            t, k = n // K, n % K
                            q = b * NU + n
                            dve.wait_ge(s["tp"], q)
                            ins = dve.tensor_tensor(
                                wt[:, n % 2, :, :, :].rearrange("p x c (m q) -> p x (c m) q", q=W),
                                xpart[:, u, t, k].unsqueeze(2).to_broadcast([P, K, WIN, W]),
                                ypart[:, u, t, k].unsqueeze(3).to_broadcast([P, K, WIN, W]), ALU.mult)
                            ins.then_inc(s["w_ok"], 1)
                            if n % K == K - 1 and t >= 1:
                                leave(t - 1)
                        dve.wait_ge(s["w_ok"], b * NU + NU)
                        dve.sem_inc(s["tent_free"], 1)
                        leave(NT - 1)
                        dve.wait_ge(s["xo_t"], b + 1)
                        add_to_tokens(dve, b, s["x1"])
                    dve.wait_ge(s["x1"], B)
                with dve.Else():
                    with dve.Fori(0, B) as b:
                        dve.wait_ge(s["g_tent"], b + 1)
                        dve.sem_inc(s_past, 1)
                        with dve.Fori(0, NT) as t:
                            bt = b * NT + t
                            dve.wait_ge(s["g_w"], bt * K * NCH)
                            dy = off[:, b, t, :].rearrange("p (a d) -> p a d", d=2)[:, :, 0]
                            dve.tensor_tensor(gy[:, :, :], dy.unsqueeze(2).to_broadcast([P, K * K, BR * NCH]),
                                              cst("yall").rearrange("p (t m) -> p t m", t=NT)[:, t, :]
                                              .unsqueeze(1).to_broadcast([P, K * K, BR * NCH]),
                                              ALU.add).then_inc(s["g_yd"], 1)
                            dve.wait_ge(s["g_y"], bt + 1)
                            for k in range(K):
                                for c in range(NCH):
                                    dve.wait_ge(s["g_tp"], bt * K * NCH + (k * NCH + c))
                                    dve.tensor_tensor(
                                        wt[:, 0, :, 0, :].rearrange("p x (m q) -> p x m q", q=W),
                                        xpart[:, 0, t, k].unsqueeze(2).to_broadcast([P, K, BR, W]),
                                        gy[:, k * K:(k + 1) * K, c * BR:(c + 1) * BR].unsqueeze(3)
                                        .to_broadcast([P, K, BR, W]), ALU.mult).then_inc(s["g_w"], 1)
                            dve.wait_ge(s["g_mm"], bt * K + K)
                            dve.tensor_copy(val[:, 0:4, bass.ds(t * P, P)],
                                            psum[:, 4, :].rearrange("p (s q) -> p s q", s=4))
                            dve.tensor_copy(val[0:C, 4, bass.ds(t * P, P)],
                                            psum[0:C, 6, 0:P]).then_inc(s["g_val"], 1)
                        dve.wait_ge(s["g_xo"], b + 1)
                        add_to_tokens(dve, b, s["g_x1"])
                    dve.wait_ge(s["g_x1"], B)
                dve.nop()

            @block.tensor
            def _(pe):
                large = load_flag(pe)
                with pe.If(large < 1):
                    pe.sem_inc(s["rows_free"], 2)
                    pe.sem_inc(s["tent_free"], 2)
                    pe.sem_inc(s["tp"], 1)
                    for u, b, i in each_image(pe):
                        def turn(n):
                            pe.wait_ge(s["w_ok"], b * NU + n + 1)
                            if n >= 2:
                                pe.wait_ge(s["wT"], b * NU + n - 1)
                            else:
                                pe.wait_ge(s["wT"], b * NU)
                            for c in range(2):
                                for x in range(K):
                                    ins = pe.transpose(psum[:, 2 * (n % 2) + c, x * P:(x + 1) * P],
                                                       wt[:, n % 2, x, c, :], ident)
                            ins.then_inc(s["tp"], 1)

                        def multiply(n):
                            t, k = n // K, n % K
                            pe.wait_ge(s["wT"], b * NU + n + 1)
                            if k == 0 and t >= 2:
                                pe.wait_ge(s["val_ok"], b * NT + t - 1)
                            elif k == 0:
                                pe.wait_ge(s["val_ok"], b * NT)
                            if n == 0:
                                pe.wait_ge(s["rows_ok"], b + 1)
                            for x, c in ((0, 0), (1, 0), (0, 1), (1, 1), (2, 0), (2, 1)):
                                sl, at = tap(k, x)
                                lo = (t % 2) * C
                                dst = (psum[at:at + C, 4 + t % 2, sl * P:(sl + 1) * P] if sl < 4
                                       else psum[lo:lo + C, 6, 0:P])
                                ins = pe.matmul(dst, rows[:, u, k, t + c, :], wtT[:, n % 2, c, x, :],
                                                start=(c == 0), stop=(c == 1))
                            ins.then_inc(s["mm"], 1)

                        turn(0)
                        for n in range(NU):
                            if n + 1 < NU:
                                turn(n + 1)
                            multiply(n)
                        pe.wait_ge(s["val_ok"], b * NT + NT)
                        pe.wait_ge(s["x1"], b)
                        product_over_kernel(pe, s["ko_mm"])
                        pe.sem_inc(s["rows_free"], 1)
                        pe.wait_ge(s["ko_sb"], b + 1)
                        back_to_tokens(pe, s["xo_t"])
                with pe.Else():
                    with pe.Fori(0, B) as b:
                        pe.wait_ge(s["g_rows"], b + 1)
                        pe.sem_inc(s_past, 1)
                        with pe.Fori(0, NT) as t:
                            bt = b * NT + t
                            pe.wait_ge(s["g_val"], bt)
                            for k in range(K):
                                for c in range(NCH):
                                    pe.wait_ge(s["g_w"], bt * K * NCH + (k * NCH + c + 1))
                                    pe.wait_ge(s["g_ev"], bt * K * NCH + (k * NCH + c))
                                    for x in range(K):
                                        ins = pe.transpose(psum[:, 0, x * P:(x + 1) * P], wt[:, 0, x, 0, :], ident)
                                    ins.then_inc(s["g_tp"], 1)
                                pe.wait_ge(s["g_ev"], bt * K * NCH + (k + 1) * NCH)
                                for x in range(K):
                                    sl, at = tap(k, x)
                                    dst = psum[at:at + C, 4, sl * P:(sl + 1) * P] if sl < 4 else psum[0:C, 6, 0:P]
                                    for c in range(NCH):
                                        ins = pe.matmul(dst, rows[:, 0, k, c, :], gT[:, c, x, :],
                                                        start=(c == 0), stop=(c == NCH - 1))
                                ins.then_inc(s["g_mm"], 1)
                        pe.wait_ge(s["g_val"], b * NT + NT)
                        pe.wait_ge(s["g_x1"], b)
                        product_over_kernel(pe, s["g_ko"])
                        pe.wait_ge(s["g_kosb"], b + 1)
                        back_to_tokens(pe, s["g_xo"])
                pe.nop()


class Norm:

    PER = 5

    def __init__(self, sb, sem, cst, tag, s_past):
        self.tmp = sb(tag + "_tmp", [P, 2, NT, C])
        self.small = sb(tag + "_small", [P, 3, NT])
        self.half = cst("half")
        self.s_past = s_past
        self.step, self.var, self.eps, self.rstd = (sem(f"{tag}_{n}") for n in ("step", "var", "eps", "rstd"))

    def vector(self, dve, src, dst, b, done):
        xc, sq = self.tmp[:, 0], self.tmp[:, 1]
        v = Steps(self.step, b, self.PER)

        def spread(x):
            return x.unsqueeze(2).to_broadcast([P, NT, C])

        v.done(dve.tensor_reduce(self.small[:, 0, :], src, AX.X, ALU.add))
        dve.wait_ge(self.step, v.value())
        v.done(dve.tensor_scalar(self.small[:, 0, :], self.small[:, 0, :], -1.0 / C, None, ALU.mult))
        dve.wait_ge(self.step, v.value())
        dve.wait_ge(done, b)
        v.done(dve.tensor_tensor(xc, src, spread(self.small[:, 0, :]), ALU.add))
        dve.wait_ge(self.step, v.value())
        v.done(dve.tensor_tensor(sq, xc, xc, ALU.mult))
        dve.wait_ge(self.step, v.value())
        v.done(dve.tensor_reduce(self.small[:, 1, :], sq, AX.X, ALU.add))
        dve.wait_ge(self.rstd, b + 1)
        dve.tensor_tensor(dst, xc, spread(self.small[:, 2, :]), ALU.mult).then_inc(done, 1)

    def gpsimd(self, pool, b):
        pool.wait_ge(self.step, (b + 1) * self.PER)
        pool.sem_inc(self.s_past, 1)
        pool.tensor_scalar(self.small[:, 2, :], self.small[:, 1, :], 1.0 / C, LN_EPS, ALU.mult,
                           ALU.add).then_inc(self.eps, 1)
        pool.wait_ge(self.eps, b + 1)
        pool.tensor_tensor(self.small[:, 2, :], self.small[:, 2, :], self.half, ALU.pow).then_inc(self.rstd, 1)


def attention(nc, dram, cst, psum, tok, wqk, wv, w1, w2, b2, s_w, s_past):
    ident, mask = cst("ident"), cst("mask")
    chunks = [(t, j, min(4, t + 1 - j)) for t in range(NT) for j in range(0, t + 1, 4)]
    NCK = len(chunks)
    with ExitStack() as ctx:
        def sb(name, shape, dt=F32):
            return ctx.enter_context(nc.sbuf_tensor(name, shape, dt))

        def sem(name):
            return ctx.enter_context(nc.semaphore(name))

        norm = Norm(sb, sem, cst, "an", s_past)
        ln = sb("ln", [P, 2, NT, C])
        lnT = sb("lnT", [C + 1, T])
        qT = sb("qT", [C, T])
        kT = sb("kT", [C, T])
        v = sb("v", [P, NT, C + 1])
        negmax = sb("negmax", [P, NT])
        prob = sb("prob", [P, 2, T])
        pT = sb("pT", [P, NT, T])
        oT = sb("oT", [C + 1, T])
        rsum = sb("rsum", [P, NT])
        att = sb("att", [P, NT, C])
        s = {n: sem("a_" + n) for n in
             "ones ln xt lnT qk v_mm q_sb k_sb v_sb sc mx ex pt pe_a pe_v pv oT ot rs at x2".split()}
        scale = 1.0 / float(np.sqrt(C))

        def scores(t):
            return psum[:, 2 * (t % 2):2 * (t % 2) + 2, :].rearrange("p a q -> p (a q)")

        def leave_prob(dve, b, chunk):
            if chunk % 2 == 0:
                return
            t, j, nb = chunks[chunk]
            dve.wait_ge(s["pt"], b * NCK + chunk + 1)
            dve.tensor_copy(pT[:, j:j + nb, t * P:(t + 1) * P],
                            psum[:, 5, 0:nb * P].rearrange("p (j q) -> p j q", q=P)).then_inc(s["pe_v"], 1)

        def last_chunk(t):
            return max(n for n, c in enumerate(chunks) if c[0] == t)

        def act_leave(act, b, chunk):
            if chunk % 2 == 1:
                return
            t, j, nb = chunks[chunk]
            act.wait_ge(s["pt"], b * NCK + chunk + 1)
            act.activation(pT[:, j:j + nb, t * P:(t + 1) * P],
                           psum[:, 4, 0:nb * P].rearrange("p (j q) -> p j q", q=P),
                           ACT.Copy).then_inc(s["pe_a"], 1)

        with nc.Block() as block:
            @block.sync
            def _(sync):
                sync.dma_start(w1[:, :, :], dram["w1"]).then_inc(s_w, 16)
                sync.dma_start(w2[:, :, :, :], dram["w2"]).then_inc(s_w, 16)
                sync.dma_start(b2[:, :], dram["b2"]).then_inc(s_w, 16)

            @block.gpsimd
            def _(pool):
                pool.memset(lnT[C:C + 1, :], 1.0).then_inc(s["ones"], 1)
                pool.wait_ge(s["ones"], 1)
                pool.memset(v[:, :, C:C + 1], 1.0).then_inc(s["ones"], 1)
                for u, b, i in each_image(pool):
                    norm.gpsimd(pool, b)

            @block.vector
            def _(dve):
                dve.sem_inc(s["xt"], 1)
                for u, b, i in each_image(dve):
                    dve.wait_ge(s["xt"], b)
                    norm.vector(dve, tok[:, b], ln[:, u], b, s["ln"])
                    dve.wait_ge(s["qk"], b + 1)
                    dve.tensor_copy(kT[:, :], psum[C:P, 2:4, :].rearrange("c a q -> c (a q)")).then_inc(s["k_sb"], 1)
                    chunk = 0
                    for t in range(NT):
                        dve.wait_ge(s["sc"], b * NT + t + 1)
                        dve.tensor_reduce(negmax[:, t:t + 1], scores(t)[:, 0:(t + 1) * P], AX.X, ALU.max,
                                          negate=True).then_inc(s["mx"], 1)
                        while t > 0 and chunk < NCK and chunks[chunk][0] == t - 1:
                            leave_prob(dve, b, chunk)
                            chunk += 1
                    while chunk < NCK:
                        leave_prob(dve, b, chunk)
                        chunk += 1
                    dve.wait_ge(s["ot"], b + 1)
                    o = psum[:, 4:6, 0:4 * (C + 1)].rearrange("p a (t f) -> p a t f", f=C + 1)
                    dve.reciprocal(rsum[:, :].rearrange("p (a t) -> p a t", a=2), o[:, :, :, C]).then_inc(s["rs"], 1)
                    dve.wait_ge(s["rs"], b + 1)
                    dve.tensor_tensor(att.rearrange("p (a t) f -> p a t f", a=2), o[:, :, :, 0:C],
                                      rsum[:, :].rearrange("p (a t) -> p a t", a=2).unsqueeze(3)
                                      .to_broadcast([P, 2, 4, C]), ALU.mult).then_inc(s["at"], 1)
                    dve.wait_ge(s["at"], b + 1)
                    dve.tensor_tensor(tok[:, b], tok[:, b], att[:, :, :], ALU.add).then_inc(s["x2"], 1)
                dve.wait_ge(s["x2"], B)

            @block.scalar
            def _(act):
                for u, b, i in each_image(act):
                    act.wait_ge(s["xt"], b + 2)
                    act.wait_ge(s["v_mm"], b)
                    act.activation(lnT[0:C, :], psum[0:C, 0:2, :].rearrange("c a q -> c (a q)"),
                                   ACT.Copy).then_inc(s["lnT"], 1)
                    act.wait_ge(s["qk"], b + 1)
                    act.activation(qT[:, :], psum[0:C, 2:4, :].rearrange("c a q -> c (a q)"), ACT.Copy,
                                   scale=scale).then_inc(s["q_sb"], 1)
                    act.wait_ge(s["v_mm"], b + 1)
                    act.activation(v[:, :, 0:C], psum[:, 4, :].rearrange("p (t f) -> p t f", f=C),
                                   ACT.Copy).then_inc(s["v_sb"], 1)
                    chunk = 0
                    for t in range(NT):
                        act.wait_ge(s["mx"], b * NT + t + 1)
                        if t >= 2:
                            act.wait_ge(s["pt"], b * NCK + last_chunk(t - 2) + 1)
                        else:
                            act.wait_ge(s["pt"], b * NCK)
                        act.activation(prob[:, t % 2, 0:(t + 1) * P], scores(t)[:, 0:(t + 1) * P], ACT.Exp,
                                       bias=negmax[:, t:t + 1]).then_inc(s["ex"], 1)
                        while t > 0 and chunk < NCK and chunks[chunk][0] == t - 1:
                            act_leave(act, b, chunk)
                            chunk += 1
                    while chunk < NCK:
                        act_leave(act, b, chunk)
                        chunk += 1
                    act.wait_ge(s["pv"], b + 1)
                    act.activation(oT[:, :], psum[0:C + 1, 6:8, :].rearrange("c a q -> c (a q)"),
                                   ACT.Copy).then_inc(s["oT"], 1)

            @block.tensor
            def _(pe):
                HC = NCK // 2
                pe.wait_ge(s["ones"], 2)
                for u, b, i in each_image(pe):
                    pe.wait_ge(s["ln"], b + 1)
                    pe.wait_ge(s["lnT"], b)
                    pe.wait_ge(s["ex"], b * NT)
                    pe.sem_inc(s_past, 1)
                    for t in range(NT):
                        ins = pe.transpose(psum[0:C, t // 4, (t % 4) * P:(t % 4 + 1) * P], ln[:, u, t, :], ident)
                    ins.then_inc(s["xt"], 1)
                    pe.wait_ge(s["lnT"], b + 1)
                    for h in range(2):
                        ins = pe.matmul(psum[:, 2 + h, :], wqk[:, :], lnT[:, h * HB:(h + 1) * HB],
                                        start=True, stop=True)
                    ins.then_inc(s["qk"], 1)
                    pe.wait_ge(s["at"], b)
                    for t in range(NT):
                        ins = pe.matmul(psum[:, 4, t * C:(t + 1) * C], lnT[:, t * P:(t + 1) * P], wv[:, :],
                                        start=True, stop=True)
                    ins.then_inc(s["v_mm"], 1)
                    pe.wait_ge(s["q_sb"], b + 1)
                    pe.wait_ge(s["k_sb"], b + 1)

                    def score(t):
                        if t >= 2:
                            pe.wait_ge(s["ex"], b * NT + t - 1)
                        for h in range(t // 4 + 1):
                            n = min(HB, (t + 1) * P - h * HB)
                            ins = pe.matmul(psum[:, 2 * (t % 2) + h, 0:n], qT[:, t * P:(t + 1) * P],
                                            kT[:, h * HB:h * HB + n], start=True, stop=(h < t // 4))
                        ins = pe.matmul(scores(t)[:, t * P:(t + 1) * P], ident, mask, start=False, stop=True)
                        ins.then_inc(s["sc"], 1)

                    score(0)
                    for n, (t, j, nb) in enumerate(chunks):
                        if j == 0 and t + 1 < NT:
                            score(t + 1)
                        if j == 0:
                            pe.wait_ge(s["ex"], b * NT + t + 1)
                        if n == 0:
                            pe.wait_ge(s["v_sb"], b + 1)
                        sem_out, done = (s["pe_a"], n // 2) if n % 2 == 0 else (s["pe_v"], n // 2)
                        pe.wait_ge(sem_out, b * HC + done)
                        for m in range(nb):
                            ins = pe.transpose(psum[:, 4 + n % 2, m * P:(m + 1) * P],
                                               prob[:, t % 2, (j + m) * P:(j + m + 1) * P], ident)
                        ins.then_inc(s["pt"], 1)
                    pe.wait_ge(s["pe_a"], b * HC + HC)
                    pe.wait_ge(s["pe_v"], b * HC + HC)
                    pe.wait_ge(s["oT"], b)
                    for h in range(2):
                        for j in range(4 * h + 4):
                            q0 = max(j * P, h * HB)
                            ins = pe.matmul(psum[0:C + 1, 6 + h, q0 - h * HB:HB], v[:, j, :],
                                            pT[:, j, q0:(h + 1) * HB], start=(j == 0), stop=(j == 4 * h + 3))
                    ins.then_inc(s["pv"], 1)
                    pe.wait_ge(s["oT"], b + 1)
                    pe.sem_inc(s_past, 1)
                    for t in range(NT):
                        ins = pe.transpose(psum[:, 4 + t // 4, (t % 4) * (C + 1):(t % 4 + 1) * (C + 1)],
                                           oT[:, t * P:(t + 1) * P], ident[0:C + 1, 0:C + 1])
                    ins.then_inc(s["ot"], 1)


def route(nc, cst, psum, tok, gate, pm, pooled_t, s_past):
    ident = cst("ident")
    with ExitStack() as ctx:
        def sb(name, shape, dt=F32):
            return ctx.enter_context(nc.sbuf_tensor(name, shape, dt))

        def sem(name):
            return ctx.enter_context(nc.semaphore(name))

        norm = Norm(sb, sem, cst, "rn", s_past)
        ln = sb("rln", [P, GI, NT, C])
        lnT = sb("rlnT", [C + 1, 2, T])
        nmx = sb("nmx", [P, 2])
        ex = sb("ex", [P, T])
        pr = sb("pr", [P, T])
        left = sb("left", [P, T])
        taken = sb("taken", [P, T])
        top = sb("top", [P, TOP])
        tsum = sb("tsum", [P, 2])
        takenT = sb("takenT", [P, NT, P])
        pool_sb = sb("pool_sb", [P, C])
        s = {n: sem("r_" + n) for n in "ones ln xt lnT lg mx ex rc pr top rep tk kept tt tT po po_sb pt pT".split()}
        logits = psum[:, 2:4, :].rearrange("p a q -> p (a q)")

        with nc.Block() as block:
            @block.gpsimd
            def _(pool):
                pool.memset(lnT[C:C + 1, :, :], 1.0).then_inc(s["ones"], 1)
                pool.wait_ge(s["ones"], 1)
                pool.memset(pooled_t[C:C + 1, :, :], 1.0).then_inc(s["ones"], 1)
                pool.wait_ge(s["ones"], 2)
                with pool.Fori(0, NG) as g:
                    for u in range(GI):
                        norm.gpsimd(pool, g * GI + u)
                    pool.wait_ge(s["tk"], g + 1)
                    pool.tensor_copy(pm[:, g, :], taken[:, :]).then_inc(s["kept"], 1)
                pool.wait_ge(s["kept"], NG)

            @block.vector
            def _(dve):
                with dve.Fori(0, NG) as g:
                    dve.wait_ge(s["po"], g)
                    for u in range(GI):
                        b = g * GI + u
                        norm.vector(dve, tok[:, b], ln[:, u], b, s["ln"])
                    dve.wait_ge(s["lg"], g * GI + GI)
                    dve.tensor_reduce(nmx[:, 0:1], logits, AX.X, ALU.max, negate=True).then_inc(s["mx"], 1)
                    dve.wait_ge(s["ex"], g + 1)
                    dve.reciprocal(tsum[:, 1:2], tsum[:, 0:1]).then_inc(s["rc"], 1)
                    dve.wait_ge(s["rc"], g + 1)
                    dve.tensor_scalar(pr[:, :], ex[:, :], tsum[:, 1:2], None, ALU.mult).then_inc(s["pr"], 1)
                    dve.wait_ge(s["pr"], g + 1)
                    dve.sem_inc(s_past, 1)
                    dve.max(top[:, :], pr[:, :]).then_inc(s["top"], 1)
                    dve.wait_ge(s["top"], g + 1)
                    dve.sem_inc(s_past, 1)
                    dve.match_replace(left[:, :], top[:, :], pr[:, :], -1.0).then_inc(s["rep"], 1)
                    dve.wait_ge(s["rep"], g + 1)
                    dve.wait_ge(s["kept"], g)
                    dve.scalar_tensor_tensor(taken[:, :], left[:, :], 0.0, pr[:, :], ALU.is_lt,
                                             ALU.mult).then_inc(s["tk"], 1)
                    dve.wait_ge(s["po"], g + 1)
                    dve.tensor_copy(pool_sb[:, :], psum[:, 6, 0:C]).then_inc(s["po_sb"], 1)
                dve.wait_ge(s["po_sb"], NG)

            @block.scalar
            def _(act):
                with act.Fori(0, NG) as g:
                    for u in range(GI):
                        b = g * GI + u
                        act.wait_ge(s["xt"], b + 1)
                        act.activation(lnT[0:C, u % 2, :], psum[0:C, 0:2, :].rearrange("c a q -> c (a q)"),
                                       ACT.Copy).then_inc(s["lnT"], 1)
                    act.wait_ge(s["mx"], g + 1)
                    act.activation(ex[:, :], logits, ACT.Exp, bias=nmx[:, 0:1],
                                   accum_out=tsum[:, 0:1]).then_inc(s["ex"], 1)
                    act.wait_ge(s["tt"], g + 1)
                    act.activation(takenT.rearrange("p a q -> p (a q)"),
                                   psum[:, 4:6, :].rearrange("p a q -> p (a q)"), ACT.Copy).then_inc(s["tT"], 1)
                    act.wait_ge(s["pt"], g + 1)
                    act.activation(pooled_t[0:C, bass.ds(g * GI, GI), :],
                                   psum[0:C, 7, 0:P].rearrange("c (u e) -> c u e", u=GI),
                                   ACT.Copy).then_inc(s["pT"], 1)
                act.wait_ge(s["pT"], NG)

            @block.tensor
            def _(pe):
                pe.wait_ge(s["ones"], 2)
                with pe.Fori(0, NG) as g:
                    pe.wait_ge(s["ex"], g)
                    for u in range(GI):
                        b = g * GI + u
                        pe.wait_ge(s["ln"], b + 1)
                        pe.wait_ge(s["lnT"], b)
                        pe.sem_inc(s_past, 1)
                        for t in range(NT):
                            ins = pe.transpose(psum[0:C, t // 4, (t % 4) * P:(t % 4 + 1) * P], ln[:, u, t, :], ident)
                        ins.then_inc(s["xt"], 1)
                        pe.wait_ge(s["lnT"], b + 1)
                        for h in range(2):
                            ins = pe.matmul(psum[E * u:E * u + E, 2 + h, :], gate[:, :],
                                            lnT[:, u % 2, h * HB:(h + 1) * HB], start=True, stop=True)
                        ins.then_inc(s["lg"], 1)
                    pe.wait_ge(s["tk"], g + 1)
                    for t in range(NT):
                        ins = pe.transpose(psum[:, 4 + t // 4, (t % 4) * P:(t % 4 + 1) * P],
                                           taken[:, t * P:(t + 1) * P], ident)
                    ins.then_inc(s["tt"], 1)
                    pe.wait_ge(s["tT"], g + 1)
                    pe.wait_ge(s["po_sb"], g)
                    for t in range(NT):
                        for u in range(GI):
                            ins = pe.matmul(psum[E * u:E * u + E, 6, 0:C], takenT[:, t, E * u:E * u + E],
                                            ln[:, u, t, :], start=(t == 0), stop=(t == NT - 1))
                    ins.then_inc(s["po"], 1)
                    pe.wait_ge(s["po_sb"], g + 1)
                    pe.wait_ge(s["pT"], g)
                    pe.sem_inc(s_past, 1)
                    pe.transpose(psum[0:C, 7, 0:P], pool_sb[:, :], ident).then_inc(s["pt"], 1)


def mlp(nc, cst, psum, w1, w2, b2, s_w, pooled_t, expert_out):
    ident = cst("ident")
    with ExitStack() as ctx:
        def sb(name, shape, dt=F32):
            return ctx.enter_context(nc.sbuf_tensor(name, shape, dt))

        def sem(name):
            return ctx.enter_context(nc.semaphore(name))

        hT = sb("hT", [P, E, 2, B])
        oT = sb("moT", [C, B, E])
        s = {n: sem("e_" + n) for n in "h gelu o oT t out".split()}
        with nc.Block() as block:
            @block.tensor
            def _(pe):
                pe.wait_ge(s_w, 16 * 3)
                for e in range(E):
                    for h in range(2):
                        ins = pe.matmul(psum[:, 0, (2 * e + h) * B:(2 * e + h + 1) * B],
                                        w1[:, e, h * P:(h + 1) * P], pooled_t[:, :, e], start=True, stop=True)
                ins.then_inc(s["h"], 1)
                pe.wait_ge(s["gelu"], 1)
                for e in range(E):
                    for h in range(2):
                        ins = pe.matmul(psum[0:C, 1, e * B:(e + 1) * B], w2[:, h, e, :], hT[:, e, h, :],
                                        start=(h == 0), stop=(h == 1))
                ins.then_inc(s["o"], 1)
                pe.wait_ge(s["oT"], 1)
                for g in range(NG):
                    ins = pe.transpose(psum[:, 2, g * C:(g + 1) * C],
                                       oT[:, g * GI:(g + 1) * GI, :].rearrange("c u e -> c (u e)"), ident[0:C, 0:C])
                ins.then_inc(s["t"], 1)

            @block.scalar
            def _(act):
                act.wait_ge(s["h"], 1)
                act.activation(hT.rearrange("p e h b -> p (e h b)"), psum[:, 0, :], ACT.Gelu).then_inc(s["gelu"], 1)
                act.wait_ge(s["t"], 1)
                act.activation(expert_out.rearrange("p g f -> p (g f)"), psum[:, 2, 0:NG * C],
                               ACT.Copy).then_inc(s["out"], 1)
                act.wait_ge(s["out"], 1)

            @block.vector
            def _(dve):
                dve.wait_ge(s["o"], 1)
                dve.tensor_tensor(oT.rearrange("c b e -> c e b"),
                                  psum[0:C, 1, 0:E * B].rearrange("c (e b) -> c e b", b=B),
                                  b2[:, :].unsqueeze(2).to_broadcast([C, E, B]), ALU.add).then_inc(s["oT"], 1)


def combine(nc, psum, tok, pm, expert_out, out_blk):
    with ExitStack() as ctx:
        def sb(name, shape, dt=F32):
            return ctx.enter_context(nc.sbuf_tensor(name, shape, dt))

        def sem(name):
            return ctx.enter_context(nc.semaphore(name))

        pm_now = sb("pm_now", [P, 2, T])
        out_now = sb("out_now", [P, 2, C])
        res = sb("res", [P, GI, NT, C])
        s = {n: sem("f_" + n) for n in "pm eo y x".split()}
        s_st = [sem(f"f_st{u}") for u in range(GI)]
        with nc.Block() as block:
            @block.gpsimd
            def _(pool):
                for g in range(NG):
                    pool.tensor_copy(out_now[:, g, :], expert_out[:, g, :]).then_inc(s["eo"], 1)
                    pool.tensor_copy(pm_now[:, g, :], pm[:, g, :]).then_inc(s["pm"], 1)

            @block.tensor
            def _(pe):
                for g in range(NG):
                    pe.wait_ge(s["eo"], g + 1)
                    pe.wait_ge(s["pm"], g + 1)
                    for u in range(GI):
                        pe.wait_ge(s["x"], max(0, g * GI + u - GI + 1))
                        rows = slice(E * u, E * u + E)
                        for t in range(NT):
                            ins = pe.matmul(psum[:, u, t * C:(t + 1) * C], pm_now[rows, g, t * P:(t + 1) * P],
                                            out_now[rows, g, :], start=True, stop=True)
                        ins.then_inc(s["y"], 1)

            @block.vector
            def _(dve):
                for g in range(NG):
                    for u in range(GI):
                        b = g * GI + u
                        dve.wait_ge(s["y"], b + 1)
                        if g:
                            dve.wait_ge(s_st[u], 16 * g)
                        dve.tensor_tensor(res[:, u], psum[:, u, :].rearrange("p (t f) -> p t f", f=C), tok[:, b],
                                          ALU.add).then_inc(s["x"], 1)

            @block.sync
            def _(sync):
                for g in range(NG):
                    for u in range(GI):
                        b = g * GI + u
                        sync.wait_ge(s["x"], b + 1)
                        sync.dma_start(out_blk[b], res[:, u]).then_inc(s_st[u], 16)
                for u in range(GI):
                    sync.wait_ge(s_st[u], 16 * NG)


def lay_out(inputs):
    f = {k: np.asarray(v) for k, v in inputs.items()}
    taps = f["L0_conv_kernel"].reshape(K * K, C, C)
    kp = np.zeros((P, SLOTS, C), np.float32)
    for n in range(K * K):
        kp[(n % 2) * C:(n % 2) * C + C, n // 2] = taps[n]
    kp[C:, SLOTS - 1] = taps[-1]
    ow = np.zeros((K, C, K, 32), np.float32)
    ow[..., :OCH] = f["L0_conv_offset_w"].transpose(0, 2, 1, 3)
    ob = np.zeros((4, 32), np.float32)
    ob[:, :OCH] = f["L0_conv_offset_b"]
    w2 = f["L1_ffn_weight2"]
    return {
        "x": f["x"],
        "const": constants()[0],
        "ow_pair": ow[0:2].reshape(P, K, 32),
        "ow_last": ow[2],
        "ob": ob.reshape(P, 1),
        "kp": kp,
        "kbias": np.tile(f["L0_conv_bias"], 2).reshape(P, 1),
        "wqk": np.concatenate([np.concatenate([f["L1_attn_Wq"], f["L1_attn_Wk"]], 1),
                               np.concatenate([f["L1_attn_bq"], f["L1_attn_bk"]])[None]], 0),
        "wv": np.concatenate([f["L1_attn_Wv"], f["L1_attn_bv"][None]], 0),
        "gate": np.concatenate([f["L1_ffn_gate_w"].T, f["L1_ffn_gate_b"][None]], 0),
        "w1": np.ascontiguousarray(f["L1_ffn_weight1"].transpose(1, 0, 2)),
        "w2": np.ascontiguousarray(w2[:, :HID].reshape(E, 2, P, C).transpose(2, 1, 0, 3)),
        "b2": np.ascontiguousarray(w2[:, HID].T),
    }


def kernel(**inputs):
    import concourse.bacc as bacc
    from concourse.bass_utils import run_bass_kernel_spmd

    nc = bacc.Bacc("TRN2", target_bir_lowering=False, num_devices=1)
    arrays = {f"in_{k}": np.ascontiguousarray(v) for k, v in lay_out(inputs).items()}
    dram = {k[3:]: nc.dram_tensor(k, a.shape, F32, kind="ExternalInput").ap() for k, a in arrays.items()}
    out = nc.dram_tensor("out", (B, H, W, C), F32, kind="ExternalOutput").ap()
    build(nc, dram, out)
    return run_bass_kernel_spmd(nc, [arrays], core_ids=[0]).results[0]["out"]
```

```python
from contextlib import ExitStack

import numpy as np

import concourse.bass as bass
from concourse import mybir

F32 = mybir.dt.float32
I32 = mybir.dt.int32
ALU = mybir.AluOpType
ACT = mybir.ActivationFunctionType
AX = mybir.AxisListType

B, H, W, C = 8, 32, 32, 64
T = H * W
P = 128
NT = T // P
BR = P // W
K = 3
NCH = NT + 1
HALO = 3
PR = 38
OCH = 2 * K * K
HB = 512
E, HID, TOP = 32, 256, 8
GI = P // E
NG = B // GI
LIMIT = 2.0
WIN = 2 * BR
GN_EPS, LN_EPS = 1e-5, 1e-5
NEG = -1e13
ONE = 1


def constants():
    p = np.arange(P)
    r, w = p // W, p % W
    ident = np.eye(P)
    same = (p[:, None] // 2 == p[None, :] // 2) * 0.5
    diff = same * np.where(p[:, None] % 2 == 0, 1.0, -1.0)
    ybase = r[:, None] + 2 - np.arange(WIN)[None, :]
    xbase = (w[:, None, None] + (np.arange(K) - 1)[None, :, None] - np.arange(W)[None, None, :]).reshape(P, -1)
    mask = np.where(p[None, :] > p[:, None], NEG, 0.0)
    half = np.full((P, NT), -0.5)
    yall = ((r + 2)[:, None, None] + BR * np.arange(NT)[None, :, None] - np.arange(BR * NCH)[None, None, :]).reshape(P, -1)
    parts = dict(ident=ident, same=same, diff=diff, ybase=ybase, xbase=xbase, mask=mask, half=half, yall=yall)
    at, cols = {}, 0
    for n, a in parts.items():
        at[n] = (cols, cols + a.shape[1])
        cols += a.shape[1]
    return np.concatenate(list(parts.values()), 1).astype(np.float32), at


def each_image(eng):
    with eng.Fori(0, B // 2) as i:
        for u in range(2):
            yield u, i * 2 + u, i


def below(value):
    return max(value, 0) if isinstance(value, int) else value


def start_at_one(nc, sems):
    with nc.Block() as block:
        @block.sync
        def _(sync):
            for x in sems[0::3]:
                sync.sem_inc(x, ONE)

        @block.gpsimd
        def _(pool):
            for x in sems[1::3]:
                pool.sem_inc(x, ONE)

        @block.vector
        def _(dve):
            for x in sems[2::3]:
                dve.sem_inc(x, ONE)


def build(nc, dram, out):
    table, at = constants()
    x_blk = dram["x"].rearrange("b (t r) w c -> b (r w) t c", r=BR)
    out_blk = out.rearrange("b (t r) w c -> b (r w) t c", r=BR)
    with ExitStack() as ctx:
        def sb(name, shape, dt=F32):
            return ctx.enter_context(nc.sbuf_tensor(name, shape, dt))

        def sem(name):
            return ctx.enter_context(nc.semaphore(name))

        const = sb("const", [P, table.shape[1]])

        def cst(name):
            return const[:, at[name][0]:at[name][1]]

        tok = sb("tok", [P, B, NT, C])
        wqk = sb("wqk", [C + 1, 2 * C])
        wv = sb("wv", [C + 1, C])
        gate = sb("gate", [C + 1, E])
        s_const, s_tok = sem("s_const"), sem("s_tok")
        s_past = sem("s_past")
        psum = ctx.enter_context(nc.psum_tensor("psum", [P, 8, HB], F32))
        with ExitStack() as conv:
            def csb(name, shape, dt=F32):
                return conv.enter_context(nc.sbuf_tensor(name, shape, dt))

            off = csb("off", [P, B, NT, OCH])
            pxn = csb("pxn", [P, B, PR, W])
            flag = csb("flag", [1, 1], I32)
            kp = csb("kp", [P, K, K * C])
            kbias = csb("kbias", [P, 1])
            prepare(nc, dram, cst, const, psum, tok, x_blk, off, pxn, flag, kp, kbias, wqk, wv, gate, s_const, s_tok, s_past)
            convolve_and_attend(nc, cst, psum, tok, off, pxn, flag, kp, kbias, wqk, wv, s_const, s_past)
        w1 = sb("w1", [C + 1, E, HID])
        w2 = sb("w2", [P, 2, E, C])
        b2 = sb("b2", [C, E])
        s_w = sem("s_w")
        pm = sb("pm", [P, NG, T])
        pooled_t = sb("pooled_t", [C + 1, B, E])
        route(nc, dram, cst, psum, tok, gate, pm, pooled_t, w1, w2, b2, s_w, s_past)
        expert_out = sb("expert_out", [P, NG, C])
        mlp(nc, cst, psum, w1, w2, b2, s_w, pooled_t, expert_out)
        combine(nc, psum, tok, pm, expert_out, out_blk)


def prepare(nc, dram, cst, const, psum, tok, x_blk, off, pxn, flag, kp, kbias, wqk, wv, gate, s_const, s_tok, s_past):
    ident = cst("ident")
    with ExitStack() as ctx:
        def sb(name, shape, dt=F32):
            return ctx.enter_context(nc.sbuf_tensor(name, shape, dt))

        def sem(name):
            return ctx.enter_context(nc.semaphore(name))

        xs = sb("xs", [P, 2, NT, 2, C])
        ow_pair = sb("ow_pair", [P, K, 32])
        ow_last = sb("ow_last", [C, K, 32])
        ob = sb("ob", [P, 1])
        img = sb("pimg", [P, 2, PR, W])
        offT = sb("offT", [P, 2, P])
        st = sb("st", [P, 2, 6])
        mv = sb("mv", [P, 2])
        gs = sb("gs", [P, 8])
        mx = sb("mx", [P, 1])
        mrow = sb("mrow", [1, 2])
        xT = [psum[:, 0:2, :], psum[:, 4:6, :]]
        offP = psum[:, 2, 0:256]
        offTok = psum[:, 6, 0:256]
        grp = psum[:, 3, 0:3]
        mxT = psum[0:1, 3, 128:256]
        s_ld = [sem(f"s_ld{u}") for u in range(2)]
        names = "xs_free x_t img_kept pad0 st mv gavg gcp vv rs1 rstd nmr pn_lo pn_hi off_mm off_sb off_t off_tok m1 m2 m3 m4".split()
        s = {n: sem("p_" + n) for n in names}
        start_at_one(nc, [s[n] for n in names])

        with nc.Block() as block:
            @block.sync
            def _(sync):
                sync.dma_start(const[:, :], dram["const"]).then_inc(s_const, 16)
                for u in range(2):
                    for copy in range(2):
                        sync.dma_start(xs[:, u, :, copy, :], x_blk[u]).then_inc(s_ld[u], 16)
                for dst, name in ((ow_pair[:, :, :], "ow_pair"), (ow_last[:, :, :], "ow_last"), (ob[:, :], "ob"),
                                  (kp[:, :, :], "kp"), (kbias[:, :], "kbias"), (wqk[:, :], "wqk"),
                                  (wv[:, :], "wv"), (gate[:, :], "gate")):
                    sync.dma_start(dst, dram[name]).then_inc(s_const, 16)
                def keep_image(b, u):
                    sync.wait_ge(s["pn_lo"], ONE + b + 1)
                    sync.wait_ge(s["pn_hi"], ONE + b + 1)
                    sync.wait_ge(s["img_kept"], ONE + 16 * b)
                    sync.dma_start(pxn[:, b], img[:, u]).then_inc(s["img_kept"], 16)

                with sync.Fori(0, B // 2 - 1) as i:
                    for u in range(2):
                        b = i * 2 + 2 + u
                        sync.wait_ge(s["xs_free"], ONE + b - 1)
                        sync.wait_ge(s_ld[u], i * 32 + 32)
                        sync.dma_start(xs[:, u, :, 0, :], x_blk[b]).then_inc(s_ld[u], 16)
                        sync.dma_start(xs[:, u, :, 1, :], x_blk[b]).then_inc(s_ld[u], 16)
                        keep_image(i * 2 + u, u)
                keep_image(B - 2, 0)
                keep_image(B - 1, 1)
                sync.wait_ge(s["img_kept"], ONE + 16 * B)
                for b in range(B):
                    sync.dma_start(tok[:, b, :, :], x_blk[b]).then_inc(s_tok, 16)
                sync.wait_ge(s_tok, 16 * B)

            @block.gpsimd
            def _(pool):
                pool.memset(img[:, :, :, :], 0.0).then_inc(s["pad0"], 1)
                with pool.Fori(0, B) as b:
                    pool.wait_ge(s["vv"], ONE + b + 1)
                    pool.sem_inc(s_past, 1)
                    pool.tensor_scalar(gs[:, 3:4], gs[:, 3:4], GN_EPS, None, ALU.add).then_inc(s["rs1"], 1)
                    pool.wait_ge(s["rs1"], ONE + b + 1)
                    pool.tensor_tensor(gs[:, 4:5], gs[:, 3:4], cst("half")[:, 0:1], ALU.pow).then_inc(s["rstd"], 1)

            @block.tensor
            def _(pe):
                def to_channels(b, u, i):
                    pe.wait_ge(s_ld[u], i * 32 + 32)
                    pe.wait_ge(s["pn_lo"], below(ONE + b - 1))
                    pe.wait_ge(s["pn_hi"], below(ONE + b - 1))
                    pe.sem_inc(s_past, 1)
                    for t in range(NT):
                        ins = pe.transpose(xT[u][:, t // 4, (t % 4) * P:(t % 4 + 1) * P],
                                           xs[:, u, t, :, :].rearrange("p a c -> p (a c)"), ident)
                    ins.then_inc(s["x_t"], 1)

                def group_sums(b):
                    pe.wait_ge(s["mv"], ONE + b + 1)
                    pe.matmul(grp[:, 0:2], cst("same"), mv[:, :], start=True, stop=True).then_inc(s["xs_free"], 1)
                    pe.matmul(grp[:, 2:3], cst("diff"), mv[:, 0:1], start=True, stop=True).then_inc(s["gavg"], 1)

                def offsets(b, u):
                    pe.wait_ge(s["pn_lo"], ONE + b + 1)
                    pe.wait_ge(s["pn_hi"], ONE + b + 1)
                    pe.wait_ge(s["off_sb"], ONE + b)
                    for n, kx in enumerate((1, 0, 2)):
                        a, z = max(0, 1 - kx), min(W, W + 1 - kx)
                        for j in range(4):
                            pe.matmul(offP[32 * j:32 * j + 32, :].rearrange("m (h w) -> m h w", w=W)[:, :, a:z],
                                      ow_pair[:, kx, :],
                                      img[:, u, 8 * j + 2:8 * j + 10, a + kx - 1:z + kx - 1],
                                      start=(n == 0), stop=False)
                    for n, kx in enumerate((0, 2, 1)):
                        a, z = max(0, 1 - kx), min(W, W + 1 - kx)
                        for j in range(4):
                            ins = pe.matmul(offP[32 * j:32 * j + 32, :].rearrange("m (h w) -> m h w", w=W)[:, :, a:z],
                                            ow_last[:, kx, :],
                                            img[0:C, u, 8 * j + 4:8 * j + 12, a + kx - 1:z + kx - 1],
                                            start=False, stop=(n == K - 1))
                    ins.then_inc(s["off_mm"], 1)

                def offsets_to_tokens(b):
                    pe.wait_ge(s["off_sb"], ONE + b + 1)
                    pe.wait_ge(s["off_tok"], ONE + b)
                    for h in range(2):
                        ins = pe.transpose(offTok[:, h * P:(h + 1) * P], offT[:, h, :], ident)
                    ins.then_inc(s["off_t"], 1)

                pe.wait_ge(s_const, 16 * 9)
                to_channels(0, 0, 0)
                group_sums(0)
                to_channels(1, 1, 0)
                with pe.Fori(0, B // 2 - 1) as i:
                    for u in range(2):
                        b = i * 2 + 1 + u
                        group_sums(b)
                        to_channels(b + 1, u, i + 1)
                        offsets(i * 2 + u, u)
                        offsets_to_tokens(i * 2 + u)
                group_sums(B - 1)
                for b in (B - 2, B - 1):
                    offsets(b, b % 2)
                    offsets_to_tokens(b)
                pe.wait_ge(s["m1"], ONE + 1)
                pe.transpose(mxT, mx[:, :], ident).then_inc(s["m2"], 1)

            @block.scalar
            def _(act):
                def normalise(b, u):
                    act.wait_ge(s["nmr"], ONE + b + 1)
                    act.wait_ge(s["off_mm"], below(ONE + b - 1))
                    act.wait_ge(s["img_kept"], below(ONE + 16 * (b - 1)))
                    act.activation(img[0:C, u, HALO:HALO + H, :],
                                   xT[u][0:C, :, :].rearrange("c a (h w) -> c (a h) w", w=W), ACT.Identity,
                                   bias=gs[0:C, 5:6], scale=gs[0:C, 4:5]).then_inc(s["pn_lo"], 1)

                def leave(b):
                    act.wait_ge(s["off_mm"], ONE + b + 1)
                    act.wait_ge(s["off_t"], ONE + b)
                    act.activation(offT[:, :, :], offP.rearrange("p (h q) -> p h q", h=2), ACT.Identity,
                                   bias=ob[:, 0:1]).then_inc(s["off_sb"], 1)

                act.wait_ge(s_const, 16 * 9)
                act.wait_ge(s["pad0"], ONE + 1)
                normalise(0, 0)
                with act.Fori(0, B // 2 - 1) as i:
                    normalise(i * 2 + 1, 1)
                    leave(i * 2)
                    normalise(i * 2 + 2, 0)
                    leave(i * 2 + 1)
                normalise(B - 1, 1)
                leave(B - 2)
                leave(B - 1)

            @block.vector
            def _(dve):
                def statistics(b, u):
                    dve.wait_ge(s["x_t"], ONE + b + 1)
                    dve.bn_stats(st[:, 0, :], xT[u][:, 0, :]).then_inc(s["st"], 1)
                    dve.bn_stats(st[:, 1, :], xT[u][:, 1, :]).then_inc(s["st"], 1)
                    dve.wait_ge(s["st"], ONE + b * 2 + 2)
                    dve.wait_ge(s["gavg"], ONE + b)
                    dve.sem_inc(s_past, 1)
                    dve.bn_aggr(mv[:, :], st[:, :, :]).then_inc(s["mv"], 1)

                def normalise(b, u):
                    dve.wait_ge(s["gavg"], ONE + b + 1)
                    dve.wait_ge(s["pn_lo"], ONE + b)
                    dve.wait_ge(s["pn_hi"], ONE + b)
                    dve.tensor_copy(gs[:, 0:3], grp).then_inc(s["gcp"], 1)
                    dve.wait_ge(s["gcp"], ONE + b + 1)
                    dve.scalar_tensor_tensor(gs[:, 3:4], gs[:, 2:3], gs[:, 2:3], gs[:, 1:2],
                                             ALU.mult, ALU.add).then_inc(s["vv"], 1)
                    dve.wait_ge(s["rstd"], ONE + b + 1)
                    dve.scalar_tensor_tensor(gs[:, 5:6], gs[:, 0:1], -1.0, gs[:, 4:5],
                                             ALU.mult, ALU.mult).then_inc(s["nmr"], 1)
                    dve.wait_ge(s["nmr"], ONE + b + 1)
                    dve.wait_ge(s["off_mm"], below(ONE + b - 1))
                    dve.wait_ge(s["img_kept"], below(ONE + 16 * (b - 1)))
                    dve.tensor_scalar(img[C:P, u, HALO - 1:HALO - 1 + H, :],
                                      xT[u][C:P, :, :].rearrange("c a (h w) -> c (a h) w", w=W),
                                      gs[C:P, 4:5], gs[C:P, 5:6], ALU.mult, ALU.add).then_inc(s["pn_hi"], 1)

                def keep_offsets(b):
                    dve.wait_ge(s["off_t"], ONE + b + 1)
                    dve.tensor_copy(off[:, b, :, :].rearrange("p (j h) o -> p j h o", h=2),
                                    offTok.rearrange("p (h j o) -> p j h o", h=2, j=4)[:, :, :, 0:OCH]
                                    ).then_inc(s["off_tok"], 1)

                dve.wait_ge(s["pad0"], ONE + 1)
                statistics(0, 0)
                normalise(0, 0)
                statistics(1, 1)
                with dve.Fori(0, B // 2 - 1) as i:
                    normalise(i * 2 + 1, 1)
                    statistics(i * 2 + 2, 0)
                    keep_offsets(i * 2)
                    normalise(i * 2 + 2, 0)
                    statistics(i * 2 + 3, 1)
                    keep_offsets(i * 2 + 1)
                normalise(B - 1, 1)
                keep_offsets(B - 2)
                keep_offsets(B - 1)
                dve.wait_ge(s["off_tok"], ONE + B)
                dve.tensor_reduce(mx[:, :], off.rearrange("p b t (k d) -> p (b t k) d", d=2)[:, :, 0], AX.X, ALU.max,
                                  apply_absolute_value=True).then_inc(s["m1"], 1)
                dve.wait_ge(s["m2"], ONE + 1)
                dve.tensor_reduce(mrow[:, 0:1], mxT, AX.X, ALU.max).then_inc(s["m3"], 1)
                dve.wait_ge(s["m3"], ONE + 1)
                dve.tensor_scalar(flag[:, :], mrow[:, 0:1], LIMIT, None, ALU.is_ge).then_inc(s["m4"], 1)
                dve.wait_ge(s["m4"], ONE + 1)


def convolve_and_attend(nc, cst, psum, tok, off, pxn, flag, kp, kbias, wqk, wv, s_const, s_past):
    ident, mask = cst("ident"), cst("mask")
    NU = NT // 2 * K * K
    XN = NT * K * K * W
    YN = NT * K * K * WIN
    NW = 4
    DEEP = 4
    with ExitStack() as ctx:
        def sb(name, shape, dt=F32):
            return ctx.enter_context(nc.sbuf_tensor(name, shape, dt))

        def sem(name):
            return ctx.enter_context(nc.semaphore(name))

        img = sb("img", [P, 2, PR, W])
        mix = sb("mix", [P, 2, K, NCH, K * C])
        tent = sb("tent", [P, 2, XN + YN])
        wt = sb("wt", [P, NW, 2, 2, P])
        wtT = sb("wtT", [P, NW, 2, 2, P])
        conv_sb = sb("conv_sb", [P, HB])
        norm = Norm(sb, sem, cst, "an", s_past)
        ln = sb("ln", [P, NT, C])
        lnT = sb("lnT", [C + 1, T])
        qT = sb("qT", [C, T])
        kT = sb("kT", [C, T])
        v = sb("v", [P, NT, C])
        negmax = sb("negmax", [P, NT])
        rsum = sb("rsum", [P, 2, NT])
        prob = sb("prob", [P, 2, T])
        pT = sb("pT", [P, DEEP, T])
        oT = sb("oT", [P, HB])
        att = sb("att", [P, NT, C])
        gT = pT.rearrange("p d t -> p (d t)")[:, 0:NCH * K * P].rearrange("p (c x q) -> p c x q", c=NCH, x=K)
        gy = att.rearrange("p t c -> p (t c)")[:, 0:K * K * BR * NCH].rearrange("p (a m) -> p a m", a=K * K)
        names = ("img_ok dist a1 tent_ok z_mm z_sb w_ok tp wT mm conv_ok xo_t x1 "
                 "ln xt lnT qk v_mm q_sb k_sb v_sb sc mx ex pt pe pv oT ot rs at x2 "
                 "g_img g_zm g_zs g_d g_a g_tent g_yd g_ya g_y g_w g_tp g_ev g_mm g_conv g_xo g_x1").split()
        s = {n: sem("c_" + n) for n in names}
        start_at_one(nc, [s[n] for n in names])
        s_ones = sem("c_ones")
        xpart = tent[:, :, 0:XN].rearrange("p u (t a q) -> p u t a q", t=NT, a=K * K)
        ypart = tent[:, :, XN:XN + YN].rearrange("p u (t a m) -> p u t a m", t=NT, a=K * K)
        xbase = cst("xbase").rearrange("p (x q) -> p x q", x=K)
        scale = 1.0 / float(np.sqrt(C))
        pieces = [(slice(0, 2), slice(c, c + 1)) for c in range(NCH)]
        pieces += [(slice(2, 3), slice(c, min(c + 2, NCH))) for c in range(0, NCH, 2)]
        NP = len(pieces)
        wide = psum[:, 4:6, :].rearrange("p a q -> p (a q)")
        chunks = [(t, j, min(4, t + 1 - j)) for t in range(NT) for j in range(0, t + 1, 4)]
        NCK = len(chunks)
        of_block = [[n for n, c in enumerate(chunks) if c[0] == t] for t in range(NT)]
        AT_BACK, AT_PIECES = 1, 4
        AT_SUM, AT_SQUARES, AT_LN, AT_QKV = 2, 4, 7, 10
        AT_SCORES = [12, 15, 18, 21, 25, 29, 33, 37]
        AT_PROBS = AT_SCORES[1:] + [AT_SCORES[-1] + 3]
        AT_VALUES = [AT_PROBS[t + 1] + 3 + t // 4 for t in range(0, NT, 2)]
        AT_OUT = AT_VALUES[-1] + 2
        AT_TENTS = [19, 23, 26, 30, 34]
        STEPS = AT_OUT + 3
        assert AT_PROBS[-1] + 2 - NU < AT_QKV and AT_OUT - NU < AT_SCORES[0]

        def distances(pool, u, b, sem_d):
            dx = off[:, b, :, :].rearrange("p t (k x d) -> p (t k) x d", k=K, d=2)[:, :, :, 1]
            pool.tensor_tensor(tent[:, u, 0:XN].rearrange("p (a x q) -> p a x q", x=K, q=W),
                               dx.unsqueeze(3).to_broadcast([P, NT * K, K, W]),
                               xbase.unsqueeze(1).to_broadcast([P, NT * K, K, W]), ALU.add).then_inc(sem_d, 1)
            dy = off[:, b, :, :].rearrange("p t (a d) -> p (t a) d", d=2)[:, :, 0]
            pool.tensor_tensor(tent[:, u, XN:XN + YN].rearrange("p (a m) -> p a m", m=WIN),
                               dy.unsqueeze(2).to_broadcast([P, NT * K * K, WIN]),
                               cst("ybase").unsqueeze(1).to_broadcast([P, NT * K * K, WIN]),
                               ALU.add).then_inc(sem_d, 1)

        def mix_piece(pe, u, m, bank, done):
            ks, cs = pieces[m]
            for n, c in enumerate(range(cs.start, cs.stop)):
                width = (ks.stop - ks.start) * K * C
                rhs = kp[:, 0:2, :] if ks.start == 0 else kp[:, 2, :]
                first = BR * c + ks.start
                ins = pe.matmul(psum[:, bank, n * width:(n + 1) * width],
                                img[:, u, first:first + BR, :].rearrange("c r w -> c (r w)"), rhs,
                                start=True, stop=True)
            ins.then_inc(done, 1)

        def keep_piece(act, u, m, bank, done):
            ks, cs = pieces[m]
            shape = dict(k=ks.stop - ks.start, c=cs.stop - cs.start)
            n = shape["k"] * shape["c"] * K * C
            act.activation(mix[:, u, ks, cs, :], psum[:, bank, 0:n].rearrange("p (k c f) -> p k c f", **shape),
                           ACT.Copy).then_inc(done, 1)

        def back_to_tokens(pe, done):
            for q in range(4):
                ins = pe.transpose(psum[:, 3, q * P:(q + 1) * P], conv_sb[:, q * P:(q + 1) * P], ident)
            ins.then_inc(done, 1)

        def add_to_tokens(dve, b, done):
            x1 = tok[:, b, :, :].rearrange("p t f -> p (t f)")
            dve.tensor_tensor(x1, psum[:, 3, :], x1, ALU.add).then_inc(done, 1)

        def load_flag(eng):
            return eng.value_load(flag[0:1, 0:1], min_val=0, max_val=1)

        def alive(b):
            return not isinstance(b, int) or 0 <= b < B

        def turns(eng, step):
            for b in range(2):
                step(b, b)
            with eng.Fori(0, B // 2 - 2) as j:
                for u in range(2):
                    step(j * 2 + 2 + u, u)
            for b in range(B - 2, B + 2):
                step(b, b % 2)

        def attention_steps(eng, attention, b, n):
            if alive(b - 2) and NU + n < STEPS:
                attention(eng, b - 2, NU + n)
            if alive(b - 1):
                attention(eng, b - 1, n)

        def query_block(n):
            return AT_SCORES.index(n) if n in AT_SCORES else None

        def prob_chunk(n):
            for c in range(2):
                if n - 2 * c in AT_PROBS:
                    t = AT_PROBS.index(n - 2 * c)
                    if c < len(of_block[t]):
                        return of_block[t][c]
            return None

        def piece_at(n):
            m, r = divmod(n - AT_PIECES, 2)
            return m if r == 0 and 0 <= m < NP else None

        def pool_distances(pool, u, b):
            pool.wait_ge(s["w_ok"], below(ONE + (b - 1) * NU))
            distances(pool, u, b, s["dist"])

        def pool_turn(pool, b, u):
            if alive(b - 1):
                norm.gpsimd(pool, tok[:, b - 1], ln[:, :, :], b - 1, s["ln"], s["xt"])
            if alive(b + 1) and alive(b):
                pool_distances(pool, 1 - u, b + 1)

        def act_tents(act, u, b, j):
            if j < NT // 2:
                act.wait_ge(s["dist"], ONE + (b + 1) * 2)
                for part in (xpart, ypart):
                    now = part[:, u, 2 * j:2 * j + 2]
                    ins = act.activation(now, now, ACT.Abs)
                ins.then_inc(s["a1"], 1)
            if j > 0:
                act.wait_ge(s["a1"], ONE + b * (NT // 2) + j)
                for part in (xpart, ypart):
                    now = part[:, u, 2 * j - 2:2 * j]
                    ins = act.activation(now, now, ACT.Relu, bias=1.0, scale=-1.0)
                ins.then_inc(s["tent_ok"], 1)

        def act_leave(act, a, n):
            t, j, nb = chunks[n]
            if j == 0 and t % 2 == 0:
                act.wait_ge(s["pv"], ONE + a * (NT // 2) + max(0, (t - DEEP) // 2 + 1))
            act.wait_ge(s["pt"], ONE + a * NCK + n + 1)
            act.activation(pT[:, t % DEEP, j * P:(j + nb) * P], psum[:, 6, 0:nb * P],
                           ACT.Copy).then_inc(s["pe"], 1)

        def act_attention(act, a, n):
            if n == AT_LN + 1:
                act.wait_ge(s["xt"], ONE + a + 1)
                act.wait_ge(s["v_mm"], ONE + a)
                act.activation(lnT[0:C, :], wide[0:C, :], ACT.Copy).then_inc(s["lnT"], 1)
            if n == AT_QKV + 1:
                act.wait_ge(s["qk"], ONE + a + 1)
                act.activation(qT[:, :], wide[0:C, :], ACT.Copy, scale=scale).then_inc(s["q_sb"], 1)
                act.wait_ge(s["v_mm"], ONE + a + 1)
                act.wait_ge(s["pv"], ONE + a * (NT // 2))
                act.activation(v.rearrange("p t f -> p (t f)"), psum[:, 6, :], ACT.Copy).then_inc(s["v_sb"], 1)
            if prob_chunk(n - 1) is not None:
                act_leave(act, a, prob_chunk(n - 1))
            t = query_block(n - 2)
            if t is not None:
                act.wait_ge(s["mx"], ONE + a * NT + t + 1)
                if t == 0:
                    act.wait_ge(s["rs"], ONE + a)
                act.activation(prob[:, t % 2, 0:(t + 1) * P], wide[:, 0:(t + 1) * P], ACT.Exp,
                               bias=negmax[:, t:t + 1], accum_out=rsum[:, 0, t:t + 1]).then_inc(s["ex"], 1)

            if n == AT_OUT - 1:
                act.wait_ge(s["pv"], ONE + (a + 1) * (NT // 2))
                act.wait_ge(s["ot"], ONE + a)
                act.activation(oT[:, :], psum[:, 7, :], ACT.Copy).then_inc(s["oT"], 1)

        def act_turn(act, b, u):
            for n in range(NU):
                if alive(b):
                    q = b * NU + n
                    act.wait_ge(s["tp"], ONE + q + 1)
                    act.wait_ge(s["mm"], below(ONE + q + 1 - NW))
                    act.activation(wtT[:, n % NW].rearrange("p x c q -> p (x c q)"),
                                   psum[:, n % 2, :], ACT.Copy).then_inc(s["wT"], 1)
                if n == 0 and alive(b - 1):
                    act.wait_ge(s["mm"], ONE + b * NU)
                    act.wait_ge(s["xo_t"], below(ONE + b - 1))
                    act.activation(conv_sb[:, :], psum[:, 2, :], ACT.Identity,
                                   bias=kbias[:, 0:1]).then_inc(s["conv_ok"], 1)
                if alive(b) and alive(b + 1):
                    if piece_at(n - 1) is not None:
                        act.wait_ge(s["z_mm"], ONE + (b + 1) * NP + piece_at(n - 1) + 1)
                        keep_piece(act, 1 - u, piece_at(n - 1), 3, s["z_sb"])
                    if n in AT_TENTS:
                        act_tents(act, 1 - u, b + 1, AT_TENTS.index(n))
                attention_steps(act, act_attention, b, n)

        def dve_attention(dve, a, n):
            if n == AT_SUM:
                dve.wait_ge(s["x1"], ONE + a + 1)
                dve.sem_inc(s_past, 1)
                norm.sums(dve, tok[:, a], a)
            if n == AT_SQUARES:
                norm.squares(dve, a)
            if n == AT_QKV + 2:
                dve.wait_ge(s["qk"], ONE + a + 1)
                dve.tensor_copy(kT[:, :], psum[C:P, 4:6, :].rearrange("c a q -> c (a q)")).then_inc(s["k_sb"], 1)
            t = query_block(n - 2)
            if t is not None:
                dve.wait_ge(s["sc"], ONE + a * NT + t + 1)
                dve.tensor_reduce(negmax[:, t:t + 1], wide[:, 0:(t + 1) * P], AX.X, ALU.max,
                                  negate=True).then_inc(s["mx"], 1)

            if n == AT_OUT:
                dve.wait_ge(s["ex"], ONE + (a + 1) * NT)
                dve.reciprocal(rsum[:, 1, :], rsum[:, 0, :]).then_inc(s["rs"], 1)
            if n == AT_OUT + 2:
                dve.wait_ge(s["ot"], ONE + a + 1)
                dve.wait_ge(s["rs"], ONE + a + 1)
                dve.tensor_tensor(att[:, :, :], psum[:, 7, :].rearrange("p (t f) -> p t f", f=C),
                                  rsum[:, 1, :].unsqueeze(2).to_broadcast([P, NT, C]), ALU.mult).then_inc(s["at"], 1)
                dve.wait_ge(s["at"], ONE + a + 1)
                dve.tensor_tensor(tok[:, a], tok[:, a], att[:, :, :], ALU.add).then_inc(s["x2"], 1)

        def dve_turn(dve, b, u):
            for n in range(NU):
                if alive(b):
                    j, tap = divmod(n, K * K)
                    q = b * NU + n
                    if tap == 0:
                        dve.wait_ge(s["tent_ok"], ONE + b * (NT // 2) + (j + 1))
                    dve.wait_ge(s["tp"], below(ONE + q + 1 - NW))
                    pair = slice(2 * j, 2 * j + 2)
                    dve.tensor_tensor(wt[:, n % NW].rearrange("p h c (m q) -> p h (c m) q", q=W),
                                      xpart[:, u, pair, tap].unsqueeze(2).to_broadcast([P, 2, WIN, W]),
                                      ypart[:, u, pair, tap].unsqueeze(3).to_broadcast([P, 2, WIN, W]),
                                      ALU.mult).then_inc(s["w_ok"], 1)
                if n == AT_BACK + 1 and alive(b - 1):
                    dve.wait_ge(s["xo_t"], ONE + b)
                    add_to_tokens(dve, b - 1, s["x1"])
                attention_steps(dve, dve_attention, b, n)

        def pe_score(pe, a, t):
            pe.wait_ge(s["ex"], ONE + a * NT + t)
            if t == 0:
                pe.wait_ge(s["q_sb"], ONE + a + 1)
                pe.wait_ge(s["k_sb"], ONE + a + 1)
            for h in range(t // 4 + 1):
                n = min(HB, (t + 1) * P - h * HB)
                pe.matmul(psum[:, 4 + h, 0:n], qT[:, t * P:(t + 1) * P], kT[:, h * HB:h * HB + n],
                          start=True, stop=(h < t // 4))
            pe.matmul(wide[:, t * P:(t + 1) * P], ident, mask, start=False, stop=True).then_inc(s["sc"], 1)

        def pe_turn_prob(pe, a, n):
            t, j, nb = chunks[n]
            pe.wait_ge(s["ex"], ONE + a * NT + t + 1)
            if n == 0:
                pe.wait_ge(s["v_sb"], ONE + a + 1)
            pe.wait_ge(s["pe"], ONE + a * NCK + n)
            for m in range(nb):
                ins = pe.transpose(psum[:, 6, m * P:(m + 1) * P],
                                   prob[:, t % 2, (j + m) * P:(j + m + 1) * P], ident)
            ins.then_inc(s["pt"], 1)

        def pe_values(pe, a, t):
            pe.wait_ge(s["pe"], ONE + a * NCK + of_block[t + 1][-1] + 1)
            if t == 0:
                pe.wait_ge(s["at"], ONE + a)
            for j in range(t + 2):
                for h in range(2):
                    if j <= t + h:
                        ins = pe.matmul(psum[C * h:C * h + C, 7, t // 2 * P:(t // 2 + 1) * P], v[:, j, :],
                                        pT[:, (t + h) % DEEP, j * P:(j + 1) * P],
                                        start=(j == 0), stop=(j == t + h))
            ins.then_inc(s["pv"], 1)

        def pe_attention(pe, a, n):
            if n == AT_LN:
                pe.wait_ge(s["ln"], ONE + a + 1)
                pe.wait_ge(s["ex"], ONE + a * NT)
                pe.sem_inc(s_past, 1)
                for t in range(NT):
                    ins = pe.transpose(psum[0:C, 4 + t // 4, (t % 4) * P:(t % 4 + 1) * P], ln[:, t, :], ident)
                ins.then_inc(s["xt"], 1)
            if n == AT_QKV:
                pe.wait_ge(s["lnT"], ONE + a + 1)
                for h in range(2):
                    ins = pe.matmul(psum[:, 4 + h, :], wqk[:, :], lnT[:, h * HB:(h + 1) * HB],
                                    start=True, stop=True)
                ins.then_inc(s["qk"], 1)
                pe.wait_ge(s["pe"], ONE + a * NCK)
                for t in range(NT):
                    ins = pe.matmul(psum[:, 6, t * C:(t + 1) * C], lnT[:, t * P:(t + 1) * P], wv[:, :],
                                    start=True, stop=True)
                ins.then_inc(s["v_mm"], 1)
            if query_block(n) is not None:
                pe_score(pe, a, query_block(n))
            if prob_chunk(n) is not None:
                pe_turn_prob(pe, a, prob_chunk(n))
            if n in AT_VALUES:
                pe_values(pe, a, 2 * AT_VALUES.index(n))

            if n == AT_OUT:
                pe.wait_ge(s["oT"], ONE + a + 1)
                for q in range(4):
                    ins = pe.transpose(psum[:, 7, q * P:(q + 1) * P], oT[:, q * P:(q + 1) * P], ident)
                ins.then_inc(s["ot"], 1)

        def turn_weights(pe, b, n):
            q = b * NU + n
            pe.wait_ge(s["w_ok"], ONE + q + 1)
            pe.wait_ge(s["wT"], below(ONE + q - 1))
            for h in range(2):
                for c in range(2):
                    ins = pe.transpose(psum[:, n % 2, (2 * h + c) * P:(2 * h + c + 1) * P],
                                       wt[:, n % NW, h, c, :], ident)
            ins.then_inc(s["tp"], 1)

        def multiply(pe, b, u, n):
            j, tap = divmod(n, K * K)
            k, x = divmod(tap, K)
            pe.wait_ge(s["wT"], ONE + b * NU + n + 1)
            if n == 0:
                pe.wait_ge(s["conv_ok"], ONE + b)
                pe.wait_ge(s["z_sb"], ONE + (b + 1) * NP)
            for c in range(2):
                for h in range(2):
                    ins = pe.matmul(psum[C * h:C * h + C, 2, j * P:(j + 1) * P],
                                    mix[:, u, k, 2 * j + h + c, x * C:(x + 1) * C], wtT[:, n % NW, h, c, :],
                                    start=(tap == 0 and c == 0), stop=(tap == K * K - 1 and c == 1))
            ins.then_inc(s["mm"], 1)

        def pe_turn(pe, b, u):
            for n in range(NU):
                if alive(b):
                    if n + 1 < NU:
                        turn_weights(pe, b, n + 1)
                    elif alive(b + 1):
                        turn_weights(pe, b + 1, 0)
                    multiply(pe, b, u, n)
                if n == AT_BACK and alive(b - 1):
                    pe.wait_ge(s["conv_ok"], ONE + b)
                    if alive(b):
                        pe.wait_ge(s["z_sb"], ONE + (b + 1) * NP)
                    back_to_tokens(pe, s["xo_t"])
                if alive(b) and alive(b + 1) and piece_at(n) is not None:
                    m = piece_at(n)
                    if m == 0:
                        pe.wait_ge(s["img_ok"], ONE + 16 * (b + 2))
                        pe.wait_ge(s["x1"], ONE + b)
                    pe.wait_ge(s["z_sb"], ONE + (b + 1) * NP + m)
                    mix_piece(pe, 1 - u, m, 3, s["z_mm"])
                attention_steps(pe, pe_attention, b, n)

        with nc.Block() as block:
            @block.sync
            def _(sync):
                large = load_flag(sync)
                with sync.If(large < 1):
                    for u in range(2):
                        sync.dma_start(img[:, u], pxn[:, u]).then_inc(s["img_ok"], 16)
                        if u == 0:
                            sync.wait_ge(s["img_ok"], ONE + 16)
                    with sync.Fori(0, B // 2 - 1) as j:
                        for u in range(2):
                            b = j * 2 + 2 + u
                            sync.wait_ge(s["img_ok"], ONE + 16 * b)
                            sync.wait_ge(s["z_mm"], ONE + (b - 1) * NP)
                            sync.dma_start(img[:, u], pxn[:, b]).then_inc(s["img_ok"], 16)
                sync.nop()

            @block.gpsimd
            def _(pool):
                pool.memset(lnT[C:C + 1, :], 1.0).then_inc(s_ones, 1)
                pool.wait_ge(s_ones, 1)
                large = load_flag(pool)
                with pool.If(large < 1):
                    pool_distances(pool, 0, 0)
                    turns(pool, lambda b, u: pool_turn(pool, b, u))
                with pool.Else():
                    with pool.Fori(0, B) as b:
                        pool.wait_ge(s["g_x1"], ONE + b)
                        pool.tensor_copy(img[:, 0, :, :], pxn[:, b, :, :]).then_inc(s["g_img"], 1)
                        distances(pool, 0, b, s["g_d"])
                    with pool.Fori(0, B) as a:
                        norm.gpsimd(pool, tok[:, a], ln[:, :, :], a, s["ln"], s["xt"])
                pool.nop()

            @block.scalar
            def _(act):
                large = load_flag(act)
                with act.If(large < 1):
                    for j in range(NT // 2 + 1):
                        act_tents(act, 0, 0, j)
                    for m in range(NP):
                        act.wait_ge(s["z_mm"], ONE + m + 1)
                        keep_piece(act, 0, m, 3 + m % 4, s["z_sb"])
                    turns(act, lambda b, u: act_turn(act, b, u))
                with act.Else():
                    with act.Fori(0, B) as b:
                        act.wait_ge(s["g_d"], ONE + b * 2 + 2)
                        act.activation(tent[:, 0, :], tent[:, 0, :], ACT.Abs).then_inc(s["g_a"], 1)
                        act.wait_ge(s["g_a"], ONE + b + 1)
                        act.activation(tent[:, 0, :], tent[:, 0, :], ACT.Relu, bias=1.0,
                                       scale=-1.0).then_inc(s["g_tent"], 1)
                        for m in range(NP):
                            act.wait_ge(s["g_zm"], ONE + b * NP + (m + 1))
                            keep_piece(act, 0, m, 3, s["g_zs"])
                        act.wait_ge(s["g_xo"], ONE + b)
                        act.sem_inc(s_past, 1)
                        with act.Fori(0, NT // 2) as jt:
                            for h in range(2):
                                bt = b * NT + jt * 2 + h
                                act.wait_ge(s["g_yd"], ONE + bt + 1)
                                act.activation(gy, gy, ACT.Abs).then_inc(s["g_ya"], 1)
                                act.wait_ge(s["g_ya"], ONE + bt + 1)
                                act.activation(gy, gy, ACT.Relu, bias=1.0, scale=-1.0).then_inc(s["g_y"], 1)
                                for k in range(K):
                                    for c in range(NCH):
                                        act.wait_ge(s["g_tp"], ONE + bt * K * NCH + (k * NCH + c + 1))
                                        if c == 0:
                                            act.wait_ge(s["g_mm"], ONE + bt * K + k)
                                        act.activation(gT[:, c, :, :].rearrange("p x q -> p (x q)"),
                                                       psum[:, 0, 0:K * P], ACT.Copy).then_inc(s["g_ev"], 1)
                                act.wait_ge(s["g_mm"], ONE + (bt + 1) * K)
                                act.activation(conv_sb[C * h:C * h + C, bass.ds(jt * P, P)], psum[0:C, 2, 0:P],
                                               ACT.Identity, bias=kbias[0:C, 0:1]).then_inc(s["g_conv"], 1)
                    with act.Fori(0, B) as a:
                        for n in range(STEPS):
                            act_attention(act, a, n)
                act.nop()

            @block.vector
            def _(dve):
                large = load_flag(dve)
                with dve.If(large < 1):
                    turns(dve, lambda b, u: dve_turn(dve, b, u))
                with dve.Else():
                    with dve.Fori(0, B) as b:
                        dve.wait_ge(s["g_tent"], ONE + b + 1)
                        dve.sem_inc(s_past, 1)
                        with dve.Fori(0, NT) as t:
                            bt = b * NT + t
                            dve.wait_ge(s["g_w"], ONE + bt * K * NCH)
                            dy = off[:, b, t, :].rearrange("p (a d) -> p a d", d=2)[:, :, 0]
                            dve.tensor_tensor(gy, dy.unsqueeze(2).to_broadcast([P, K * K, BR * NCH]),
                                              cst("yall").rearrange("p (t m) -> p t m", t=NT)[:, t, :]
                                              .unsqueeze(1).to_broadcast([P, K * K, BR * NCH]),
                                              ALU.add).then_inc(s["g_yd"], 1)
                            dve.wait_ge(s["g_y"], ONE + bt + 1)
                            for k in range(K):
                                taps = slice(k * K, (k + 1) * K)
                                for c in range(NCH):
                                    dve.wait_ge(s["g_tp"], ONE + bt * K * NCH + (k * NCH + c))
                                    dve.tensor_tensor(
                                        wt.rearrange("p n x c q -> p (n x c) q")[:, 0:K, :]
                                        .rearrange("p x (m q) -> p x m q", q=W),
                                        xpart[:, 0, t, taps].unsqueeze(2).to_broadcast([P, K, BR, W]),
                                        gy[:, taps, c * BR:(c + 1) * BR].unsqueeze(3)
                                        .to_broadcast([P, K, BR, W]), ALU.mult).then_inc(s["g_w"], 1)
                        dve.wait_ge(s["g_xo"], ONE + b + 1)
                        add_to_tokens(dve, b, s["g_x1"])
                    dve.wait_ge(s["g_x1"], ONE + B)
                    dve.sem_inc(s["x1"], B)
                    with dve.Fori(0, B) as a:
                        for n in range(STEPS):
                            dve_attention(dve, a, n)
                dve.nop()

            @block.tensor
            def _(pe):
                pe.wait_ge(s_ones, 1)
                large = load_flag(pe)
                with pe.If(large < 1):
                    pe.wait_ge(s["img_ok"], ONE + 16)
                    for m in range(NP):
                        pe.wait_ge(s["z_sb"], below(ONE + m - 3))
                        mix_piece(pe, 0, m, 3 + m % 4, s["z_mm"])
                    turn_weights(pe, 0, 0)
                    turns(pe, lambda b, u: pe_turn(pe, b, u))
                with pe.Else():
                    with pe.Fori(0, B) as b:
                        pe.wait_ge(s["g_img"], ONE + b + 1)
                        pe.wait_ge(s["g_x1"], ONE + b)
                        for m in range(NP):
                            pe.wait_ge(s["g_zs"], ONE + b * NP + m)
                            mix_piece(pe, 0, m, 3, s["g_zm"])
                        pe.wait_ge(s["g_zs"], ONE + (b + 1) * NP)
                        pe.sem_inc(s_past, 1)
                        with pe.Fori(0, NT // 2) as j:
                            for h in range(2):
                                bt = b * NT + j * 2 + h
                                pe.wait_ge(s["g_conv"], ONE + bt)
                                for k in range(K):
                                    for c in range(NCH):
                                        pe.wait_ge(s["g_w"], ONE + bt * K * NCH + (k * NCH + c + 1))
                                        pe.wait_ge(s["g_ev"], ONE + bt * K * NCH + (k * NCH + c))
                                        for x in range(K):
                                            ins = pe.transpose(psum[:, 0, x * P:(x + 1) * P],
                                                               wt.rearrange("p n x c q -> p (n x c) q")[:, x, :],
                                                               ident)
                                        ins.then_inc(s["g_tp"], 1)
                                    pe.wait_ge(s["g_ev"], ONE + bt * K * NCH + (k + 1) * NCH)
                                    for x in range(K):
                                        for c in range(NCH):
                                            ins = pe.matmul(psum[0:C, 2, 0:P],
                                                            mix[:, 0, k, c, x * C:(x + 1) * C], gT[:, c, x, :],
                                                            start=(k == 0 and x == 0 and c == 0),
                                                            stop=(k == K - 1 and x == K - 1 and c == NCH - 1))
                                    ins.then_inc(s["g_mm"], 1)
                        pe.wait_ge(s["g_conv"], ONE + (b + 1) * NT)
                        back_to_tokens(pe, s["g_xo"])
                    pe.wait_ge(s["g_x1"], ONE + B)
                    with pe.Fori(0, B) as a:
                        for n in range(STEPS):
                            pe_attention(pe, a, n)
                pe.nop()


class Norm:

    def __init__(self, sb, sem, cst, tag, s_past):
        self.tmp = sb(tag + "_tmp", [P, 2, NT, C])
        self.small = sb(tag + "_small", [P, 3, NT])
        self.half = cst("half")
        self.s_past = s_past
        (self.s_sum, self.s_mean, self.s_xc, self.s_sq, self.s_var, self.s_eps,
         self.s_rstd) = (sem(f"{tag}_{n}") for n in ("sum", "mean", "xc", "sq", "var", "eps", "rstd"))

    def sums(self, dve, src, b):
        small = self.small
        dve.tensor_reduce(small[:, 0, :], src, AX.X, ALU.add).then_inc(self.s_sum, 1)
        dve.wait_ge(self.s_sum, b + 1)
        dve.tensor_scalar(small[:, 0, :], small[:, 0, :], -1.0 / C, None, ALU.mult).then_inc(self.s_mean, 1)

    def squares(self, dve, b):
        small = self.small
        dve.wait_ge(self.s_sq, b + 1)
        dve.tensor_reduce(small[:, 1, :], self.tmp[:, 1], AX.X, ALU.add).then_inc(self.s_var, 1)

    def gpsimd(self, pool, src, dst, b, done, free):
        xc, sq, small = self.tmp[:, 0], self.tmp[:, 1], self.small

        def spread(x):
            return x.unsqueeze(2).to_broadcast([P, NT, C])

        pool.wait_ge(self.s_mean, b + 1)
        pool.wait_ge(done, ONE + b)
        pool.tensor_tensor(xc, src, spread(small[:, 0, :]), ALU.add).then_inc(self.s_xc, 1)
        pool.wait_ge(self.s_xc, b + 1)
        pool.tensor_tensor(sq, xc, xc, ALU.mult).then_inc(self.s_sq, 1)
        pool.wait_ge(self.s_var, b + 1)
        pool.sem_inc(self.s_past, 1)
        pool.tensor_scalar(small[:, 2, :], small[:, 1, :], 1.0 / C, LN_EPS, ALU.mult, ALU.add).then_inc(self.s_eps, 1)
        pool.wait_ge(self.s_eps, b + 1)
        pool.tensor_tensor(small[:, 2, :], small[:, 2, :], self.half, ALU.pow).then_inc(self.s_rstd, 1)
        pool.wait_ge(self.s_rstd, b + 1)
        pool.wait_ge(free, ONE + b)
        pool.tensor_tensor(dst, xc, spread(small[:, 2, :]), ALU.mult).then_inc(done, 1)


def route(nc, dram, cst, psum, tok, gate, pm, pooled_t, w1, w2, b2, s_w, s_past):
    ident = cst("ident")
    with ExitStack() as ctx:
        def sb(name, shape, dt=F32):
            return ctx.enter_context(nc.sbuf_tensor(name, shape, dt))

        def sem(name):
            return ctx.enter_context(nc.semaphore(name))

        norm = Norm(sb, sem, cst, "rn", s_past)
        ln = sb("rln", [P, GI, NT, C])
        lnT = sb("rlnT", [C + 1, 2, T])
        nmx = sb("nmx", [P, 2])
        ex = sb("ex", [P, T])
        pr = sb("pr", [P, T])
        left = sb("left", [P, T])
        taken = sb("taken", [P, T])
        top = sb("top", [P, TOP])
        tsum = sb("tsum", [P, 2])
        takenT = sb("takenT", [P, NT, P])
        pool_sb = sb("pool_sb", [P, C])
        s = {n: sem("r_" + n) for n in "ones ln xt lnT lg mx ex rc pr top rep tk kept tt tT po po_sb pt pT".split()}
        start_at_one(nc, list(s.values()))
        logits = psum[:, 2:4, :].rearrange("p a q -> p (a q)")

        with nc.Block() as block:
            @block.sync
            def _(sync):
                sync.dma_start(w1[:, :, :], dram["w1"]).then_inc(s_w, 16)
                sync.dma_start(w2[:, :, :, :], dram["w2"]).then_inc(s_w, 16)
                sync.dma_start(b2[:, :], dram["b2"]).then_inc(s_w, 16)

            @block.gpsimd
            def _(pool):
                pool.memset(lnT[C:C + 1, :, :], 1.0).then_inc(s["ones"], 1)
                pool.wait_ge(s["ones"], ONE + 1)
                pool.memset(pooled_t[C:C + 1, :, :], 1.0).then_inc(s["ones"], 1)
                pool.wait_ge(s["ones"], ONE + 2)
                with pool.Fori(0, NG) as g:
                    pool.wait_ge(s["po"], ONE + g)
                    for u in range(GI):
                        norm.gpsimd(pool, tok[:, g * GI + u], ln[:, u], g * GI + u, s["ln"], s["xt"])
                    pool.wait_ge(s["tk"], ONE + g + 1)
                    pool.tensor_copy(pm[:, g, :], taken[:, :]).then_inc(s["kept"], 1)
                pool.wait_ge(s["kept"], ONE + NG)

            @block.vector
            def _(dve):
                with dve.Fori(0, NG) as g:
                    for u in range(GI):
                        b = g * GI + u
                        norm.sums(dve, tok[:, b], b)
                        norm.squares(dve, b)
                    dve.wait_ge(s["lg"], ONE + g * GI + GI)
                    dve.tensor_reduce(nmx[:, 0:1], logits, AX.X, ALU.max, negate=True).then_inc(s["mx"], 1)
                    dve.wait_ge(s["ex"], ONE + g + 1)
                    dve.reciprocal(tsum[:, 1:2], tsum[:, 0:1]).then_inc(s["rc"], 1)
                    dve.wait_ge(s["rc"], ONE + g + 1)
                    dve.tensor_scalar(pr[:, :], ex[:, :], tsum[:, 1:2], None, ALU.mult).then_inc(s["pr"], 1)
                    dve.wait_ge(s["pr"], ONE + g + 1)
                    dve.sem_inc(s_past, 1)
                    dve.max(top[:, :], pr[:, :]).then_inc(s["top"], 1)
                    dve.wait_ge(s["top"], ONE + g + 1)
                    dve.sem_inc(s_past, 1)
                    dve.match_replace(left[:, :], top[:, :], pr[:, :], -1.0).then_inc(s["rep"], 1)
                    dve.wait_ge(s["rep"], ONE + g + 1)
                    dve.wait_ge(s["kept"], ONE + g)
                    dve.scalar_tensor_tensor(taken[:, :], left[:, :], 0.0, pr[:, :], ALU.is_lt,
                                             ALU.mult).then_inc(s["tk"], 1)
                    dve.wait_ge(s["po"], ONE + g + 1)
                    dve.tensor_copy(pool_sb[:, :], psum[:, 6, 0:C]).then_inc(s["po_sb"], 1)
                dve.wait_ge(s["po_sb"], ONE + NG)

            @block.scalar
            def _(act):
                with act.Fori(0, NG) as g:
                    for u in range(GI):
                        b = g * GI + u
                        act.wait_ge(s["xt"], ONE + b + 1)
                        act.activation(lnT[0:C, u % 2, :], psum[0:C, 0:2, :].rearrange("c a q -> c (a q)"),
                                       ACT.Copy).then_inc(s["lnT"], 1)
                    act.wait_ge(s["mx"], ONE + g + 1)
                    act.activation(ex[:, :], logits, ACT.Exp, bias=nmx[:, 0:1],
                                   accum_out=tsum[:, 0:1]).then_inc(s["ex"], 1)
                    act.wait_ge(s["tt"], ONE + g + 1)
                    act.activation(takenT.rearrange("p a q -> p (a q)"),
                                   psum[:, 4:6, :].rearrange("p a q -> p (a q)"), ACT.Copy).then_inc(s["tT"], 1)
                    act.wait_ge(s["pt"], ONE + g + 1)
                    act.activation(pooled_t[0:C, bass.ds(g * GI, GI), :],
                                   psum[0:C, 7, 0:P].rearrange("c (u e) -> c u e", u=GI),
                                   ACT.Copy).then_inc(s["pT"], 1)
                act.wait_ge(s["pT"], ONE + NG)

            @block.tensor
            def _(pe):
                pe.wait_ge(s["ones"], ONE + 2)
                with pe.Fori(0, NG) as g:
                    pe.wait_ge(s["ex"], ONE + g)
                    for u in range(GI):
                        b = g * GI + u
                        pe.wait_ge(s["ln"], ONE + b + 1)
                        pe.wait_ge(s["lnT"], ONE + b)
                        pe.sem_inc(s_past, 1)
                        for t in range(NT):
                            ins = pe.transpose(psum[0:C, t // 4, (t % 4) * P:(t % 4 + 1) * P], ln[:, u, t, :], ident)
                        ins.then_inc(s["xt"], 1)
                        pe.wait_ge(s["lnT"], ONE + b + 1)
                        for h in range(2):
                            ins = pe.matmul(psum[E * u:E * u + E, 2 + h, :], gate[:, :],
                                            lnT[:, u % 2, h * HB:(h + 1) * HB], start=True, stop=True)
                        ins.then_inc(s["lg"], 1)
                    pe.wait_ge(s["tk"], ONE + g + 1)
                    for t in range(NT):
                        ins = pe.transpose(psum[:, 4 + t // 4, (t % 4) * P:(t % 4 + 1) * P],
                                           taken[:, t * P:(t + 1) * P], ident)
                    ins.then_inc(s["tt"], 1)
                    pe.wait_ge(s["tT"], ONE + g + 1)
                    pe.wait_ge(s["po_sb"], ONE + g)
                    for t in range(NT):
                        for u in range(GI):
                            ins = pe.matmul(psum[E * u:E * u + E, 6, 0:C], takenT[:, t, E * u:E * u + E],
                                            ln[:, u, t, :], start=(t == 0), stop=(t == NT - 1))
                    ins.then_inc(s["po"], 1)
                    pe.wait_ge(s["po_sb"], ONE + g + 1)
                    pe.wait_ge(s["pT"], ONE + g)
                    pe.sem_inc(s_past, 1)
                    pe.transpose(psum[0:C, 7, 0:P], pool_sb[:, :], ident).then_inc(s["pt"], 1)


def mlp(nc, cst, psum, w1, w2, b2, s_w, pooled_t, expert_out):
    ident = cst("ident")
    with ExitStack() as ctx:
        def sb(name, shape, dt=F32):
            return ctx.enter_context(nc.sbuf_tensor(name, shape, dt))

        def sem(name):
            return ctx.enter_context(nc.semaphore(name))

        hT = sb("hT", [P, E, 2, B])
        oT = sb("moT", [C, B, E])
        s = {n: sem("e_" + n) for n in "h gelu o oT t out".split()}
        with nc.Block() as block:
            @block.tensor
            def _(pe):
                pe.wait_ge(s_w, 16 * 3)
                for e in range(E):
                    for h in range(2):
                        ins = pe.matmul(psum[:, 0, (2 * e + h) * B:(2 * e + h + 1) * B],
                                        w1[:, e, h * P:(h + 1) * P], pooled_t[:, :, e], start=True, stop=True)
                ins.then_inc(s["h"], 1)
                pe.wait_ge(s["gelu"], 1)
                for e in range(E):
                    for h in range(2):
                        ins = pe.matmul(psum[0:C, 1, e * B:(e + 1) * B], w2[:, h, e, :], hT[:, e, h, :],
                                        start=(h == 0), stop=(h == 1))
                ins.then_inc(s["o"], 1)
                pe.wait_ge(s["oT"], 1)
                for g in range(NG):
                    ins = pe.transpose(psum[:, 2, g * C:(g + 1) * C],
                                       oT[:, g * GI:(g + 1) * GI, :].rearrange("c u e -> c (u e)"), ident[0:C, 0:C])
                ins.then_inc(s["t"], 1)

            @block.scalar
            def _(act):
                act.wait_ge(s["h"], 1)
                act.activation(hT.rearrange("p e h b -> p (e h b)"), psum[:, 0, :], ACT.Gelu).then_inc(s["gelu"], 1)
                act.wait_ge(s["t"], 1)
                act.activation(expert_out.rearrange("p g f -> p (g f)"), psum[:, 2, 0:NG * C],
                               ACT.Copy).then_inc(s["out"], 1)
                act.wait_ge(s["out"], 1)

            @block.vector
            def _(dve):
                dve.wait_ge(s["o"], 1)
                dve.tensor_tensor(oT.rearrange("c b e -> c e b"),
                                  psum[0:C, 1, 0:E * B].rearrange("c (e b) -> c e b", b=B),
                                  b2[:, :].unsqueeze(2).to_broadcast([C, E, B]), ALU.add).then_inc(s["oT"], 1)


def combine(nc, psum, tok, pm, expert_out, out_blk):
    with ExitStack() as ctx:
        def sb(name, shape, dt=F32):
            return ctx.enter_context(nc.sbuf_tensor(name, shape, dt))

        def sem(name):
            return ctx.enter_context(nc.semaphore(name))

        pm_now = sb("pm_now", [P, 2, T])
        out_now = sb("out_now", [P, 2, C])
        res = sb("res", [P, GI, NT, C])
        s = {n: sem("f_" + n) for n in "pm eo y x".split()}
        s_st = [sem(f"f_st{u}") for u in range(GI)]
        with nc.Block() as block:
            @block.gpsimd
            def _(pool):
                for g in range(NG):
                    pool.tensor_copy(out_now[:, g, :], expert_out[:, g, :]).then_inc(s["eo"], 1)
                    pool.tensor_copy(pm_now[:, g, :], pm[:, g, :]).then_inc(s["pm"], 1)

            @block.tensor
            def _(pe):
                for g in range(NG):
                    pe.wait_ge(s["eo"], g + 1)
                    pe.wait_ge(s["pm"], g + 1)
                    for u in range(GI):
                        pe.wait_ge(s["x"], max(0, g * GI + u - GI + 1))
                        rows = slice(E * u, E * u + E)
                        for t in range(NT):
                            ins = pe.matmul(psum[:, u, t * C:(t + 1) * C], pm_now[rows, g, t * P:(t + 1) * P],
                                            out_now[rows, g, :], start=True, stop=True)
                        ins.then_inc(s["y"], 1)

            @block.vector
            def _(dve):
                for g in range(NG):
                    for u in range(GI):
                        b = g * GI + u
                        dve.wait_ge(s["y"], b + 1)
                        if g:
                            dve.wait_ge(s_st[u], 16 * g)
                        dve.tensor_tensor(res[:, u], psum[:, u, :].rearrange("p (t f) -> p t f", f=C), tok[:, b],
                                          ALU.add).then_inc(s["x"], 1)

            @block.sync
            def _(sync):
                for g in range(NG):
                    for u in range(GI):
                        b = g * GI + u
                        sync.wait_ge(s["x"], b + 1)
                        sync.dma_start(out_blk[b], res[:, u]).then_inc(s_st[u], 16)
                for u in range(GI):
                    sync.wait_ge(s_st[u], 16 * NG)


def lay_out(inputs):
    f = {k: np.asarray(v) for k, v in inputs.items()}
    taps = f["L0_conv_kernel"].reshape(K * K, C, C)
    kp = np.zeros((P, K, K * C), np.float32)
    for k, half in ((0, 0), (1, C), (2, 0)):
        kp[half:half + C, k] = taps[K * k:K * k + K].transpose(1, 0, 2).reshape(C, K * C)
    ow = np.zeros((K, C, K, 32), np.float32)
    ow[..., :OCH] = f["L0_conv_offset_w"].transpose(0, 2, 1, 3)
    ob = np.zeros((4, 32), np.float32)
    ob[:, :OCH] = f["L0_conv_offset_b"]
    w2 = f["L1_ffn_weight2"]
    return {
        "x": f["x"],
        "const": constants()[0],
        "ow_pair": ow[0:2].reshape(P, K, 32),
        "ow_last": ow[2],
        "ob": ob.reshape(P, 1),
        "kp": kp,
        "kbias": np.tile(f["L0_conv_bias"], 2).reshape(P, 1),
        "wqk": np.concatenate([np.concatenate([f["L1_attn_Wq"], f["L1_attn_Wk"]], 1),
                               np.concatenate([f["L1_attn_bq"], f["L1_attn_bk"]])[None]], 0),
        "wv": np.concatenate([f["L1_attn_Wv"], f["L1_attn_bv"][None]], 0),
        "gate": np.concatenate([f["L1_ffn_gate_w"].T, f["L1_ffn_gate_b"][None]], 0),
        "w1": np.ascontiguousarray(f["L1_ffn_weight1"].transpose(1, 0, 2)),
        "w2": np.ascontiguousarray(w2[:, :HID].reshape(E, 2, P, C).transpose(2, 1, 0, 3)),
        "b2": np.ascontiguousarray(w2[:, HID].T),
    }


def kernel(**inputs):
    import concourse.bacc as bacc
    from concourse.bass_utils import run_bass_kernel_spmd

    nc = bacc.Bacc("TRN2", target_bir_lowering=False, num_devices=1)
    arrays = {f"in_{k}": np.ascontiguousarray(v) for k, v in lay_out(inputs).items()}
    dram = {k[3:]: nc.dram_tensor(k, a.shape, F32, kind="ExternalInput").ap() for k, a in arrays.items()}
    out = nc.dram_tensor("out", (B, H, W, C), F32, kind="ExternalOutput").ap()
    build(nc, dram, out)
    return run_bass_kernel_spmd(nc, [arrays], core_ids=[0]).results[0]["out"]
```

```python
from contextlib import ExitStack

import numpy as np

import concourse.bass as bass
from concourse import mybir

F32 = mybir.dt.float32
BF16 = mybir.dt.bfloat16
I32 = mybir.dt.int32
ALU = mybir.AluOpType
ACT = mybir.ActivationFunctionType
AX = mybir.AxisListType

B, H, W, C = 8, 32, 32, 64
T = H * W
P = 128
NT = T // P
BR = P // W
K = 3
NCH = NT + 1
HALO = 3
PR = 38
OCH = 2 * K * K
HB = 512
E, HID, TOP = 32, 256, 8
GI = P // E
NG = B // GI
LIMIT = 2.0
WIN = 2 * BR
GN_EPS, LN_EPS = 1e-5, 1e-5
NEG = -2.0 ** 43
ONE = 1


def constants():
    p = np.arange(P)
    r, w = p // W, p % W
    ident = np.eye(P)
    same = (p[:, None] // 2 == p[None, :] // 2) * 0.5
    diff = same * np.where(p[:, None] % 2 == 0, 1.0, -1.0)
    ybase = r[:, None] + 2 - np.arange(WIN)[None, :]
    xbase = (w[:, None, None] + (np.arange(K) - 1)[None, :, None] - np.arange(W)[None, None, :]).reshape(P, -1)
    mask = np.where(p[None, :] > p[:, None], NEG, 0.0)
    half = np.full((P, NT), -0.5)
    yall = ((r + 2)[:, None, None] + BR * np.arange(NT)[None, :, None] - np.arange(BR * NCH)[None, None, :]).reshape(P, -1)
    parts = dict(ident=ident, same=same, diff=diff, ybase=ybase, xbase=xbase, mask=mask, half=half, yall=yall)
    at, cols = {}, 0
    for n, a in parts.items():
        at[n] = (cols, cols + a.shape[1])
        cols += a.shape[1]
    return np.concatenate(list(parts.values()), 1).astype(np.float32), at


def each_image(eng):
    with eng.Fori(0, B // 2) as i:
        for u in range(2):
            yield u, i * 2 + u, i


def below(value):
    return max(value, 0) if isinstance(value, int) else value


def at_most(value, most):
    return min(value, most) if isinstance(value, int) else value


def start_at_one(nc, sems):
    with nc.Block() as block:
        @block.sync
        def _(sync):
            for x in sems[0::3]:
                sync.sem_inc(x, ONE)

        @block.gpsimd
        def _(pool):
            for x in sems[1::3]:
                pool.sem_inc(x, ONE)

        @block.vector
        def _(dve):
            for x in sems[2::3]:
                dve.sem_inc(x, ONE)


def build(nc, dram, out):
    table, at = constants()
    x_blk = dram["x"].rearrange("b (t r) w c -> b (r w) t c", r=BR)
    with ExitStack() as ctx:
        def sb(name, shape, dt=F32):
            return ctx.enter_context(nc.sbuf_tensor(name, shape, dt))

        def sem(name):
            return ctx.enter_context(nc.semaphore(name))

        const = sb("const", [P, table.shape[1]])

        def cst(name):
            return const[:, at[name][0]:at[name][1]]

        tok = sb("tok", [P, B, NT, C])
        wqk = sb("wqk", [C + 1, 2 * C])
        wv = sb("wv", [C + 1, C])
        gate = sb("gate", [C + 1, E])
        s_const, s_tok = sem("s_const"), sem("s_tok")
        s_past = sem("s_past")
        psum = ctx.enter_context(nc.psum_tensor("psum", [P, 8, HB], F32))
        pxn = sb("pxn", [P, B, PR, W])
        flat = pxn.rearrange("p b r w -> p (b r w)")
        pad = PR * W
        logits = [flat[:, g * pad:g * pad + T] for g in range(NG)]
        ln2 = flat[:, NG * pad:NG * pad + B * NT * C].rearrange("p (b t f) -> p b t f", b=B, t=NT)
        first = NG * pad + B * NT * C
        pm = flat[:, first:first + NG * T].rearrange("p (g t) -> p g t", g=NG)
        with ExitStack() as conv:
            def csb(name, shape, dt=F32):
                return conv.enter_context(nc.sbuf_tensor(name, shape, dt))

            img = csb("img", [P, 2, PR, W])
            off = csb("off", [P, B, NT, OCH])
            flag = csb("flag", [1, 1], I32)
            kp = csb("kp", [P, K, K * C])
            kbias = csb("kbias", [P, 1])
            prepare(nc, dram, cst, const, psum, tok, x_blk, off, pxn, img, flag, kp, kbias, wqk, wv, gate, s_const, s_tok, s_past)
            convolve_and_attend(nc, cst, psum, tok, off, pxn, img, flag, kp, kbias, wqk, wv, gate, ln2, logits, pm, s_tok,
                                s_past)
        w1 = sb("w1", [C + 1, E, HID])
        w2 = sb("w2", [P, 2, E, C])
        b2 = sb("b2", [P, E * E // P, C])
        pick = sb("pick", [P, NG, P + E - P // E])
        s_w = sem("s_w")
        lhs = sb("lhs", [C + 1, E, E])
        route(nc, dram, cst, psum, ln2, logits, pm, lhs, w1, w2, b2, pick, s_w, s_past)
        expert_out = sb("expert_out", [P, NG, GI, C])
        mlp(nc, cst, psum, w1, w2, b2, pick, s_w, lhs, expert_out)
        combine(nc, psum, tok, pm, expert_out, out)


def prepare(nc, dram, cst, const, psum, tok, x_blk, off, pxn, img, flag, kp, kbias, wqk, wv, gate, s_const, s_tok, s_past):
    ident = cst("ident")
    with ExitStack() as ctx:
        def sb(name, shape, dt=F32):
            return ctx.enter_context(nc.sbuf_tensor(name, shape, dt))

        def sem(name):
            return ctx.enter_context(nc.semaphore(name))

        xs = sb("xs", [P, 2, NT, 2, C])
        ow_pair = sb("ow_pair", [P, K, 32])
        ow_last = sb("ow_last", [C, K, 32])
        ob = sb("ob", [P, 1])
        offT = sb("offT", [P, 2, P])
        st = sb("st", [P, 2, 6])
        mv = sb("mv", [P, 2])
        gs = sb("gs", [P, 8])
        mx = sb("mx", [P, 1])
        mrow = sb("mrow", [1, 2])
        xT = [psum[:, 0:2, :], psum[:, 4:6, :]]
        offP = psum[:, 2, 0:256]
        offTok = psum[:, 6, 0:256]
        grp = psum[:, 3, 0:3]
        mxT = psum[0:1, 3, 128:256]
        s_ld = [sem(f"s_ld{u}") for u in range(2)]
        s_rest = sem("s_rest")
        names = "xs_free x_t img_kept pad0 st mv gavg gcp vv rs1 rstd nmr pn_lo pn_hi off_mm off_sb off_t off_tok m1 m2 m3 m4".split()
        s = {n: sem("p_" + n) for n in names}
        start_at_one(nc, [s[n] for n in names])

        with nc.Block() as block:
            @block.sync
            def _(sync):
                def load(u, image):
                    sync.dma_start(xs[:, u, :, 0, :], x_blk[image]).then_inc(s_ld[u], 16)
                    sync.dma_start(xs[:, u, :, 1, :], x_blk[image]).then_inc(s_ld[u], 16)

                def keep_image(b, u):
                    sync.wait_ge(s["pn_lo"], ONE + b + 1)
                    sync.wait_ge(s["pn_hi"], ONE + b + 1)
                    sync.wait_ge(s["img_kept"], ONE + 16 * b)
                    sync.dma_start(pxn[:, b + 2], img[:, u]).then_inc(s["img_kept"], 16)

                load(0, 2)
                load(1, 3)
                with sync.Fori(0, B // 2 - 2) as i:
                    for u in range(2):
                        b = i * 2 + 2 + u
                        sync.wait_ge(s["xs_free"], ONE + b - 1)
                        sync.wait_ge(s_ld[u], i * 32 + 32)
                        load(u, b + 2)
                        keep_image(i * 2 + u, u)
                for u in range(2):
                    b = B - 2 + u
                    sync.wait_ge(s["xs_free"], ONE + b - 1)
                    sync.wait_ge(s_ld[u], (B // 2 - 1) * 32)
                    load(u, u)
                    keep_image(b - 2, u)
                    for image in range(4 * u, 4 * u + 4):
                        sync.dma_start(tok[:, image, :, :], x_blk[image]).then_inc(s_tok, 16)
                sync.wait_ge(s["img_kept"], ONE + 16 * (B - 2))

            @block.gpsimd
            def _(pool):
                pool.memset(img[:, :, :, :], 0.0).then_inc(s["pad0"], 1)
                pool.wait_ge(s_const, 16)
                with pool.Fori(0, B) as b:
                    pool.wait_ge(s["vv"], ONE + b + 1)
                    pool.sem_inc(s_past, 1)
                    pool.tensor_scalar(gs[:, 3:4], gs[:, 3:4], GN_EPS, None, ALU.add).then_inc(s["rs1"], 1)
                    pool.wait_ge(s["rs1"], ONE + b + 1)
                    pool.tensor_tensor(gs[:, 4:5], gs[:, 3:4], cst("half")[:, 0:1], ALU.pow).then_inc(s["rstd"], 1)

            @block.tensor
            def _(pe):
                def to_channels(b, u, i):
                    pe.wait_ge(s_ld[u], i * 32 + 32)
                    pe.wait_ge(s["pn_lo"], below(ONE + b - 1))
                    pe.wait_ge(s["pn_hi"], below(ONE + b - 1))
                    pe.sem_inc(s_past, 1)
                    for t in range(NT):
                        ins = pe.transpose(xT[u][:, t // 4, (t % 4) * P:(t % 4 + 1) * P],
                                           xs[:, u, t, :, :].rearrange("p a c -> p (a c)"), ident)
                    ins.then_inc(s["x_t"], 1)

                def group_sums(b):
                    pe.wait_ge(s["mv"], ONE + b + 1)
                    pe.matmul(grp[:, 0:2], cst("same"), mv[:, :], start=True, stop=True).then_inc(s["xs_free"], 1)
                    pe.matmul(grp[:, 2:3], cst("diff"), mv[:, 0:1], start=True, stop=True).then_inc(s["gavg"], 1)

                def offsets(b, u):
                    pe.wait_ge(s["pn_lo"], ONE + b + 1)
                    pe.wait_ge(s["pn_hi"], ONE + b + 1)
                    pe.wait_ge(s["off_sb"], ONE + b)
                    for n, kx in enumerate((1, 0, 2)):
                        a, z = max(0, 1 - kx), min(W, W + 1 - kx)
                        for j in range(4):
                            pe.matmul(offP[32 * j:32 * j + 32, :].rearrange("m (h w) -> m h w", w=W)[:, :, a:z],
                                      ow_pair[:, kx, :],
                                      img[:, u, 8 * j + 2:8 * j + 10, a + kx - 1:z + kx - 1],
                                      start=(n == 0), stop=False)
                    for n, kx in enumerate((0, 2, 1)):
                        a, z = max(0, 1 - kx), min(W, W + 1 - kx)
                        for j in range(4):
                            ins = pe.matmul(offP[32 * j:32 * j + 32, :].rearrange("m (h w) -> m h w", w=W)[:, :, a:z],
                                            ow_last[:, kx, :],
                                            img[0:C, u, 8 * j + 4:8 * j + 12, a + kx - 1:z + kx - 1],
                                            start=False, stop=(n == K - 1))
                    ins.then_inc(s["off_mm"], 1)

                def offsets_to_tokens(b):
                    pe.wait_ge(s["off_sb"], ONE + b + 1)
                    pe.wait_ge(s["off_tok"], ONE + b)
                    for h in range(2):
                        ins = pe.transpose(offTok[:, h * P:(h + 1) * P], offT[:, h, :], ident)
                    ins.then_inc(s["off_t"], 1)

                pe.wait_ge(s_const, 16)
                to_channels(0, 0, 0)
                group_sums(0)
                to_channels(1, 1, 0)
                pe.wait_ge(s_rest, 16 * 8)
                with pe.Fori(0, B // 2 - 1) as i:
                    for u in range(2):
                        b = i * 2 + 1 + u
                        group_sums(b)
                        to_channels(b + 1, u, i + 1)
                        offsets(i * 2 + u, u)
                        offsets_to_tokens(i * 2 + u)
                group_sums(B - 1)
                for b in (B - 2, B - 1):
                    offsets(b, b % 2)
                    offsets_to_tokens(b)
                pe.wait_ge(s["m1"], ONE + 1)
                pe.transpose(mxT, mx[:, :], ident).then_inc(s["m2"], 1)

            @block.scalar
            def _(act):
                def normalise(b, u):
                    act.wait_ge(s["nmr"], ONE + b + 1)
                    act.wait_ge(s["off_mm"], below(ONE + b - 1))
                    act.wait_ge(s["img_kept"], below(ONE + 16 * (b - 1)))
                    act.activation(img[0:C, u, HALO:HALO + H, :],
                                   xT[u][0:C, :, :].rearrange("c a (h w) -> c (a h) w", w=W), ACT.Identity,
                                   bias=gs[0:C, 5:6], scale=gs[0:C, 4:5]).then_inc(s["pn_lo"], 1)

                def leave(b):
                    act.wait_ge(s["off_mm"], ONE + b + 1)
                    act.wait_ge(s["off_t"], ONE + b)
                    act.activation(offT[:, :, :], offP.rearrange("p (h q) -> p h q", h=2), ACT.Identity,
                                   bias=ob[:, 0:1]).then_inc(s["off_sb"], 1)

                act.dma_start(const[:, :], dram["const"]).then_inc(s_const, 16)
                for dst, name in ((ow_pair[:, :, :], "ow_pair"), (ow_last[:, :, :], "ow_last"), (ob[:, :], "ob"),
                                  (kp[:, :, :], "kp"), (kbias[:, :], "kbias"), (wqk[:, :], "wqk"),
                                  (wv[:, :], "wv"), (gate[:, :], "gate")):
                    act.dma_start(dst, dram[name]).then_inc(s_rest, 16)
                act.wait_ge(s_rest, 16 * 8)
                act.wait_ge(s["pad0"], ONE + 1)
                normalise(0, 0)
                with act.Fori(0, B // 2 - 1) as i:
                    normalise(i * 2 + 1, 1)
                    leave(i * 2)
                    normalise(i * 2 + 2, 0)
                    leave(i * 2 + 1)
                normalise(B - 1, 1)
                leave(B - 2)
                leave(B - 1)

            @block.vector
            def _(dve):
                def statistics(b, u):
                    dve.wait_ge(s["x_t"], ONE + b + 1)
                    dve.bn_stats(st[:, 0, :], xT[u][:, 0, :]).then_inc(s["st"], 1)
                    dve.bn_stats(st[:, 1, :], xT[u][:, 1, :]).then_inc(s["st"], 1)
                    dve.wait_ge(s["st"], ONE + b * 2 + 2)
                    dve.wait_ge(s["gavg"], ONE + b)
                    dve.sem_inc(s_past, 1)
                    dve.bn_aggr(mv[:, :], st[:, :, :]).then_inc(s["mv"], 1)

                def normalise(b, u):
                    dve.wait_ge(s["gavg"], ONE + b + 1)
                    dve.wait_ge(s["pn_lo"], ONE + b)
                    dve.wait_ge(s["pn_hi"], ONE + b)
                    dve.tensor_copy(gs[:, 0:3], grp).then_inc(s["gcp"], 1)
                    dve.wait_ge(s["gcp"], ONE + b + 1)
                    dve.scalar_tensor_tensor(gs[:, 3:4], gs[:, 2:3], gs[:, 2:3], gs[:, 1:2],
                                             ALU.mult, ALU.add).then_inc(s["vv"], 1)
                    dve.wait_ge(s["rstd"], ONE + b + 1)
                    dve.scalar_tensor_tensor(gs[:, 5:6], gs[:, 0:1], -1.0, gs[:, 4:5],
                                             ALU.mult, ALU.mult).then_inc(s["nmr"], 1)
                    dve.wait_ge(s["nmr"], ONE + b + 1)
                    dve.wait_ge(s["off_mm"], below(ONE + b - 1))
                    dve.wait_ge(s["img_kept"], below(ONE + 16 * (b - 1)))
                    dve.tensor_scalar(img[C:P, u, HALO - 1:HALO - 1 + H, :],
                                      xT[u][C:P, :, :].rearrange("c a (h w) -> c (a h) w", w=W),
                                      gs[C:P, 4:5], gs[C:P, 5:6], ALU.mult, ALU.add).then_inc(s["pn_hi"], 1)

                def keep_offsets(b):
                    dve.wait_ge(s["off_t"], ONE + b + 1)
                    image = (b + 2) % B if isinstance(b, int) else b + 2
                    dve.tensor_copy(off[:, image, :, :].rearrange("p (j h) o -> p j h o", h=2),
                                    offTok.rearrange("p (h j o) -> p j h o", h=2, j=4)[:, :, :, 0:OCH]
                                    ).then_inc(s["off_tok"], 1)

                dve.wait_ge(s["pad0"], ONE + 1)
                statistics(0, 0)
                normalise(0, 0)
                statistics(1, 1)
                with dve.Fori(0, B // 2 - 1) as i:
                    normalise(i * 2 + 1, 1)
                    statistics(i * 2 + 2, 0)
                    keep_offsets(i * 2)
                    normalise(i * 2 + 2, 0)
                    statistics(i * 2 + 3, 1)
                    keep_offsets(i * 2 + 1)
                normalise(B - 1, 1)
                keep_offsets(B - 2)
                keep_offsets(B - 1)
                dve.wait_ge(s["off_tok"], ONE + B)
                dve.tensor_reduce(mx[:, :], off.rearrange("p b t (k d) -> p (b t k) d", d=2)[:, :, 0], AX.X, ALU.max,
                                  apply_absolute_value=True).then_inc(s["m1"], 1)
                dve.wait_ge(s["m2"], ONE + 1)
                dve.tensor_reduce(mrow[:, 0:1], mxT, AX.X, ALU.max).then_inc(s["m3"], 1)
                dve.wait_ge(s["m3"], ONE + 1)
                dve.tensor_scalar(flag[:, :], mrow[:, 0:1], LIMIT, None, ALU.is_ge).then_inc(s["m4"], 1)
                dve.wait_ge(s["m4"], ONE + 1)


def convolve_and_attend(nc, cst, psum, tok, off, pxn, img, flag, kp, kbias, wqk, wv, gate, ln2, logits, pm, s_tok, s_past):
    ident, mask = cst("ident"), cst("mask")
    NU = NT // 2 * K * K
    XN = NT * K * K * W
    YN = NT * K * K * WIN
    NW = 4
    LEAD = 2
    DEEP = 4
    with ExitStack() as ctx:
        def sb(name, shape, dt=F32):
            return ctx.enter_context(nc.sbuf_tensor(name, shape, dt))

        def sem(name):
            return ctx.enter_context(nc.semaphore(name))

        mix = sb("mix", [P, 2, K, NCH, K * C])
        tent = sb("tent", [P, 2, XN + YN])
        wt = sb("wt", [P, NW, 2, 2, P])
        wtT = sb("wtT", [P, NW, 2, 2, P])
        conv_sb = sb("conv_sb", [P, HB])
        exact = sb("exact", [P, 2, P], BF16)
        norm_tmp = sb("norm_tmp", [P, 2, NT, C])
        norm = Norm(sb, sem, cst, "an", norm_tmp, s_past)
        norm2 = Norm(sb, sem, cst, "rn", norm_tmp, s_past)
        ln = sb("ln", [P, NT, C])
        channels = sb("channels", [P, T])
        lnT = channels[0:C + 1, :]
        now = slice(P - E, P)
        qT = sb("qT", [C, T])
        kT = sb("kT", [C, T])
        v = sb("v", [P, NT, C])
        negmax = sb("negmax", [P, NT])
        rsum = sb("rsum", [P, 2, NT])
        prob = sb("prob", [P, 2, T])
        pT = sb("pT", [P, DEEP, T])
        oT = sb("oT", [P, HB])
        att = sb("att", [P, NT, C])
        gT = pT.rearrange("p d t -> p (d t)")[:, 0:NCH * K * P].rearrange("p (c x q) -> p c x q", c=NCH, x=K)
        gy = att.rearrange("p t c -> p (t c)")[:, 0:K * K * BR * NCH].rearrange("p (a m) -> p a m", a=K * K)
        names = ("img_ok dist a1 tent_ok z_mm z_sb w_ok tp wT mm conv_ok xo_t x1 "
                 "ln xt lnT qk v_mm q_sb k_sb v_sb sc mx ex pt pe pv oT ot rs at x2 ln2 kept xt2 lnT2 lg lg_sb lg_ok "
                 "g_img g_zm g_zs g_d g_a g_tent g_yd g_ya g_y g_w g_tp g_ev g_mm g_conv g_xo g_x1").split()
        s = {n: sem("c_" + n) for n in names}
        start_at_one(nc, [s[n] for n in names])
        s_ones, s_exact = sem("c_ones"), sem("c_exact")
        spare = mix.rearrange("p u k c f -> p (u k c f)")
        choice = Choice(sb, sem, "r0", logits[0], pm[:, 0, :], [spare[:, n * T:(n + 1) * T] for n in range(3)])
        xpart = tent[:, :, 0:XN].rearrange("p u (t a q) -> p u t a q", t=NT, a=K * K)
        ypart = tent[:, :, XN:XN + YN].rearrange("p u (t a m) -> p u t a m", t=NT, a=K * K)
        xbase = cst("xbase").rearrange("p (x q) -> p x q", x=K)
        scale = 1.0 / float(np.sqrt(C))
        pieces = [(slice(0, 2), slice(c, c + 1)) for c in range(NCH)]
        pieces += [(slice(2, 3), slice(c, min(c + 2, NCH))) for c in range(0, NCH, 2)]
        NP = len(pieces)

        def alone(a):
            return isinstance(a, int) and a == B - 1

        def score_bank(t, a):
            return 0 if alone(a) and t % 2 else 4

        def wide(t, a):
            return psum[:, score_bank(t, a):score_bank(t, a) + 2, :].rearrange("p a q -> p (a q)")

        def prob_bank(n, a):
            return 3 if alone(a) and n % 2 else 6

        chunks = [(t, j, min(4, t + 1 - j)) for t in range(NT) for j in range(0, t + 1, 4)]
        NCK = len(chunks)
        of_block = [[n for n, c in enumerate(chunks) if c[0] == t] for t in range(NT)]
        AT_BACK, AT_PIECES = 1, 4
        AT_SUM, AT_SQUARES, AT_LN, AT_QKV = 2, 5, 7, 10
        AT_SCORES = [12, 14, 17, 25, 28, 31, 35, 39]
        AT_PROBS = AT_SCORES[1:] + [AT_SCORES[-1] + 3]
        AT_VALUES = [AT_PROBS[t + 1] + 3 + t // 4 for t in range(0, NT, 2)]
        AT_OUT = AT_VALUES[-1] + 1
        AT_SUM2, AT_SQUARES2 = AT_OUT + 3, AT_OUT + 5
        AT_LN2, LOGITS_AFTER = NU + AT_SCORES[2] + 3, 2
        STEPS = AT_LN2 + LOGITS_AFTER + 3
        AFTER_LOGITS, LAST_AFTER_LOGITS = 3, 6
        AT_LN2_LATE = NU + AT_SCORES[4] + 2
        AT_CHOICE = [3, 5, 7, 9, 16]
        AT_TENTS = [15, 18, 20, 22, 23]

        def at_ln2(a):
            return AT_LN2_LATE if isinstance(a, int) and a == B - 2 else AT_LN2

        assert AT_PROBS[-1] + 2 - NU < AT_QKV and AT_OUT - NU < AT_SCORES[0] and STEPS - NU <= AT_SCORES[3]

        def distances(pool, u, b, sem_d):
            dx = off[:, b, :, :].rearrange("p t (k x d) -> p (t k) x d", k=K, d=2)[:, :, :, 1]
            pool.tensor_tensor(tent[:, u, 0:XN].rearrange("p (a x q) -> p a x q", x=K, q=W),
                               dx.unsqueeze(3).to_broadcast([P, NT * K, K, W]),
                               xbase.unsqueeze(1).to_broadcast([P, NT * K, K, W]), ALU.add).then_inc(sem_d, 1)
            dy = off[:, b, :, :].rearrange("p t (a d) -> p (t a) d", d=2)[:, :, 0]
            pool.tensor_tensor(tent[:, u, XN:XN + YN].rearrange("p (a m) -> p a m", m=WIN),
                               dy.unsqueeze(2).to_broadcast([P, NT * K * K, WIN]),
                               cst("ybase").unsqueeze(1).to_broadcast([P, NT * K * K, WIN]),
                               ALU.add).then_inc(sem_d, 1)

        def mix_piece(pe, u, m, bank, done):
            ks, cs = pieces[m]
            for n, c in enumerate(range(cs.start, cs.stop)):
                width = (ks.stop - ks.start) * K * C
                rhs = kp[:, 0:2, :] if ks.start == 0 else kp[:, 2, :]
                first = BR * c + ks.start
                ins = pe.matmul(psum[:, bank, n * width:(n + 1) * width],
                                img[:, u, first:first + BR, :].rearrange("c r w -> c (r w)"), rhs,
                                start=True, stop=True)
            ins.then_inc(done, 1)

        def keep_piece(act, u, m, bank, done):
            ks, cs = pieces[m]
            shape = dict(k=ks.stop - ks.start, c=cs.stop - cs.start)
            n = shape["k"] * shape["c"] * K * C
            act.activation(mix[:, u, ks, cs, :], psum[:, bank, 0:n].rearrange("p (k c f) -> p k c f", **shape),
                           ACT.Copy).then_inc(done, 1)

        def back_to_tokens(pe, done):
            for q in range(4):
                ins = pe.transpose(psum[:, 3, q * P:(q + 1) * P], conv_sb[:, q * P:(q + 1) * P], ident)
            ins.then_inc(done, 1)

        def add_to_tokens(dve, b, done):
            x1 = tok[:, b, :, :].rearrange("p t f -> p (t f)")
            dve.tensor_tensor(x1, psum[:, 3, :], x1, ALU.add).then_inc(done, 1)

        def load_flag(eng):
            return eng.value_load(flag[0:1, 0:1], min_val=0, max_val=1)

        def alive(b):
            return not isinstance(b, int) or 0 <= b < B

        def turns(eng, step):
            for b in range(2):
                step(b, b)
            with eng.Fori(0, B // 2 - 2) as j:
                for u in range(2):
                    step(j * 2 + 2 + u, u)
            for b in range(B - 2, B + 2):
                step(b, b % 2)

        def attention_steps(eng, attention, b, n):
            if alive(b - 2):
                attention(eng, b - 2, NU + n)
            if alive(b - 1):
                attention(eng, b - 1, n)

        def query_block(n):
            return AT_SCORES.index(n) if n in AT_SCORES else None

        def prob_chunk(n):
            for c in range(2):
                if n - 2 * c in AT_PROBS:
                    t = AT_PROBS.index(n - 2 * c)
                    if c < len(of_block[t]):
                        return of_block[t][c]
            return None

        def piece_at(n):
            m, r = divmod(n - AT_PIECES, 2)
            return m if r == 0 and 0 <= m < NP else None

        def keep_logits(sync, a):
            g, r = divmod(a, GI)
            sync.wait_ge(s["lg_sb"], ONE + a + 1)
            sync.dma_start(logits[g][E * r:E * r + E, :], channels[now, :]).then_inc(s["lg_ok"], 16)

        def pool_distances(pool, u, b):
            pool.wait_ge(s["w_ok"], below(ONE + (b - 1) * NU))
            distances(pool, u, b, s["dist"])

        def pool_norm(pool, a, uses):
            pool.wait_ge(s["kept"], uses)
            norm.gpsimd(pool, tok[:, a], ln[:, :, :], a, s["ln"], s["xt2"], uses)

        def pool_norm2(pool, a, uses):
            pool.wait_ge(s["ln"], uses)
            norm2.gpsimd(pool, tok[:, a], ln[:, :, :], a, s["ln2"], s["xt"], uses)
            pool.wait_ge(s["ln2"], ONE + a + 1)
            pool.sem_inc(s_past, 1)
            pool.tensor_copy(ln2[:, a], ln[:, :, :]).then_inc(s["kept"], 1)

        def pool_turn(pool, b, u):
            if alive(b - 1):
                pool_norm(pool, b - 1, below(ONE + b - 2))
            if alive(b + 1) and alive(b):
                pool_distances(pool, 1 - u, b + 1)
            if alive(b - 2):
                pool.wait_ge(s["img_ok"], ONE + 16 * at_most(b + 1, B))
                pool_norm2(pool, b - 2, ONE + at_most(b, B))

        def act_tents(act, u, b, j):
            if j < NT // 2:
                act.wait_ge(s["dist"], ONE + (b + 1) * 2)
                for part in (xpart, ypart):
                    now = part[:, u, 2 * j:2 * j + 2]
                    ins = act.activation(now, now, ACT.Abs)
                ins.then_inc(s["a1"], 1)
            if j > 0:
                act.wait_ge(s["a1"], ONE + b * (NT // 2) + j)
                for part in (xpart, ypart):
                    now = part[:, u, 2 * j - 2:2 * j]
                    ins = act.activation(now, now, ACT.Relu, bias=1.0, scale=-1.0)
                ins.then_inc(s["tent_ok"], 1)

        def act_leave(act, a, n):
            t, j, nb = chunks[n]
            if j == 0 and t % 2 == 0:
                act.wait_ge(s["pv"], ONE + a * (NT // 2) + max(0, (t - DEEP) // 2 + 1))
            act.wait_ge(s["pt"], ONE + a * NCK + n + 1)
            act.activation(pT[:, t % DEEP, j * P:(j + nb) * P], psum[:, prob_bank(n, a), 0:nb * P],
                           ACT.Copy).then_inc(s["pe"], 1)

        def keep_channels(act, done):
            blocks = lnT[0:C, :].rearrange("c (q h p) -> c q h p", h=2, p=P)
            for h in range(2):
                ins = act.activation(blocks[:, :, h, :], psum[C * h:C * h + C, 4, :].rearrange("c (q p) -> c q p", p=P),
                                     ACT.Copy)
            ins.then_inc(done, 1)

        def act_attention(act, a, n):
            if n == AT_LN + 1:
                act.wait_ge(s["xt"], ONE + a + 1)
                act.wait_ge(s["v_mm"], ONE + a)
                keep_channels(act, s["lnT"])
            if n == AT_QKV + 1:
                act.wait_ge(s["qk"], ONE + a + 1)
                act.activation(qT[:, :], wide(0, a)[0:C, :], ACT.Copy, scale=scale).then_inc(s["q_sb"], 1)
                act.wait_ge(s["v_mm"], ONE + a + 1)
                act.wait_ge(s["pv"], ONE + a * (NT // 2))
                act.activation(v.rearrange("p t f -> p (t f)"), psum[:, 6, :], ACT.Copy).then_inc(s["v_sb"], 1)
            if prob_chunk(n - 1) is not None:
                act_leave(act, a, prob_chunk(n - 1))
            t = query_block(n - 2)
            if t is not None:
                act.wait_ge(s["mx"], ONE + a * NT + t + 1)
                if t == 0:
                    act.wait_ge(s["rs"], ONE + a)
                act.activation(prob[:, t % 2, 0:(t + 1) * P], wide(t, a)[:, 0:(t + 1) * P], ACT.Exp,
                               bias=negmax[:, t:t + 1], accum_out=rsum[:, 0, t:t + 1]).then_inc(s["ex"], 1)

            if n == at_ln2(a) + 1:
                act.wait_ge(s["xt2"], ONE + a + 1)
                keep_channels(act, s["lnT2"])
            if n == at_ln2(a) + LOGITS_AFTER + 2:
                act.wait_ge(s["lg"], ONE + a + 1)
                act.wait_ge(s["lg_ok"], ONE + 16 * a)
                act.activation(channels[now, :], wide(0, a)[now, :], ACT.Copy).then_inc(s["lg_sb"], 1)
            if n == AT_OUT - 1:
                act.wait_ge(s["pv"], ONE + (a + 1) * (NT // 2))
                act.wait_ge(s["ot"], ONE + a)
                act.activation(oT[:, :], psum[:, 7, :], ACT.Copy).then_inc(s["oT"], 1)

        def turned_weights(act, b, n):
            if n >= NU:
                b, n = b + 1, n - NU
            if not alive(b):
                return
            act.wait_ge(s["tp"], ONE + b * NU + (n + 1))
            act.wait_ge(s["mm"], below(ONE + b * NU + (n + 1 - NW)))
            act.activation(wtT[:, n % NW].rearrange("p x c q -> p (x c q)"),
                           psum[:, n % 2, :], ACT.Copy).then_inc(s["wT"], 1)

        def act_turn(act, b, u):
            for n in range(NU):
                if n == 0 and alive(b - 1):
                    act.wait_ge(s["mm"], ONE + b * NU)
                    act.wait_ge(s["xo_t"], below(ONE + b - 1))
                    act.activation(conv_sb[:, :], psum[:, 2, :], ACT.Identity,
                                   bias=kbias[:, 0:1]).then_inc(s["conv_ok"], 1)
                if alive(b):
                    turned_weights(act, b, n + 1)
                if alive(b) and alive(b + 1):
                    if piece_at(n - 1) is not None:
                        act.wait_ge(s["z_mm"], ONE + (b + 1) * NP + piece_at(n - 1) + 1)
                        keep_piece(act, 1 - u, piece_at(n - 1), 3, s["z_sb"])
                    if n in AT_TENTS:
                        act_tents(act, 1 - u, b + 1, AT_TENTS.index(n))
                attention_steps(act, act_attention, b, n)
                if isinstance(b, int) and b == B and n == AT_CHOICE[0] + 1:
                    choice.exponentials(act)

        def dve_attention(dve, a, n):
            if n == AT_SUM:
                dve.wait_ge(s["x1"], ONE + a + 1)
                dve.sem_inc(s_past, 1)
                norm.sums(dve, tok[:, a], a)
            if n == AT_SQUARES:
                norm.squares(dve, a)
            if n == AT_SUM2:
                dve.wait_ge(s["x2"], ONE + a + 1)
                dve.sem_inc(s_past, 1)
                norm2.sums(dve, tok[:, a], a)
            if n == AT_SQUARES2:
                norm2.squares(dve, a)
            if n == AT_QKV + 2:
                dve.wait_ge(s["qk"], ONE + a + 1)
                dve.tensor_copy(kT[:, :], psum[C:P, 4:6, :].rearrange("c a q -> c (a q)")).then_inc(s["k_sb"], 1)
            t = query_block(n - 1)
            if t is not None:
                dve.wait_ge(s["sc"], ONE + a * NT + t + 1)
                dve.tensor_reduce(negmax[:, t:t + 1], wide(t, a)[:, 0:(t + 1) * P], AX.X, ALU.max,
                                  negate=True).then_inc(s["mx"], 1)

            if n == AT_OUT:
                dve.wait_ge(s["ex"], ONE + (a + 1) * NT)
                dve.reciprocal(rsum[:, 1, :], rsum[:, 0, :]).then_inc(s["rs"], 1)
            if n == AT_OUT + 2:
                dve.wait_ge(s["ot"], ONE + a + 1)
                dve.wait_ge(s["rs"], ONE + a + 1)
                dve.tensor_tensor(att[:, :, :], psum[:, 7, :].rearrange("p (t f) -> p t f", f=C),
                                  rsum[:, 1, :].unsqueeze(2).to_broadcast([P, NT, C]), ALU.mult).then_inc(s["at"], 1)
                dve.wait_ge(s["at"], ONE + a + 1)
                dve.tensor_tensor(tok[:, a], tok[:, a], att[:, :, :], ALU.add).then_inc(s["x2"], 1)

        def dve_choice(dve, step):
            if step == 0:
                dve.wait_ge(s["lg_ok"], ONE + 16 * GI)
                choice.largest(dve)
            if step == 1:
                choice.probabilities(dve)
            if step == 2:
                choice.top_values(dve)
            if step == 3:
                choice.mark(dve)
            if step == 4:
                choice.keep(dve)

        def weights(dve, b, u, n):
            if n >= NU:
                b, u, n = b + 1, 1 - u, n - NU
            if not alive(b):
                return
            j, tap = divmod(n, K * K)
            if tap == 0:
                dve.wait_ge(s["tent_ok"], ONE + b * (NT // 2) + (j + 1))
            dve.wait_ge(s["tp"], below(ONE + b * NU + (n + 1 - NW)))
            pair = slice(2 * j, 2 * j + 2)
            dve.tensor_tensor(wt[:, n % NW].rearrange("p h c (m q) -> p h (c m) q", q=W),
                              xpart[:, u, pair, tap].unsqueeze(2).to_broadcast([P, 2, WIN, W]),
                              ypart[:, u, pair, tap].unsqueeze(3).to_broadcast([P, 2, WIN, W]),
                              ALU.mult).then_inc(s["w_ok"], 1)

        def dve_turn(dve, b, u):
            for n in range(NU):
                if alive(b):
                    weights(dve, b, u, n + LEAD)
                if n == AT_BACK + 1 and alive(b - 1):
                    dve.wait_ge(s["xo_t"], ONE + b)
                    add_to_tokens(dve, b - 1, s["x1"])
                attention_steps(dve, dve_attention, b, n)
                if isinstance(b, int) and b == B and n in AT_CHOICE:
                    dve_choice(dve, AT_CHOICE.index(n))

        def pe_score(pe, a, t):
            pe.wait_ge(s["ex"], ONE + a * NT + (max(t - 1, 0) if alone(a) else t))
            if t == (LAST_AFTER_LOGITS if alone(a) else AFTER_LOGITS):
                pe.wait_ge(s["lg_sb"], ONE + a)
            if t == 0:
                pe.wait_ge(s["q_sb"], ONE + a + 1)
                pe.wait_ge(s["k_sb"], ONE + a + 1)
            for h in range(t // 4 + 1):
                n = min(HB, (t + 1) * P - h * HB)
                pe.matmul(psum[:, score_bank(t, a) + h, 0:n], qT[:, t * P:(t + 1) * P], kT[:, h * HB:h * HB + n],
                          start=True, stop=(h < t // 4))
            pe.matmul(wide(t, a)[:, t * P:(t + 1) * P], exact[:, 0, :], exact[:, 1, :], start=False, stop=True).then_inc(s["sc"], 1)

        def pe_turn_prob(pe, a, n):
            t, j, nb = chunks[n]
            pe.wait_ge(s["ex"], ONE + a * NT + t + 1)
            if n == 0:
                pe.wait_ge(s["v_sb"], ONE + a + 1)
            pe.wait_ge(s["pe"], ONE + a * NCK + (max(n - 1, 0) if alone(a) else n))
            for m in range(nb):
                ins = pe.transpose(psum[:, prob_bank(n, a), m * P:(m + 1) * P],
                                   prob[:, t % 2, (j + m) * P:(j + m + 1) * P], ident)
            ins.then_inc(s["pt"], 1)

        def pe_values(pe, a, t):
            pe.wait_ge(s["pe"], ONE + a * NCK + of_block[t + 1][-1] + 1)
            if t == 0:
                pe.wait_ge(s["at"], ONE + a)
            for j in range(t + 2):
                for h in range(2):
                    if j <= t + h:
                        ins = pe.matmul(psum[C * h:C * h + C, 7, t // 2 * P:(t // 2 + 1) * P], v[:, j, :],
                                        pT[:, (t + h) % DEEP, j * P:(j + 1) * P],
                                        start=(j == 0), stop=(j == t + h))
            ins.then_inc(s["pv"], 1)

        def blocks_before_logits(a):
            if alone(a):
                return 0
            return LAST_AFTER_LOGITS - 1 if at_ln2(a) == AT_LN2_LATE else AFTER_LOGITS

        def to_channels(pe, done):
            for q in range(NT // 2):
                ins = pe.transpose(psum[:, 4, q * P:(q + 1) * P],
                                   ln[:, 2 * q:2 * q + 2, :].rearrange("p t c -> p (t c)"), ident)
            ins.then_inc(done, 1)

        def pe_attention(pe, a, n, beside=True):
            if n == AT_LN:
                pe.wait_ge(s["ln"], ONE + a + 1)
                pe.wait_ge(s["ex"], ONE + a * NT)
                pe.wait_ge(s["lg_sb"], below(ONE + a - 1) if beside else ONE + a)
                pe.sem_inc(s_past, 1)
                to_channels(pe, s["xt"])
            if n == AT_QKV:
                pe.wait_ge(s["lnT"], ONE + a + 1)
                for h in range(2):
                    ins = pe.matmul(psum[:, 4 + h, :], wqk[:, :], lnT[:, h * HB:(h + 1) * HB],
                                    start=True, stop=True)
                ins.then_inc(s["qk"], 1)
                pe.wait_ge(s["pe"], ONE + a * NCK)
                for t in range(NT):
                    ins = pe.matmul(psum[:, 6, t * C:(t + 1) * C], lnT[:, t * P:(t + 1) * P], wv[:, :],
                                    start=True, stop=True)
                ins.then_inc(s["v_mm"], 1)
            if query_block(n) is not None:
                pe_score(pe, a, query_block(n))
            if prob_chunk(n) is not None:
                pe_turn_prob(pe, a, prob_chunk(n))
            if n in AT_VALUES:
                pe_values(pe, a, 2 * AT_VALUES.index(n))
            if n == at_ln2(a):
                pe.wait_ge(s["ln2"], ONE + a + 1)
                pe.wait_ge(s["ex"], ONE + (a + 1) * NT + (blocks_before_logits(a) if beside else 0))
                pe.sem_inc(s_past, 1)
                to_channels(pe, s["xt2"])
            if n == at_ln2(a) + LOGITS_AFTER:
                pe.wait_ge(s["lnT2"], ONE + a + 1)
                for h in range(2):
                    ins = pe.matmul(psum[now, 4 + h, :], gate[:, :], lnT[:, h * HB:(h + 1) * HB],
                                    start=True, stop=True)
                ins.then_inc(s["lg"], 1)
            if n == AT_OUT:
                pe.wait_ge(s["oT"], ONE + a + 1)
                for q in range(4):
                    ins = pe.transpose(psum[:, 7, q * P:(q + 1) * P], oT[:, q * P:(q + 1) * P], ident)
                ins.then_inc(s["ot"], 1)

        def turn_weights(pe, b, n):
            q = b * NU + n
            pe.wait_ge(s["w_ok"], ONE + q + 1)
            pe.wait_ge(s["wT"], below(ONE + q - 1))
            for h in range(2):
                for c in range(2):
                    ins = pe.transpose(psum[:, n % 2, (2 * h + c) * P:(2 * h + c + 1) * P],
                                       wt[:, n % NW, h, c, :], ident)
            ins.then_inc(s["tp"], 1)

        def multiply(pe, b, u, n):
            j, tap = divmod(n, K * K)
            k, x = divmod(tap, K)
            pe.wait_ge(s["wT"], ONE + b * NU + n + 1)
            if n == 0:
                pe.wait_ge(s["conv_ok"], ONE + b)
                pe.wait_ge(s["z_sb"], ONE + (b + 1) * NP)
            for c in range(2):
                for h in range(2):
                    ins = pe.matmul(psum[C * h:C * h + C, 2, j * P:(j + 1) * P],
                                    mix[:, u, k, 2 * j + h + c, x * C:(x + 1) * C], wtT[:, n % NW, h, c, :],
                                    start=(tap == 0 and c == 0), stop=(tap == K * K - 1 and c == 1))
            ins.then_inc(s["mm"], 1)

        def pe_turn(pe, b, u):
            for n in range(NU):
                if alive(b):
                    if n + 1 < NU:
                        turn_weights(pe, b, n + 1)
                    elif alive(b + 1):
                        turn_weights(pe, b + 1, 0)
                    multiply(pe, b, u, n)
                if n == AT_BACK and alive(b - 1):
                    pe.wait_ge(s["conv_ok"], ONE + b)
                    if alive(b):
                        pe.wait_ge(s["z_sb"], ONE + (b + 1) * NP)
                    back_to_tokens(pe, s["xo_t"])
                if alive(b) and alive(b + 1) and piece_at(n) is not None:
                    m = piece_at(n)
                    if m == 0:
                        pe.wait_ge(s["img_ok"], ONE + 16 * (b + 2))
                        pe.wait_ge(s["x1"], ONE + b)
                    pe.wait_ge(s["z_sb"], ONE + (b + 1) * NP + m)
                    mix_piece(pe, 1 - u, m, 3, s["z_mm"])
                attention_steps(pe, pe_attention, b, n)

        with nc.Block() as block:
            @block.sync
            def _(sync):
                large = load_flag(sync)
                with sync.If(large < 1):
                    sync.sem_inc(s["img_ok"], 2 * 16)
                    for b in range(2, B + 4):
                        if b < B:
                            sync.wait_ge(s["img_ok"], ONE + 16 * b)
                            sync.wait_ge(s["z_mm"], ONE + (b - 1) * NP)
                            sync.dma_start(img[:, b % 2], pxn[:, b]).then_inc(s["img_ok"], 16)
                        if 0 <= b - 4 < B:
                            keep_logits(sync, b - 4)
                with sync.Else():
                    for b in range(2):
                        sync.dma_start(pxn[:, b], img[:, b]).then_inc(s["img_ok"], 16)
                    for a in range(B):
                        keep_logits(sync, a)
                sync.wait_ge(s["lg_ok"], ONE + 16 * B)

            @block.gpsimd
            def _(pool):
                pool.memset(lnT[C:C + 1, :], 1.0).then_inc(s_ones, 1)
                pool.wait_ge(s_ones, 1)
                large = load_flag(pool)
                with pool.If(large < 1):
                    pool_distances(pool, 0, 0)
                    turns(pool, lambda b, u: pool_turn(pool, b, u))
                with pool.Else():
                    pool.wait_ge(s["img_ok"], ONE + 2 * 16)
                    with pool.Fori(0, B) as b:
                        pool.wait_ge(s["g_x1"], ONE + b)
                        pool.tensor_copy(img[:, 0, :, :], pxn[:, b, :, :]).then_inc(s["g_img"], 1)
                        distances(pool, 0, b, s["g_d"])
                    pool.wait_ge(s["g_img"], ONE + B)
                    with pool.Fori(0, B) as a:
                        pool_norm(pool, a, ONE + a)
                        pool_norm2(pool, a, ONE + a + 1)
                pool.nop()

            @block.scalar
            def _(act):
                large = load_flag(act)
                with act.If(large < 1):
                    for m in range(NP):
                        act.wait_ge(s["z_mm"], ONE + m + 1)
                        keep_piece(act, 0, m, 3 + m % 4, s["z_sb"])
                        if 0 <= m - 4 <= NT // 2:
                            act_tents(act, 0, 0, m - 4)
                    turned_weights(act, 0, 0)
                    turns(act, lambda b, u: act_turn(act, b, u))
                with act.Else():
                    with act.Fori(0, B) as b:
                        act.wait_ge(s["g_d"], ONE + b * 2 + 2)
                        act.activation(tent[:, 0, :], tent[:, 0, :], ACT.Abs).then_inc(s["g_a"], 1)
                        act.wait_ge(s["g_a"], ONE + b + 1)
                        act.activation(tent[:, 0, :], tent[:, 0, :], ACT.Relu, bias=1.0,
                                       scale=-1.0).then_inc(s["g_tent"], 1)
                        for m in range(NP):
                            act.wait_ge(s["g_zm"], ONE + b * NP + (m + 1))
                            keep_piece(act, 0, m, 3, s["g_zs"])
                        act.wait_ge(s["g_xo"], ONE + b)
                        act.sem_inc(s_past, 1)
                        with act.Fori(0, NT // 2) as jt:
                            for h in range(2):
                                bt = b * NT + jt * 2 + h
                                act.wait_ge(s["g_yd"], ONE + bt + 1)
                                act.activation(gy, gy, ACT.Abs).then_inc(s["g_ya"], 1)
                                act.wait_ge(s["g_ya"], ONE + bt + 1)
                                act.activation(gy, gy, ACT.Relu, bias=1.0, scale=-1.0).then_inc(s["g_y"], 1)
                                for k in range(K):
                                    for c in range(NCH):
                                        act.wait_ge(s["g_tp"], ONE + bt * K * NCH + (k * NCH + c + 1))
                                        if c == 0:
                                            act.wait_ge(s["g_mm"], ONE + bt * K + k)
                                        act.activation(gT[:, c, :, :].rearrange("p x q -> p (x q)"),
                                                       psum[:, 0, 0:K * P], ACT.Copy).then_inc(s["g_ev"], 1)
                                act.wait_ge(s["g_mm"], ONE + (bt + 1) * K)
                                act.activation(conv_sb[C * h:C * h + C, bass.ds(jt * P, P)], psum[0:C, 2, 0:P],
                                               ACT.Identity, bias=kbias[0:C, 0:1]).then_inc(s["g_conv"], 1)
                    with act.Fori(0, B) as a:
                        for n in range(STEPS):
                            act_attention(act, a, n)
                    choice.exponentials(act)
                act.nop()

            @block.vector
            def _(dve):
                dve.wait_ge(s_tok, 16 * B)
                dve.tensor_copy(exact[:, 0, :], ident).then_inc(s_exact, 1)
                dve.tensor_copy(exact[:, 1, :], mask).then_inc(s_exact, 1)
                large = load_flag(dve)
                with dve.If(large < 1):
                    for n in range(LEAD):
                        weights(dve, 0, 0, n)
                    turns(dve, lambda b, u: dve_turn(dve, b, u))
                with dve.Else():
                    with dve.Fori(0, B) as b:
                        dve.wait_ge(s["g_tent"], ONE + b + 1)
                        dve.sem_inc(s_past, 1)
                        with dve.Fori(0, NT) as t:
                            bt = b * NT + t
                            dve.wait_ge(s["g_w"], ONE + bt * K * NCH)
                            dy = off[:, b, t, :].rearrange("p (a d) -> p a d", d=2)[:, :, 0]
                            dve.tensor_tensor(gy, dy.unsqueeze(2).to_broadcast([P, K * K, BR * NCH]),
                                              cst("yall").rearrange("p (t m) -> p t m", t=NT)[:, t, :]
                                              .unsqueeze(1).to_broadcast([P, K * K, BR * NCH]),
                                              ALU.add).then_inc(s["g_yd"], 1)
                            dve.wait_ge(s["g_y"], ONE + bt + 1)
                            for k in range(K):
                                taps = slice(k * K, (k + 1) * K)
                                for c in range(NCH):
                                    dve.wait_ge(s["g_tp"], ONE + bt * K * NCH + (k * NCH + c))
                                    dve.tensor_tensor(
                                        wt.rearrange("p n x c q -> p (n x c) q")[:, 0:K, :]
                                        .rearrange("p x (m q) -> p x m q", q=W),
                                        xpart[:, 0, t, taps].unsqueeze(2).to_broadcast([P, K, BR, W]),
                                        gy[:, taps, c * BR:(c + 1) * BR].unsqueeze(3)
                                        .to_broadcast([P, K, BR, W]), ALU.mult).then_inc(s["g_w"], 1)
                        dve.wait_ge(s["g_xo"], ONE + b + 1)
                        add_to_tokens(dve, b, s["g_x1"])
                    dve.wait_ge(s["g_x1"], ONE + B)
                    dve.sem_inc(s["x1"], B)
                    with dve.Fori(0, B) as a:
                        for n in range(STEPS):
                            dve_attention(dve, a, n)
                    for step in range(len(AT_CHOICE)):
                        dve_choice(dve, step)
                dve.wait_ge(choice.s_tk, 1)
                dve.nop()

            @block.tensor
            def _(pe):
                pe.wait_ge(s_ones, 1)
                pe.wait_ge(s_exact, 2)
                large = load_flag(pe)
                with pe.If(large < 1):
                    for m in range(NP):
                        pe.wait_ge(s["z_sb"], below(ONE + m - 3))
                        mix_piece(pe, 0, m, 3 + m % 4, s["z_mm"])
                    turn_weights(pe, 0, 0)
                    turns(pe, lambda b, u: pe_turn(pe, b, u))
                with pe.Else():
                    with pe.Fori(0, B) as b:
                        pe.wait_ge(s["g_img"], ONE + b + 1)
                        pe.wait_ge(s["g_x1"], ONE + b)
                        for m in range(NP):
                            pe.wait_ge(s["g_zs"], ONE + b * NP + m)
                            mix_piece(pe, 0, m, 3, s["g_zm"])
                        pe.wait_ge(s["g_zs"], ONE + (b + 1) * NP)
                        pe.sem_inc(s_past, 1)
                        with pe.Fori(0, NT // 2) as j:
                            for h in range(2):
                                bt = b * NT + j * 2 + h
                                pe.wait_ge(s["g_conv"], ONE + bt)
                                for k in range(K):
                                    for c in range(NCH):
                                        pe.wait_ge(s["g_w"], ONE + bt * K * NCH + (k * NCH + c + 1))
                                        pe.wait_ge(s["g_ev"], ONE + bt * K * NCH + (k * NCH + c))
                                        for x in range(K):
                                            ins = pe.transpose(psum[:, 0, x * P:(x + 1) * P],
                                                               wt.rearrange("p n x c q -> p (n x c) q")[:, x, :],
                                                               ident)
                                        ins.then_inc(s["g_tp"], 1)
                                    pe.wait_ge(s["g_ev"], ONE + bt * K * NCH + (k + 1) * NCH)
                                    for x in range(K):
                                        for c in range(NCH):
                                            ins = pe.matmul(psum[0:C, 2, 0:P],
                                                            mix[:, 0, k, c, x * C:(x + 1) * C], gT[:, c, x, :],
                                                            start=(k == 0 and x == 0 and c == 0),
                                                            stop=(k == K - 1 and x == K - 1 and c == NCH - 1))
                                    ins.then_inc(s["g_mm"], 1)
                        pe.wait_ge(s["g_conv"], ONE + (b + 1) * NT)
                        back_to_tokens(pe, s["g_xo"])
                    pe.wait_ge(s["g_x1"], ONE + B)
                    with pe.Fori(0, B) as a:
                        for n in range(STEPS):
                            pe_attention(pe, a, n, beside=False)
                pe.nop()


class Norm:

    def __init__(self, sb, sem, cst, tag, tmp, s_past):
        self.tmp = tmp
        self.small = sb(tag + "_small", [P, 3, NT])
        self.half = cst("half")
        self.s_past = s_past
        (self.s_sum, self.s_mean, self.s_xc, self.s_sq, self.s_var, self.s_eps,
         self.s_rstd) = (sem(f"{tag}_{n}") for n in ("sum", "mean", "xc", "sq", "var", "eps", "rstd"))

    def sums(self, dve, src, b):
        small = self.small
        dve.tensor_reduce(small[:, 0, :], src, AX.X, ALU.add).then_inc(self.s_sum, 1)
        dve.wait_ge(self.s_sum, b + 1)
        dve.tensor_scalar(small[:, 0, :], small[:, 0, :], -1.0 / C, None, ALU.mult).then_inc(self.s_mean, 1)

    def squares(self, dve, b):
        small = self.small
        dve.wait_ge(self.s_sq, b + 1)
        dve.tensor_reduce(small[:, 1, :], self.tmp[:, 1], AX.X, ALU.add).then_inc(self.s_var, 1)

    def gpsimd(self, pool, src, dst, b, done, free, uses):
        xc, sq, small = self.tmp[:, 0], self.tmp[:, 1], self.small

        def spread(x):
            return x.unsqueeze(2).to_broadcast([P, NT, C])

        pool.wait_ge(self.s_mean, b + 1)
        pool.wait_ge(done, ONE + b)
        pool.sem_inc(self.s_past, 1)
        pool.tensor_tensor(xc, src, spread(small[:, 0, :]), ALU.add).then_inc(self.s_xc, 1)
        pool.wait_ge(self.s_xc, b + 1)
        pool.tensor_tensor(sq, xc, xc, ALU.mult).then_inc(self.s_sq, 1)
        pool.wait_ge(self.s_var, b + 1)
        pool.sem_inc(self.s_past, 1)
        pool.tensor_scalar(small[:, 2, :], small[:, 1, :], 1.0 / C, LN_EPS, ALU.mult, ALU.add).then_inc(self.s_eps, 1)
        pool.wait_ge(self.s_eps, b + 1)
        pool.tensor_tensor(small[:, 2, :], small[:, 2, :], self.half, ALU.pow).then_inc(self.s_rstd, 1)
        pool.wait_ge(self.s_rstd, b + 1)
        pool.wait_ge(free, uses)
        pool.tensor_tensor(dst, xc, spread(small[:, 2, :]), ALU.mult).then_inc(done, 1)


class Choice:

    def __init__(self, sb, sem, tag, logits, pm, work):
        self.logits, self.pm = logits, pm
        self.ex, self.pr, self.left = work
        self.nmx, self.tsum, self.top = (sb(tag + "_nmx", [P, 1]), sb(tag + "_tsum", [P, 2]),
                                         sb(tag + "_top", [P, TOP]))
        (self.s_mx, self.s_ex, self.s_rc, self.s_pr, self.s_top, self.s_rep,
         self.s_tk) = (sem(f"{tag}_{n}") for n in ("mx", "ex", "rc", "pr", "top", "rep", "tk"))

    def largest(self, dve):
        dve.tensor_reduce(self.nmx[:, :], self.logits, AX.X, ALU.max, negate=True).then_inc(self.s_mx, 1)

    def exponentials(self, act):
        act.wait_ge(self.s_mx, 1)
        act.activation(self.ex, self.logits, ACT.Exp, bias=self.nmx[:, 0:1],
                       accum_out=self.tsum[:, 0:1]).then_inc(self.s_ex, 1)

    def probabilities(self, dve):
        dve.wait_ge(self.s_ex, 1)
        dve.reciprocal(self.tsum[:, 1:2], self.tsum[:, 0:1]).then_inc(self.s_rc, 1)
        dve.wait_ge(self.s_rc, 1)
        dve.tensor_scalar(self.pr, self.ex, self.tsum[:, 1:2], None, ALU.mult).then_inc(self.s_pr, 1)

    def top_values(self, dve):
        dve.wait_ge(self.s_pr, 1)
        dve.max(self.top[:, :], self.pr).then_inc(self.s_top, 1)

    def mark(self, dve):
        dve.wait_ge(self.s_top, 1)
        dve.match_replace(self.left, self.top[:, :], self.pr, -1.0).then_inc(self.s_rep, 1)

    def keep(self, dve):
        dve.wait_ge(self.s_rep, 1)
        dve.scalar_tensor_tensor(self.pm, self.left, 0.0, self.pr, ALU.is_lt, ALU.mult).then_inc(self.s_tk, 1)


def route(nc, dram, cst, psum, ln2, logits, pm, lhs, w1, w2, b2, pick, s_w, s_past):
    ident = cst("ident")
    with ExitStack() as ctx:
        def sb(name, shape, dt=F32):
            return ctx.enter_context(nc.sbuf_tensor(name, shape, dt))

        def sem(name):
            return ctx.enter_context(nc.semaphore(name))

        work = sb("work", [P, 3, T])
        choice = Choice(sb, sem, "r1", logits[1], pm[:, 1, :], [work[:, n, :] for n in range(3)])
        takenT = sb("takenT", [P, NG, NT, P])
        s = {n: sem("r_" + n) for n in "pad tt tT po pT".split()}

        with nc.Block() as block:
            @block.sync
            def _(sync):
                sync.dma_start(w1[:, :, :], dram["w1"]).then_inc(s_w, 16)
                sync.dma_start(w2[:, :, :, :], dram["w2"]).then_inc(s_w, 16)
                sync.dma_start(b2[:, :, :], dram["b2"]).then_inc(s_w, 16)
                sync.dma_start(pick[:, :, :], dram["pick"]).then_inc(s_w, 16)

            @block.gpsimd
            def _(pool):
                pool.memset(lhs[0:C, :, :], 0.0).then_inc(s["pad"], 1)
                pool.wait_ge(s["pad"], 1)
                pool.memset(lhs[C:C + 1, :, :], 1.0).then_inc(s["pad"], 1)
                pool.wait_ge(s["pad"], 2)

            @block.vector
            def _(dve):
                choice.largest(dve)
                choice.probabilities(dve)
                choice.top_values(dve)
                choice.mark(dve)
                choice.keep(dve)
                dve.wait_ge(choice.s_tk, 1)

            @block.scalar
            def _(act):
                choice.exponentials(act)
                act.wait_ge(s["pad"], 2)
                for g in range(NG):
                    act.wait_ge(s["tt"], g + 1)
                    act.activation(takenT[:, g].rearrange("p a q -> p (a q)"),
                                   psum[:, 2 * g:2 * g + 2, :].rearrange("p a q -> p (a q)"),
                                   ACT.Copy).then_inc(s["tT"], 1)
                    act.wait_ge(s["po"], g + 1)
                    for h in range(2):
                        act.activation(lhs[0:C, :, g * GI + h:(g + 1) * GI:2].rearrange("c e q -> c q e"),
                                       psum[C * h:C * h + C, 4 + g, 0:GI // 2 * E]
                                       .rearrange("c (q e) -> c q e", e=E), ACT.Copy).then_inc(s["pT"], 1)
                act.wait_ge(s["pT"], 2 * NG)

            @block.tensor
            def _(pe):
                for g in range(NG):
                    if g == 1:
                        pe.wait_ge(choice.s_tk, 1)
                    for t in range(NT):
                        ins = pe.transpose(psum[:, 2 * g + t // 4, (t % 4) * P:(t % 4 + 1) * P],
                                           pm[:, g, t * P:(t + 1) * P], ident)
                    ins.then_inc(s["tt"], 1)
                    pe.wait_ge(s["tT"], g + 1)
                    for q in range(GI // 2):
                        for t in range(NT):
                            for h in range(2):
                                u = 2 * q + h
                                ins = pe.matmul(psum[C * h:C * h + C, 4 + g, E * q:E * q + E],
                                                ln2[:, g * GI + u, t, :], takenT[:, g, t, E * u:E * u + E],
                                                start=(t == 0), stop=(t == NT - 1))
                    ins.then_inc(s["po"], 1)


def mlp(nc, cst, psum, w1, w2, b2, pick, s_w, lhs, expert_out):
    ident = cst("ident")
    QN = P // E
    NI = E // QN
    with ExitStack() as ctx:
        def sb(name, shape, dt=F32):
            return ctx.enter_context(nc.sbuf_tensor(name, shape, dt))

        def sem(name):
            return ctx.enter_context(nc.semaphore(name))

        h = sb("h", [P, NI, HID])
        hT = sb("hT", [P, NI, 2, P])
        outs = sb("outs", [P, NI, C])
        s = {n: sem("e_" + n) for n in "h gelu t hT o out moved zero kept".split()}
        layer1 = psum[:, 0:4, :].rearrange("p a q -> p (a q)").rearrange("p (i q) -> p i q", i=NI)
        with nc.Block() as block:
            @block.tensor
            def _(pe):
                pe.wait_ge(s_w, 16 * 4)
                for i in range(NI):
                    for j in range(QN):
                        e = QN * i + j
                        ins = pe.matmul(layer1[E * j:E * j + E, i, :], lhs[:, e, :], w1[:, e, :],
                                        start=True, stop=True)
                    ins.then_inc(s["h"], 1)
                for i in range(NI):
                    pe.wait_ge(s["gelu"], i // 2 + 1)
                    for f in range(2):
                        n = 2 * i + f
                        ins = pe.transpose(psum[:, 4 + n // 4, (n % 4) * P:(n % 4 + 1) * P],
                                           h[:, i, f * P:(f + 1) * P], ident)
                    ins.then_inc(s["t"], 1)
                for i in range(NI):
                    if i % 2 == 0:
                        pe.wait_ge(s["hT"], i // 2 + 1)
                    for f in range(2):
                        for j in range(QN):
                            ins = pe.matmul(psum[E * j:E * j + E, 0, i * C:(i + 1) * C],
                                            hT[:, i, f, E * j:E * j + E], w2[:, f, QN * i + j, :],
                                            start=(f == 0), stop=(f == 1))
                ins.then_inc(s["o"], 1)
                pe.wait_ge(s["out"], 1)
                for g in range(NG):
                    for i in range(NI):
                        first = (NI - 1 - i) * QN
                        ins = pe.matmul(psum[:, 1, g * C:(g + 1) * C], pick[:, g, first:first + P], outs[:, i, :],
                                        start=(i == 0), stop=(i == NI - 1))
                ins.then_inc(s["moved"], 1)

            @block.scalar
            def _(act):
                for n in range(NI // 2):
                    act.wait_ge(s["h"], 2 * n + 2)
                    act.activation(h[:, 2 * n:2 * n + 2, :], layer1[:, 2 * n:2 * n + 2, :],
                                   ACT.Gelu).then_inc(s["gelu"], 1)

            @block.vector
            def _(dve):
                for n in range(NI // 2):
                    dve.wait_ge(s["t"], 2 * n + 2)
                    dve.tensor_copy(hT[:, 2 * n:2 * n + 2].rearrange("p i f q -> p (i f q)"),
                                    psum[:, 4 + n, :]).then_inc(s["hT"], 1)
                dve.wait_ge(s["o"], 1)
                dve.tensor_tensor(outs.rearrange("p i f -> p (i f)"), psum[:, 0, :],
                                  b2.rearrange("p i f -> p (i f)"), ALU.add).then_inc(s["out"], 1)
                dve.wait_ge(s["moved"], 1)
                dve.wait_ge(s["zero"], 1)
                for u in range(GI):
                    rows = slice(E * u, E * u + E)
                    dve.tensor_copy(expert_out[rows, :, u, :],
                                    psum[rows, 1, 0:NG * C].rearrange("p (g f) -> p g f", g=NG)).then_inc(s["kept"], 1)
                dve.wait_ge(s["kept"], GI)

            @block.gpsimd
            def _(pool):
                pool.memset(expert_out[:, :, :, :], 0.0).then_inc(s["zero"], 1)


def combine(nc, psum, tok, pm, expert_out, out):
    pieces = [(g, h) for g in range(NG) for h in range(NT // 2)]
    out_tok = out.rearrange("b (t r) w c -> (r w) b t c", r=BR)
    with ExitStack() as ctx:
        def sem(name):
            return ctx.enter_context(nc.semaphore(name))

        s = {n: sem("f_" + n) for n in "y x st_sync st_act".split()}

        def store(eng, odd, done):
            for n, (g, h) in enumerate(pieces):
                images, t = slice(g * GI, (g + 1) * GI), 2 * h + odd
                eng.wait_ge(s["x"], n + 1)
                eng.dma_start(out_tok[:, images, t, :], tok[:, images, t, :]).then_inc(done, 16)
            eng.wait_ge(done, 16 * len(pieces))

        with nc.Block() as block:
            @block.tensor
            def _(pe):
                for n, (g, h) in enumerate(pieces):
                    for t in (2 * h, 2 * h + 1):
                        ins = pe.matmul(psum[:, n, t % 2 * GI * C:(t % 2 + 1) * GI * C],
                                        pm[:, g, t * P:(t + 1) * P], expert_out[:, g].rearrange("p u f -> p (u f)"),
                                        start=True, stop=True)
                    ins.then_inc(s["y"], 1)

            @block.vector
            def _(dve):
                for n, (g, h) in enumerate(pieces):
                    x = tok[:, g * GI:(g + 1) * GI, 2 * h:2 * h + 2, :]
                    dve.wait_ge(s["y"], n + 1)
                    dve.tensor_tensor(x, psum[:, n, :].rearrange("p (t u f) -> p u t f", t=2, u=GI), x,
                                      ALU.add).then_inc(s["x"], 1)

            @block.sync
            def _(sync):
                store(sync, 0, s["st_sync"])

            @block.scalar
            def _(act):
                store(act, 1, s["st_act"])


def lay_out(inputs):
    f = {k: np.asarray(v) for k, v in inputs.items()}
    taps = f["L0_conv_kernel"].reshape(K * K, C, C)
    kp = np.zeros((P, K, K * C), np.float32)
    for k, half in ((0, 0), (1, C), (2, 0)):
        kp[half:half + C, k] = taps[K * k:K * k + K].transpose(1, 0, 2).reshape(C, K * C)
    ow = np.zeros((K, C, K, 32), np.float32)
    ow[..., :OCH] = f["L0_conv_offset_w"].transpose(0, 2, 1, 3)
    ob = np.zeros((4, 32), np.float32)
    ob[:, :OCH] = f["L0_conv_offset_b"]
    w2 = f["L1_ffn_weight2"]
    strips = P // E
    shift = E - strips
    pick = np.zeros((P, NG, P + shift), np.float32)
    for g in range(NG):
        for u in range(GI):
            for j in range(strips):
                pick[E * j + g * GI + u, g, E * u + j + shift] = 1.0
    return {
        "x": f["x"],
        "const": constants()[0],
        "ow_pair": ow[0:2].reshape(P, K, 32),
        "ow_last": ow[2],
        "ob": ob.reshape(P, 1),
        "kp": kp,
        "kbias": np.tile(f["L0_conv_bias"], 2).reshape(P, 1),
        "wqk": np.concatenate([np.concatenate([f["L1_attn_Wq"], f["L1_attn_Wk"]], 1),
                               np.concatenate([f["L1_attn_bq"], f["L1_attn_bk"]])[None]], 0),
        "wv": np.concatenate([f["L1_attn_Wv"], f["L1_attn_bv"][None]], 0),
        "gate": np.concatenate([f["L1_ffn_gate_w"].T, f["L1_ffn_gate_b"][None]], 0),
        "w1": np.ascontiguousarray(f["L1_ffn_weight1"].transpose(1, 0, 2)),
        "w2": np.ascontiguousarray(w2[:, :HID].reshape(E, 2, P, C).transpose(2, 1, 0, 3)),
        "pick": pick,
        "b2": np.repeat(w2[:, HID].reshape(E * E // P, P // E, C).transpose(1, 0, 2), E, 0),
    }


def kernel(**inputs):
    import concourse.bacc as bacc
    from concourse.bass_utils import run_bass_kernel_spmd

    nc = bacc.Bacc("TRN2", target_bir_lowering=False, num_devices=1)
    arrays = {f"in_{k}": np.ascontiguousarray(v) for k, v in lay_out(inputs).items()}
    dram = {k[3:]: nc.dram_tensor(k, a.shape, F32, kind="ExternalInput").ap() for k, a in arrays.items()}
    out = nc.dram_tensor("out", (B, H, W, C), F32, kind="ExternalOutput").ap()
    build(nc, dram, out)
    return run_bass_kernel_spmd(nc, [arrays], core_ids=[0]).results[0]["out"]
```
